# Optimizing a Trainium2 kernel written in Bass

```python
import numpy as np
import jax
import jax.numpy as jnp

def _softmax(x, axis=-1):
    return jax.nn.softmax(x, axis=axis)

def _gelu(x):
    return jax.nn.gelu(x, approximate=True)

def _silu(x):
    return jax.nn.silu(x)

def _sigmoid(x):
    return jax.nn.sigmoid(x)

def _layernorm(x, axis=-1, eps=1e-05):
    m = jnp.mean(x, axis=axis, keepdims=True)
    v = jnp.var(x, axis=axis, keepdims=True)
    return (x - m) / jnp.sqrt(v + eps)

def _scatter_add(tgt, idx, src, axis=0):
    return tgt.at[idx].add(src)

def _segment_sum(src, seg, n):
    return jax.ops.segment_sum(src, seg, n)
kernel_name = 'mk_gps_d1_gnn_r8_c8199a'

def setup_inputs(seed: int=0):
    np.random.seed(seed)
    _w = jnp.asarray

    def _rec_inputs():
        import jax
        import jax.numpy as jnp
        _gk = jax.random.key(seed)
        x = -0.0001126 + 1 * jax.random.normal(jax.random.fold_in(_gk, 1), (6250, 768), jnp.float32)
        _s = jax.random.randint(jax.random.fold_in(_gk, 2), (50000,), 0, 6250, jnp.int32)
        _d = jax.random.randint(jax.random.fold_in(_gk, 3), (50000,), 0, 6250, jnp.int32)
        _loop = jnp.arange(6250, dtype=jnp.int32)
        src = jnp.concatenate([_s, _d, _loop])
        dst = jnp.concatenate([_d, _s, _loop])
        _o = jnp.argsort(dst, stable=True)
        src = src[_o]
        dst = dst[_o]
        return (x, src, dst)
    x, src, dst = _rec_inputs()

    def _L0_gnn_setup():
        import jax, jax.numpy as jnp
        import numpy as np
        N_NODES = 1250
        key = jax.random.key(seed)
        k1, k2, k3 = jax.random.split(key, 3)
        x = jax.random.normal(k1, (N_NODES, 768), dtype=jnp.float32)
        edge_index = jax.random.randint(k2, (2, 12500), 0, N_NODES, dtype=jnp.int32)
        W = jax.random.normal(k3, (768, 768), dtype=jnp.float32) * (1.0 / np.sqrt(768))
        b = jnp.zeros((768,), dtype=jnp.float32)
        return {'x': x, 'edge_index': edge_index, 'W': W, 'b': b}
    _L0_gnn_all = _L0_gnn_setup()
    _L0_gnn_in = {k: v for k, v in _L0_gnn_all.items() if k in ('W', 'b')}
    del _L0_gnn_all

    def _L0_mix_setup():
        import jax, jax.numpy as jnp
        import numpy as np
        import math
        EPS = 0.001

        def _relu_features(t, proj_mat):
            ratio = 1.0 / math.sqrt(float(proj_mat.shape[0]))
            z = ratio * jnp.einsum('blhd,md->blhm', t, proj_mat)
            return jax.nn.relu(z) + EPS
        key = jax.random.key(seed)
        ks = jax.random.split(key, 6)
        B, L, DIM = (8, 512, 768)
        H, D, M = (12, 64, 256)
        x = jax.random.normal(ks[0], (B, L, DIM), dtype=jnp.float32)
        qkv_w = jax.random.normal(ks[1], (3 * DIM, DIM), dtype=jnp.float32) * DIM ** (-0.5)
        qkv_b = jnp.zeros((3 * DIM,), dtype=jnp.float32)
        proj_w = jax.random.normal(ks[2], (DIM, DIM), dtype=jnp.float32) * DIM ** (-0.5)
        proj_b = jnp.zeros((DIM,), dtype=jnp.float32)
        blocks = []
        for i in range(M // D):
            g = jax.random.normal(ks[3 + 0] if False else jax.random.fold_in(ks[3], i), (D, D), dtype=jnp.float32)
            q, _ = jnp.linalg.qr(g)
            blocks.append(q.T)
        pm = jnp.concatenate(blocks, axis=0)
        mult = jnp.linalg.norm(jax.random.normal(ks[4], (M, D), dtype=jnp.float32), axis=1)
        proj_mat = mult[:, None] * pm
        return {'x': x, 'qkv_w': qkv_w, 'qkv_b': qkv_b, 'proj_w': proj_w, 'proj_b': proj_b, 'proj_mat': proj_mat}
    _L0_mix_all = _L0_mix_setup()
    _L0_mix_in = {k: v for k, v in _L0_mix_all.items() if k in ('qkv_w', 'qkv_b', 'proj_w', 'proj_b', 'proj_mat')}
    del _L0_mix_all

    def _L0_ffn_setup():
        import jax, jax.numpy as jnp
        import numpy as np
        DEPTH = 11

        def _fff_forward(inputs, weights_in, weights_out, depth=DEPTH):
            B, S, _ = inputs.shape
            n_nodes = weights_in.shape[0]
            max_index = n_nodes - 1
            all_logits = jnp.einsum('bsd,nd->bsn', inputs, weights_in)

            def step(prev_idx, _):
                sel = jnp.clip(prev_idx, 0, max_index)
                logits = jnp.take_along_axis(all_logits, sel[..., None], axis=-1)[..., 0]
                new_idx = jnp.clip(2 * sel + 1 + (logits > 0).astype(sel.dtype), 0, max_index)
                return (new_idx, (logits, new_idx))
            idx0 = jnp.zeros((B, S), dtype=jnp.int32)
            _, (logits_seq, idx_seq) = jax.lax.scan(step, idx0, None, length=depth - 1)
            logits = jnp.concatenate([jnp.zeros((1, B, S), all_logits.dtype), logits_seq], axis=0)
            node_idx = jnp.concatenate([idx0[None], idx_seq], axis=0)
            act = jax.nn.gelu(logits, approximate=False)
            onehot = jax.nn.one_hot(node_idx, n_nodes, dtype=act.dtype)
            coeff = jnp.einsum('dbs,dbsn->bsn', act, onehot)
            return jnp.einsum('bsn,nd->bsd', coeff, weights_out)
        key = jax.random.key(seed)
        k1, k2, k3 = jax.random.split(key, 3)
        B, S, D = (4, 512, 768)
        n_nodes = 2 * DEPTH - 1
        return {'inputs': jax.random.normal(k1, (B, S, D), dtype=jnp.float32), 'weights_in': jax.random.normal(k2, (n_nodes, D), dtype=jnp.float32), 'weights_out': jax.random.normal(k3, (n_nodes, D), dtype=jnp.float32)}
    _L0_ffn_all = _L0_ffn_setup()
    _L0_ffn_in = {k: v for k, v in _L0_ffn_all.items() if k in ('weights_in', 'weights_out')}
    del _L0_ffn_all
    return {'x': x, 'src': src, 'dst': dst, 'L0_gnn_W': _L0_gnn_in['W'], 'L0_gnn_b': _L0_gnn_in['b'], 'L0_mix_qkv_w': _L0_mix_in['qkv_w'], 'L0_mix_qkv_b': _L0_mix_in['qkv_b'], 'L0_mix_proj_w': _L0_mix_in['proj_w'], 'L0_mix_proj_b': _L0_mix_in['proj_b'], 'L0_mix_proj_mat': _L0_mix_in['proj_mat'], 'L0_ffn_weights_in': _L0_ffn_in['weights_in'], 'L0_ffn_weights_out': _L0_ffn_in['weights_out']}

def reference(x, src, dst, L0_gnn_W, L0_gnn_b, L0_mix_qkv_w, L0_mix_qkv_b, L0_mix_proj_w, L0_mix_proj_b, L0_mix_proj_mat, L0_ffn_weights_in, L0_ffn_weights_out):
    import jax
    import jax.numpy as jnp

    def _L0_gnn_ref(x, edge_index, W, b):
        import jax, jax.numpy as jnp
        import numpy as np
        N_NODES = 1250
        n = x.shape[0]
        loops = jnp.arange(n, dtype=edge_index.dtype)
        row = jnp.concatenate([edge_index[0], loops])
        col = jnp.concatenate([edge_index[1], loops])
        ones = jnp.ones(row.shape[0], dtype=x.dtype)
        deg = jax.ops.segment_sum(ones, col, num_segments=n)
        dinv = jnp.where(deg > 0, jax.lax.rsqrt(deg), 0.0)
        norm = dinv[row] * dinv[col]
        h = x @ W
        msg = h[row] * norm[:, None]
        out = jax.ops.segment_sum(msg, col, num_segments=n) + b
        return out

    def _L0_mix_ref(x, qkv_w, qkv_b, proj_w, proj_b, proj_mat):
        import jax, jax.numpy as jnp
        import numpy as np
        import math
        EPS = 0.001

        def _relu_features(t, proj_mat):
            ratio = 1.0 / math.sqrt(float(proj_mat.shape[0]))
            z = ratio * jnp.einsum('blhd,md->blhm', t, proj_mat)
            return jax.nn.relu(z) + EPS
        B, L, DIM = x.shape
        H = 12
        D = DIM // H
        qkv = x @ qkv_w.T + qkv_b
        qkv = qkv.reshape(B, L, 3, H, D)
        q, k, v = (qkv[:, :, 0], qkv[:, :, 1], qkv[:, :, 2])
        q_p = _relu_features(q, proj_mat)
        k_p = _relu_features(k, proj_mat)
        kv = jnp.einsum('blhm,blhd->bhmd', k_p, v)
        k_sum = k_p.sum(axis=1)
        num = jnp.einsum('blhm,bhmd->blhd', q_p, kv)
        den = jnp.einsum('blhm,bhm->blh', q_p, k_sum)
        out = num / den[..., None]
        out = out.reshape(B, L, DIM)
        return out @ proj_w.T + proj_b

    def _L0_ffn_ref(inputs, weights_in, weights_out):
        import jax, jax.numpy as jnp
        import numpy as np
        DEPTH = 11

        def _fff_forward(inputs, weights_in, weights_out, depth=DEPTH):
            B, S, _ = inputs.shape
            n_nodes = weights_in.shape[0]
            max_index = n_nodes - 1
            all_logits = jnp.einsum('bsd,nd->bsn', inputs, weights_in)

            def step(prev_idx, _):
                sel = jnp.clip(prev_idx, 0, max_index)
                logits = jnp.take_along_axis(all_logits, sel[..., None], axis=-1)[..., 0]
                new_idx = jnp.clip(2 * sel + 1 + (logits > 0).astype(sel.dtype), 0, max_index)
                return (new_idx, (logits, new_idx))
            idx0 = jnp.zeros((B, S), dtype=jnp.int32)
            _, (logits_seq, idx_seq) = jax.lax.scan(step, idx0, None, length=depth - 1)
            logits = jnp.concatenate([jnp.zeros((1, B, S), all_logits.dtype), logits_seq], axis=0)
            node_idx = jnp.concatenate([idx0[None], idx_seq], axis=0)
            act = jax.nn.gelu(logits, approximate=False)
            onehot = jax.nn.one_hot(node_idx, n_nodes, dtype=act.dtype)
            coeff = jnp.einsum('dbs,dbsn->bsn', act, onehot)
            return jnp.einsum('bsn,nd->bsd', coeff, weights_out)
        return _fff_forward(inputs, weights_in, weights_out)
    edge_index = jnp.stack([src, dst])
    xn = _layernorm(x, axis=-1)
    x = x + _L0_gnn_ref(xn, edge_index, L0_gnn_W, L0_gnn_b) + _L0_mix_ref(xn[None], L0_mix_qkv_w, L0_mix_qkv_b, L0_mix_proj_w, L0_mix_proj_b, L0_mix_proj_mat)[0]
    x = x + _L0_ffn_ref(_layernorm(x, axis=-1)[None], L0_ffn_weights_in, L0_ffn_weights_out)[0]
    return x

_drawn_inputs = setup_inputs


def setup_inputs(seed=0):
    import zlib

    import numpy as np

    out = dict(_drawn_inputs(seed))
    spreads = {'L0_gnn_b': (0.0, 0.1), 'L0_mix_qkv_b': (0.0, 0.1), 'L0_mix_proj_b': (0.0, 0.1)}
    factors = {}
    for name, (base, spread) in spreads.items():
        noise = np.random.default_rng([zlib.crc32(name.encode()), seed]).standard_normal(out[name].shape)
        drawn = base * np.exp(spread * noise) if base else spread * noise
        out[name] = jnp.asarray(drawn.astype(out[name].dtype))
    for name, factor in factors.items():
        out[name] = (out[name] * factor).astype(out[name].dtype)
    return out
```

```python
from contextlib import ExitStack

import concourse.bass as bass
from concourse import mybir

P = 128
ALU = mybir.AluOpType
ACT = mybir.ActivationFunctionType
F32 = mybir.dt.float32
F16 = mybir.dt.float16
I32 = mybir.dt.int32
U32 = mybir.dt.uint32

D = 768
DC = D // P
H = 12
DH = D // H
DV = DH + 1
M = 256
NN = 21
B = 2 * P
BANK = 512
WS = 8.0
ZS = 128.0
TS = 16.0
EPS_LN = 1e-5
EPS_FEAT = 1e-3
WIN = 18
UNIT = 3
RING = 12
SRING = 4
BIG = 1 << 20
PAIRS = ((0, 0), (1, 0), (0, 1))


def wait_for(eng, sem, value):
    if not (isinstance(value, int) and value <= 0):
        eng.wait_ge(sem, value)


def wait_apart(eng, sem, value, passed):
    if not (isinstance(value, int) and value <= 0):
        eng.wait_ge(sem, value)
        eng.sem_inc(passed, 1)


def slots(names, readers, before):
    out, n, a, v, last = {}, 0, 0, 0, before
    for u in names:
        r_last = readers[last] if last else "av"
        out[u] = (n, a, v, a - ("a" in r_last), v - ("v" in r_last))
        r = readers[u[0]]
        n, a, v, last = n + 1, a + ("a" in r), v + ("v" in r), u[0]
    return out, (n, a, v)


def gps_layer(nc, x, src, dst, gnn_w, gnn_b, qkv_w, qkv_b, proj_w, proj_b, proj_mat, w_in, w_out, out):
    N, E = x.shape[0], src.shape[0]
    NB, TAIL = N // B, N % B
    assert 0 < TAIL <= P and NB >= 3 and NB % 2 == 0
    NT = 2 * NB + 1
    NTP = NT + 1
    HC = -(-(E + WIN * P) // (P * (NB + 1)))
    EC = HC * (NB + 1)
    EP = EC * P

    with ExitStack() as ctx:
        def sb(name, shape, dt):
            return ctx.enter_context(nc.sbuf_tensor(name, shape, dt))

        def sem(name):
            return ctx.enter_context(nc.semaphore(name))

        src_pad = nc.dram_tensor("src_pad", (EP,), I32).ap()
        dst_pad = nc.dram_tensor("dst_pad", (EP + P,), I32).ap()
        xn_dram = nc.dram_tensor("xn_dram", (N, D), F32).ap()
        xnt_dram = nc.dram_tensor("xnt_dram", ((NB + 1) * P, 2 * DC * B), F16).ap()
        table = nc.dram_tensor("table", (N, 2 * D), F16).ap()

        acc = [ctx.enter_context(nc.psum_tensor(f"acc{i}", [P, 2 * BANK], F32)) for i in range(2)]
        zps = ctx.enter_context(nc.psum_tensor("zps", [P, 2 * BANK], F32))
        slot = [ctx.enter_context(nc.psum_tensor(f"slot{i}", [P, BANK], F32)) for i in range(2)]

        ident = sb("ident", [P, P], F32)
        ident16 = sb("ident16", [P, P], F16)
        ones = sb("ones", [P, P], F32)
        epsk = sb("epsk", [P, P], F32)
        iota_i = sb("iota_i", [P, P], I32)
        iota16 = sb("iota16", [P, P], F16)
        padrow = sb("padrow", [P, 2 * P], I32)
        wq = sb("wq", [P, 2, DC, D], F16)
        wp = sb("wp", [P, 2, DC, D], F16)
        wg = sb("wg", [P, 2, DC, D], F16)
        region = sb("region", [P, 2 * 2 * DC * D], F16)
        wk = region[:, 0:2 * DC * D].rearrange("p (s k n) -> p s k n", s=2, k=DC)
        wv = region[:, 2 * DC * D:4 * DC * D].rearrange("p (s k n) -> p s k n", s=2, k=DC)
        pmT = sb("pmT", [P, 2, M], F16)
        winT = sb("winT", [P, 2, DC, NN], F16)
        wo = sb("wo", [96, D], F16)
        bqk_r = sb("bqk_r", [P, 3 * DC], F32)
        bqk = sb("bqk", [P, 3 * DC], F32)
        gpb = sb("gpb", [P, D], F32)
        lo7 = sb("lo7", [P, EC], F16)
        hi7 = sb("hi7", [P, EC], F16)
        degs = sb("degs", [P, NTP], F32)
        dinvT = sb("dinvT", [P, NTP], F32)
        dinvZ = sb("dinvZ", [P, NTP], F32)
        dinv = sb("dinv", [P, NTP], F32)
        scanA = sb("scanA", [P, NTP], F32)
        scanB = sb("scanB", [P, NTP], F32)
        scanC = sb("scanC", [P, NTP], F32)
        mhalf = sb("mhalf", [P, NTP], F32)
        var_eps = sb("var_eps", [P, 2], F32)
        eps_ln = sb("eps_ln", [P, 1], F32)
        cnt = sb("cnt", [P, NTP], F32)
        e0f = sb("e0f", [P, NTP], F32)
        e0 = sb("e0", [P, NTP], I32)
        tile_base = sb("tile_base", [P, NTP], F32)
        tile_i = sb("tile_i", [P, NTP], I32)
        kvs = sb("kvs", [P, 24, DV], F32)
        kvp = sb("kvp", [P, 2, 24, DV], F16)
        vacc = sb("vacc", [P, H * DV], F32)
        cn = vacc[:].rearrange("p (h d) -> p h d", h=H)
        kf = sb("kf", [P, 2 * H], F32)
        xa = sb("xa", [P, 2, D], F32)
        xb = sb("xb", [P, 2, D], F32)
        st = sb("st", [P, 2, 2, 6], F32)
        mv = sb("mv", [P, 2, 2], F32)
        rs = sb("rs", [P, 2], F32)
        xT = sb("xT", [P, 2, DC, B], F16)
        hd = sb("hd", [P, H, B], F16)
        vp = sb("vp", [P, 2, 2, H * DV], F16)
        big = sb("big", [P, 2 * 2 * H * M], F16)
        kfeat = big[:].rearrange("p (s t n) -> p s t n", s=2, t=2)
        oT = big[:, 0:2 * DC * B].rearrange("p (s k n) -> p s k n", s=2, k=DC)
        zT = big[:, 2 * DC * B:4 * DC * B].rearrange("p (s k n) -> p s k n", s=2, k=DC)
        x1T = big[:, 4 * DC * B:6 * DC * B].rearrange("p (s k n) -> p s k n", s=2, k=DC)
        yo = big[:, 6 * DC * B:6 * DC * B + 4 * D].bitcast(F32).rearrange("p (t n) -> p t n", t=2)
        ed = big[:, 0:4 * EC].bitcast(I32)
        winr = big[0:32, 6144:6144 + 2 * D].bitcast(F32)
        wout3 = big[0:96, 6144 + 2 * D:6144 + 4 * D].bitcast(F32)
        pm2 = big[:, 6144 + 4 * D:6144 + 4 * D + 4 * P].bitcast(F32).rearrange("p (c n) -> p c n", c=2)
        hots = sb("hots", [P, max(HC * P, 16 * B)], F16)
        onesb = hots[:, 0:HC * P].rearrange("p (c n) -> p c n", c=HC)
        qfeat = hots[:, 0:16 * B].rearrange("p (r s c n) -> p r s c n", r=4, s=2, c=2)
        tiles_hot = sb("tiles_hot", [P, max(HC * NTP, SRING * UNIT * P)], F16)
        onesa = tiles_hot[:, 0:HC * NTP].rearrange("p (c n) -> p c n", c=HC)
        hot = tiles_hot[:, 0:SRING * UNIT * P].rearrange("p (r i n) -> p r i n", r=SRING, i=UNIT)
        zz = sb("zz", [P, 2, D], F32)
        oo = sb("oo", [P, 2, D], F32)
        x1 = kvs[:].rearrange("p a d -> p (a d)")[:, 0:2 * D].rearrange("p (t n) -> p t n", t=2)
        pbr = hd[:].rearrange("p h n -> p (h n)")[:, 0:2 * D].bitcast(F32)
        own = vp[:].rearrange("p s t n -> p (s t n)")[:, 0:4 * D].rearrange("p (j n) -> p j n", j=2)
        srcw = sb("srcw", [P, 2, WIN], I32)
        dstw = sb("dstw", [P, 2, WIN], I32)
        dstl = sb("dstl", [P, 2, WIN], F32)
        den = sb("den", [P, 2, H], F32)
        rec = sb("rec", [P, 2, H], F32)
        gl = sb("gl", [P, 2, NN], F32)
        sg = sb("sg", [P, 2, NN], F32)
        ns = sb("ns", [P, 2, NN], F32)
        rr = sb("rr", [P, 2, NN], F32)
        cf = sb("cf", [P, 2, NN], F32)
        ux = sb("ux", [P, 2, NN], F32)
        su = sb("su", [P, 2, 4], F32)
        co = sb("co", [P, 2, 96], F16)
        coT = sb("coT", [96, B], F16)
        ring = region[:].rearrange("p (r n) -> p r n", n=2 * D)
        assert ring.shape[1] >= RING
        tin = [region[:, i * 2 * D:(i + 1) * 2 * D].bitcast(F32) for i in range(4)]
        tout = [region[:, (4 + i) * 2 * D:(5 + i) * 2 * D] for i in range(4)]
        dcol = hots[:, 0:2 * EC].bitcast(I32)
        assert 4 * EC <= 6144 and 2 * EC <= max(HC * P, 16 * B)
        wst = [zz, oo]

        padded = sem("padded")
        pad_ready = sem("pad_ready")
        edges_in = sem("edges_in")
        edges_split = sem("edges_split")
        consts = sem("consts")
        vconsts = sem("vconsts")
        w_in_s = [sem("w_in0"), sem("w_in1")]
        small_in = sem("small_in")
        w_turned = sem("w_turned")
        wg_hi = sem("wg_hi")
        wg_lo = sem("wg_lo")
        small_v = sem("small_v")
        slot_full = sem("slot_full")
        slot_a = sem("slot_a")
        slot_v = sem("slot_v")
        x_in = sem("x_in")
        stats = sem("stats")
        rstd = sem("rstd")
        normed = sem("normed")
        xn_out = sem("xn_out")
        xnt_out = sem("xnt_out")
        v_full = sem("v_full")
        v_hi = sem("v_hi")
        v_lo = sem("v_lo")
        v_summed = sem("v_summed")
        kv_full = sem("kv_full")
        kv_added = sem("kv_added")
        hots_built = sem("hots_built")
        vch = sem("vch")
        pch = sem("pch")
        mid_full = sem("mid_full")
        deg_done = sem("deg_done")
        dinv_done = sem("dinv_done")
        ranges_done = sem("ranges_done")
        mid_v = sem("mid_v")
        kv_ready = sem("kv_ready")
        tin_s = [sem(f"tin{i}") for i in range(4)]
        tout_s = [sem(f"tout{i}") for i in range(4)]
        t_hi = sem("t_hi")
        t_lo = sem("t_lo")
        xt_in = sem("xt_in")
        q_done = sem("q_done")
        win_s = [sem("win0"), sem("win1")]
        own_s = [sem("own0"), sem("own1")]
        local = sem("local")
        hot_ready = sem("hot_ready")
        chunk_used = sem("chunk_used")
        got = [sem(f"got{i}") for i in range(RING)]
        z_full = sem("z_full")
        z_read = sem("z_read")
        xr_in = sem("xr_in")
        xr_biased = sem("xr_biased")
        acc_full = sem("acc_full")
        acc_read = sem("acc_read")
        o_ready = sem("o_ready")
        x1_stats = sem("x1_stats")
        x1_rstd = sem("x1_rstd")
        x1_normed = sem("x1_normed")
        gelu_done = sem("gelu_done")
        coef = sem("coef")
        y_out = sem("y_out")
        stored = sem("stored")
        stats_passed = sem("stats_passed")
        gather_passed = sem("gather_passed")

        READ = {"W": "av", "T": "av", "K": "av", "F": "av", "H": "v", "Q": "av", "X": "av", "L": "av",
                "C": "a", "Z": "av", "O": "av"}
        NPREP = 3 * DC // 2 + DC // 2
        prep, prep_n = slots([("W", i, c) for i in range(NPREP) for c in range(3)]
                             + [("W", "pm", 0), ("W", "win", 0)], READ, None)

        def feat_uses(nt):
            return [("F", t, p) for t in range(nt) for p in range(H // 2)]

        def pass1(nt, before):
            return slots([("T", c, 0) for c in range(3)] + [("K", m, 0) for m in range(DC)] + [("H", 0, 0)]
                         + feat_uses(nt), READ, before)
        p1, p1_n = pass1(2, "F")
        p1_first, _ = pass1(2, "W")
        p1_tail, p1_tail_n = pass1(1, "F")
        base1 = prep_n
        tail1 = tuple(base1[i] + NB * p1_n[i] for i in range(3))
        base3 = tuple(tail1[i] + p1_tail_n[i] for i in range(3))
        assert base1[0] % 2 == 0 and p1_n[0] % 2 == 0

        def pass3(nt_prev, before, body=True):
            names = [("Q", 0, 0), ("Q", 1, 0)] if body else []
            names += [("X", c, 0) for c in range(3)] if nt_prev else []
            names += [("Q", 2, 0), ("Q", 3, 0)] if body else []
            names += [("L", t, 0) for t in range(nt_prev)]
            names += [("Q", 4, 0), ("Q", 5, 0)] if body else []
            names += [("C", 0, 0)] if nt_prev else []
            if body:
                names += [("F", h, 0) for h in range(H)] + [("Z", c, 0) for c in range(3)]
                names += [("O", c, 0) for c in range(3)]
            return slots(names, READ, before)
        p3_first, p3_first_n = pass3(0, "F")
        p3, p3_n = pass3(2, "O")
        p3_end, p3_end_n = pass3(1, "O", body=False)
        assert p3_n[0] % 2 == 0 and (base3[0] + p3_first_n[0]) % 1 == 0

        def bases1(b):
            return tuple(base1[i] + b * p1_n[i] for i in range(3))

        def bases3(b):
            if isinstance(b, int) and b == 0:
                return base3
            return tuple(base3[i] + p3_first_n[i] + (b - 1) * p3_n[i] for i in range(3))
        end3 = tuple(base3[i] + p3_first_n[i] + NB * p3_n[i] for i in range(3))

        def parity(base, u):
            return slot[(base + u[0]) % 2]
        par1 = base1[0] % 2
        par1_tail = tail1[0] % 2
        par3_first = base3[0] % 2
        par3 = (base3[0] + p3_first_n[0]) % 2
        par3_end = end3[0] % 2

        def acc_base(b):
            if isinstance(b, int) and b == 0:
                return 0
            return 4 + (b - 1) * 6

        PER = WIN // UNIT

        def unit_plan(nt):
            ahead, nu, at, u = (3, 2 * PER, [], 3) if nt == 2 else (2, PER, [], 2)
            for h in range(H):
                run = u < nu and u <= ahead + h * (nu - ahead) // (H - 1)
                at.append(u if run else None)
                u += run
            assert u == nu
            return ahead, at, [at.index(PER * (t + 1) - 1) for t in range(nt)]

        block = ctx.enter_context(nc.Block())

        @block.sync
        def _(sp):
            sp.dma_start(dst_pad[0:E].rearrange("(a n) -> a n", a=1), dst.rearrange("(a n) -> a n", a=1)).then_inc(padded, 16)
            sp.dma_start(src_pad[0:E].rearrange("(a n) -> a n", a=1), src.rearrange("(a n) -> a n", a=1)).then_inc(padded, 16)
            k_first = [DC // 2 + i for i in range(DC)] + [i for i in range(DC // 2)]
            rows = [("qkv", i) for i in k_first] + [("proj", i) for i in range(DC // 2)] + [("gnn", i) for i in range(DC // 2)]
            srcs = {"qkv": qkv_w, "proj": proj_w, "gnn": gnn_w}
            sp.dma_start(pm2[:, :, 0:DH], proj_mat.rearrange("(c p) d -> p c d", p=P)).then_inc(small_in, 16)
            sp.dma_start(pm2[:, :, DH:P], proj_mat.rearrange("(c p) d -> p c d", p=P)).then_inc(small_in, 16)
            sp.dma_start(winr[0:NN, :], w_in).then_inc(small_in, 16)
            sp.wait_ge(vconsts, 1)
            for g in range(3):
                sp.dma_start(wout3[32 * g:32 * g + NN, :], w_out).then_inc(small_in, 16)
            sp.dma_start(bqk_r[:], qkv_b.rearrange("(c p) -> p c", p=P), allow_slow_non_contiguous=True).then_inc(small_in, 16)
            sp.dma_start(gpb[:], gnn_b.rearrange("(a n) -> a n", a=1).broadcast_to([P, D])).then_inc(small_in, 16)
            sp.dma_start(pbr, proj_b.rearrange("(a n) -> a n", a=1).broadcast_to([P, D])).then_inc(small_in, 16)
            sp.dma_start(xa[:, :, :], x[0:B, :].rearrange("(t p) d -> p t d", p=P)).then_inc(x_in, 16)
            sp.wait_ge(pad_ready, 2)
            n_dst, n_src = EP + P - E, EP - E
            for dram, row, n in ((dst_pad, 0, n_dst), (src_pad, 1, n_src)):
                cols = -(-n // 2 // 1)
                del cols
                full, rest = n // P, n % P
                sp.dma_start(dram[E:E + full * P].rearrange("(r n) -> r n", n=P),
                             padrow[0:full, row * P:(row + 1) * P]).then_inc(padded, 16)
                if rest:
                    sp.dma_start(dram[E + full * P:E + n].rearrange("(a n) -> a n", a=1),
                                 padrow[0:1, row * P:row * P + rest]).then_inc(padded, 16)
            npad = 2 + sum(1 + bool(n % P) for n in (n_dst, n_src))
            sp.wait_ge(padded, 16 * npad)
            sp.dma_start(dcol, dst_pad[0:EP].rearrange("(p c) -> p c", p=P)).then_inc(edges_in, 16)
            for n, (kind, i) in enumerate(rows):
                if n >= 2:
                    m = n - 2
                    if m < NPREP:
                        sp.wait_ge(w_turned, m + 1)
                    else:
                        sp.wait_ge(wg_lo, m - NPREP + 1)
                sp.dma_start(wst[n % 2][:, :, :], srcs[kind][i * B:(i + 1) * B, :].rearrange("(t p) d -> p t d", p=P)).then_inc(w_in_s[n % 2], 16)

            def store_norm(b, nt, tok):
                if nt == 2:
                    sp.dma_start(xn_dram[bass.ds(b * B, B), :].rearrange("(t p) d -> p t d", p=P), xb[:, :, :]).then_inc(xn_out, 16)
                else:
                    sp.dma_start(xn_dram[b * B:b * B + tok, :], xb[0:tok, 0, :]).then_inc(xn_out, 16)

            def store_turned(b, w, n_v):
                sp.wait_ge(slot_v, n_v)
                sp.dma_start(xnt_dram[bass.ds(b * P, P), :].rearrange("p (s n) -> p s n", s=2 * DC)[:, :, 0:w],
                             xT[:, :, :, 0:w].rearrange("p s k n -> p (s k) n")).then_inc(xnt_out, 16)

            with sp.Fori(0, NB - 1) as b:
                sp.wait_ge(normed, 2 * b + 2)
                sp.dma_start(xa[:, :, :], x[bass.ds((b + 1) * B, B), :].rearrange("(t p) d -> p t d", p=P)).then_inc(x_in, 16)
                store_norm(b, 2, P)
                store_turned(b, B, bases1(b)[2] + 3)
            b = NB - 1
            sp.wait_ge(normed, 2 * b + 2)
            sp.dma_start(xa[0:TAIL, 0, :], x[NB * B:N, :]).then_inc(x_in, 16)
            store_norm(b, 2, P)
            store_turned(b, B, bases1(b)[2] + 3)
            sp.wait_ge(normed, 2 * NB + 1)
            store_norm(NB, 1, TAIL)
            store_turned(NB, TAIL, tail1[2] + 3)
            sp.wait_ge(xn_out, 16 * (NB + 1))
            sp.wait_ge(xnt_out, 16 * (NB + 1))

            sp.wait_ge(kv_added, 2 * (NB + 1))
            def table_in(t, i, tok):
                sp.dma_start(tin[i][0:tok, :], xn_dram[bass.ds(t * P, tok), :]).then_inc(tin_s[i], 16)

            def table_out(t, i, tok):
                sp.wait_ge(t_lo, t + 1)
                sp.dma_start(table[bass.ds(t * P, tok), :], tout[i][0:tok, :]).then_inc(tout_s[i], 16)

            for i in range(4):
                table_in(i, i, P)
            with sp.Fori(0, NT // 4 - 1) as g:
                for i in range(4):
                    table_out(4 * g + i, i, P)
                    table_in(4 * g + 4 + i, i, P)
            for i in range(4):
                table_out(NT // 4 * 4 - 4 + i, i, P)
            for t in range(NT // 4 * 4, NT):
                tok = P if t < NT - 1 else TAIL
                table_in(t, t % 4, tok)
                table_out(t, t % 4, tok)
            for i in range(4):
                sp.wait_ge(tout_s[i], 16 * ((NT - 1 - i) // 4 + 1))
            sp.wait_ge(ranges_done, 1)

            def load_turned(b, w):
                sp.dma_start(xT[:, :, :, 0:w].rearrange("p s k n -> p (s k) n"),
                             xnt_dram[bass.ds(b * P, P), :].rearrange("p (s n) -> p s n", s=2 * DC)[:, :, 0:w]).then_inc(xt_in, 16)

            def load_window(b, j, tok):
                at = sp.value_load(e0[0:1, bass.ds(2 * b + j, 1)], min_val=0, max_val=E)
                sp.dma_start(srcw[:, j, :], src_pad[bass.ds(at, WIN * P)].rearrange("(p k) -> p k", p=P)).then_inc(win_s[j], 16)
                sp.dma_start(dstw[:, j, :], dst_pad[bass.ds(at, WIN * P)].rearrange("(p k) -> p k", p=P)).then_inc(win_s[j], 16)
                sp.dma_start(own[0:tok, j, :], table[bass.ds(b * B + j * P, tok), :]).then_inc(own_s[j], 16)

            def load_residual(b, nt, tok):
                if nt == 2:
                    sp.dma_start(xa[:, :, :], x[bass.ds(b * B, B), :].rearrange("(t p) d -> p t d", p=P)).then_inc(xr_in, 16)
                else:
                    sp.dma_start(xa[0:tok, 0, :], x[b * B:b * B + tok, :]).then_inc(xr_in, 16)

            def store_out(b, n_y, nt=2, tok=P):
                sp.wait_ge(y_out, n_y)
                if nt == 2:
                    sp.dma_start(out[bass.ds(b * B, B), :].rearrange("(t p) d -> p t d", p=P), yo[:, :, :]).then_inc(stored, 16)
                else:
                    sp.dma_start(out[b * B:b * B + tok, :], yo[0:tok, 0, :]).then_inc(stored, 16)

            load_turned(0, B)
            load_window(0, 0, P)
            load_window(0, 1, P)
            load_residual(0, 2, P)

            def loads(b, nt=2, tok=P, store=True):
                sp.wait_ge(q_done, b)
                load_turned(b, B if nt == 2 else tok)
                if store:
                    store_out(b - 2, 2 * b - 2)
                for j in range(nt):
                    sp.wait_ge(z_full, 2 * b - 1 + j)
                    load_window(b, j, P if nt == 2 else tok)
                sp.wait_ge(x1_stats, 2 * b)
                load_residual(b, nt, tok)
            loads(1, store=False)
            with sp.Fori(2, NB) as b:
                loads(b)
            loads(NB, 1, TAIL)
            store_out(NB - 1, 2 * NB)
            store_out(NB, 2 * NB + 1, 1, TAIL)
            sp.wait_ge(stored, 16 * (NB + 1))

        @block.gpsimd
        def _(pool):
            g = nc.gpsimd
            n_chain = [0]

            def link(ins):
                n_chain[0] += 1
                ins.then_inc(pch, 1)
                pool.wait_ge(pch, n_chain[0])
            g.memset(padrow[:, 0:P], BIG).then_inc(pad_ready, 1)
            g.memset(padrow[:, P:2 * P], 0).then_inc(pad_ready, 1)
            link(g.memset(ident[:], 0.0))
            link(g.affine_select(out=ident[:], in_=ident[:], compare_op=ALU.not_equal, fill=1.0, base=0,
                                 pattern=[[-1, P]], channel_multiplier=1))
            g.tensor_copy(ident16[:], ident[:]).then_inc(consts, 1)
            link(g.iota(iota_i[:], pattern=[[1, P]], base=0, channel_multiplier=0))
            g.tensor_copy(iota16[:], iota_i[:]).then_inc(consts, 1)
            link(g.iota(tile_i[:], pattern=[[P, NTP]], base=0, channel_multiplier=0))
            g.tensor_copy(tile_base[:], tile_i[:]).then_inc(consts, 1)
            g.memset(ones[:], 1.0).then_inc(consts, 1)
            g.memset(epsk[:], ZS * EPS_FEAT).then_inc(consts, 1)
            link(g.memset(mhalf[:], -0.5))
            link(g.memset(eps_ln[:], EPS_LN))
            link(g.memset(vacc[:], 0.0))

            def inverse_std(n_stats, t, tok):
                pool.wait_ge(stats, n_stats)
                g.tensor_tensor(var_eps[0:tok, t:t + 1], mv[0:tok, t, 1:2], eps_ln[0:tok, :], ALU.add).then_inc(rstd, 1)
                pool.wait_ge(rstd, 2 * n_stats - 1)
                g.tensor_tensor(rs[0:tok, t:t + 1], var_eps[0:tok, t:t + 1], mhalf[0:tok, 0:1], ALU.pow).then_inc(rstd, 1)

            def sum_v(n, t, tok):
                pool.wait_ge(v_lo, n + 1)
                wait_for(pool, v_summed, 2 * n)
                g.tensor_tensor(vacc[0:tok, :], vacc[0:tok, :], vp[0:tok, 0, t, :], ALU.add).then_inc(v_summed, 1)
                pool.wait_ge(v_summed, 2 * n + 1)
                g.tensor_tensor(vacc[0:tok, :], vacc[0:tok, :], vp[0:tok, 1, t, :], ALU.add).then_inc(v_summed, 1)
            inverse_std(1, 0, P)
            inverse_std(2, 1, P)

            def gp1(b, nt_next, tok_next):
                for t in range(nt_next):
                    inverse_std(2 * b + 3 + t, t, tok_next)
                for t in range(2):
                    sum_v(2 * b + t, t, P)
            gp1(0, 2, P)
            with pool.Fori(1, NB - 1) as b:
                gp1(b, 2, P)
            gp1(NB - 1, 1, TAIL)
            sum_v(2 * NB, 0, TAIL)

            pool.wait_ge(deg_done, 1)
            link(g.tensor_scalar(scanB[:], degs[:], 1.0, None, ALU.add))
            g.tensor_tensor(dinv[:], scanB[:], mhalf[:], ALU.pow).then_inc(dinv_done, 1)

            def gather(b, k):
                j, r = k // WIN, k % RING
                if k % WIN == 0:
                    wait_apart(pool, win_s[j], 32 * (b + 1), gather_passed)
                wait_apart(pool, chunk_used, 2 * WIN * b + k - RING + 1, gather_passed)
                g.indirect_dma_start(ring[:, r, :], None, table,
                                     bass.IndirectOffsetOnAxis(ap=srcw[:, j, k % WIN:k % WIN + 1].bitcast(U32), axis=0)).then_inc(got[r], 16)

            def bias_residual(b, nt, tok):
                pool.wait_ge(xr_in, 16 * (b + 1))
                for t in range(nt):
                    g.tensor_tensor(xa[0:tok, t, :], xa[0:tok, t, :], gpb[0:tok, :], ALU.add).then_inc(xr_biased, 1)

            def inverse_std_x1(n, t, tok):
                pool.wait_ge(x1_stats, n)
                g.tensor_tensor(var_eps[0:tok, t:t + 1], mv[0:tok, t, 1:2], eps_ln[0:tok, :], ALU.add).then_inc(x1_rstd, 1)
                pool.wait_ge(x1_rstd, 2 * n - 1)
                g.tensor_tensor(rs[0:tok, t:t + 1], var_eps[0:tok, t:t + 1], mhalf[0:tok, 0:1], ALU.pow).then_inc(x1_rstd, 1)

            def gp3(b, nt=2, tok=P, prev=True):
                for k in range(RING):
                    gather(b, k)
                if prev:
                    for t in range(2):
                        inverse_std_x1(2 * b - 1 + t, t, P)
                for k in range(RING, nt * WIN):
                    gather(b, k)
                bias_residual(b, nt, tok)
            gp3(0, prev=False)
            with pool.Fori(1, NB) as b:
                gp3(b)
            gp3(NB, 1, TAIL)
            inverse_std_x1(2 * NB + 1, 0, TAIL)

        @block.scalar
        def _(act):
            a = nc.scalar

            def evac(base, u, ops):
                act.wait_ge(slot_full, base[0] + u[0] + 1)
                for o, i, f, kw in ops:
                    last = a.activation(o, i, f, **kw)
                last.then_inc(slot_a, 1)

            def weight_dest(i):
                w = (wk, wv, wq, wp)[i // 3]
                return w, (i % 3) * B
            for i in range(NPREP):
                w, c0 = weight_dest(i)
                for c in range(3):
                    u = prep[("W", i, c)]
                    evac((0, 0, 0), u, [(w[:, 0, 2 * c:2 * c + 2, c0:c0 + B],
                                         slot[u[0] % 2][:].rearrange("p (k n) -> p k n", k=2), ACT.Copy, dict(scale=WS))])
            u = prep[("W", "pm", 0)]
            evac((0, 0, 0), u, [(pmT[:, 0, :], slot[u[0] % 2][:, 0:M], ACT.Copy, {})])
            u = prep[("W", "win", 0)]
            evac((0, 0, 0), u, [(winT[:, 0, :, :], slot[u[0] % 2][:, 0:DC * 32].rearrange("p (k n) -> p k n", k=DC)[:, :, 0:NN], ACT.Copy, {})])
            for i in range(DC // 2):
                n = NPREP + i
                act.wait_ge(w_in_s[n % 2], 16 * (n // 2 + 1))
                a.activation(wg[:, 0, 2 * i:2 * i + 2, :], wst[n % 2][:, :, :], ACT.Copy, scale=WS).then_inc(wg_hi, 1)

            def turned_hi(base, par, plan, kind, dst_, w):
                for c in range(3):
                    u = plan[(kind, c, 0)]
                    evac(base, u, [(dst_[:, 0, 2 * c:2 * c + 2, 0:w],
                                    parity(par, u)[:].rearrange("p (k n) -> p k n", k=2)[:, :, 0:w], ACT.Copy, {})])

            def heads_hi(base, par, plan, kind, m, col, w):
                u = plan[(kind, m, 0)]
                s = parity(par, u)
                evac(base, u, [(hd[64 * e:64 * e + 64, 2 * m + e, 0:w], s[64 * e:64 * e + 64, 0:w], ACT.Identity,
                                dict(bias=bqk[64 * e:64 * e + 64, col + m:col + m + 1])) for e in range(2)])

            def act1(b, plan, nt, tok, base, par):
                w = B if nt == 2 else tok
                wait_for(act, xnt_out, 16 * b)
                turned_hi(base, par, plan, "T", xT, w)
                for m in range(DC):
                    heads_hi(base, par, plan, "K", m, DC, w)
                for t in range(nt):
                    for p in range(H // 2):
                        u = plan[("F", t, p)]
                        evac(base, u, [(kfeat[0:tok, 0, t, 2 * p * M:(2 * p + 2) * M], parity(par, u)[0:tok, :], ACT.Relu, {})])
                    act.wait_ge(v_full, 2 * b + t + 1)
                    wait_for(act, v_summed, 2 * (2 * b + t) - 2)
                    a.activation(vp[0:tok, 0, t, :].rearrange("p (h d) -> p h d", h=H)[:, :, 0:DH],
                                 acc[t][0:tok, 0:D].rearrange("p (h d) -> p h d", h=H), ACT.Copy).then_inc(v_hi, 1)
            act.wait_ge(small_v, 1)
            act1(0, p1_first, 2, P, bases1(0), par1)
            with act.Fori(1, NB) as b:
                act1(b, p1, 2, P, bases1(b), par1)
            act1(NB, p1_tail, 1, TAIL, tail1, par1_tail)

            act.wait_ge(dinv_done, 2)

            def table_hi(t, i, tok, n_in, n_out):
                act.wait_ge(tin_s[i], n_in)
                wait_for(act, tout_s[i], n_out)
                a.activation(tout[i][0:tok, 0:D], tin[i][0:tok, :], ACT.Copy, scale=dinvT[0:tok, bass.ds(t, 1)]).then_inc(t_hi, 1)
            for i in range(4):
                table_hi(i, i, P, 16, 0)
            with act.Fori(1, NT // 4) as g:
                for i in range(4):
                    table_hi(4 * g + i, i, P, 16 * g + 16, 16 * g)
            for t in range(NT // 4 * 4, NT):
                table_hi(t, t % 4, P if t < NT - 1 else TAIL, 16 * (t // 4 + 1), 16 * (t // 4))

            def ffn_a(b, plan, base, par, nt, tok, w):
                turned_hi(base, par, plan, "X", x1T, w)
                yield
                for t in range(nt):
                    u = plan[("L", t, 0)]
                    evac(base, u, [(gl[0:tok, t, :], parity(par, u)[0:tok, 0:NN], ACT.Gelu, {})])
                yield
                u = plan[("C", 0, 0)]
                evac(base, u, [(coT[:, 0:w], parity(par, u)[0:96, :].bitcast(F16)[:, 0:w], ACT.Copy, {})])
                yield

            def read_z(n, t, tok):
                act.wait_ge(z_full, n + 1)
                a.activation(zz[0:tok, t, :], zps[0:tok, 0:D], ACT.Copy, scale=dinvZ[0:tok, bass.ds(n, 1)]).then_inc(z_read, 1)

            def act3(b, plan, nt, tok, prev):
                base, w = bases3(b), (B if nt == 2 else tok)
                par = par3_first if prev is None else par3
                f = ffn_a(b - 1, plan, base, par, 2, P, B) if prev else None
                z_ends = unit_plan(nt)[2]
                for m in range(DC):
                    heads_hi(base, par, plan, "Q", m, 0, w)
                    if prev and m % 2 == 1:
                        next(f)
                for h in range(H):
                    u = plan[("F", h, 0)]
                    evac(base, u, [(qfeat[:, h % 4, 0, :, 0:w], parity(par, u)[:].rearrange("p (c n) -> p c n", c=2)[:, :, 0:w], ACT.Relu, {})])
                    if h in z_ends:
                        read_z(2 * b + z_ends.index(h), z_ends.index(h), tok)
                turned_hi(base, par, plan, "Z", zT, w)
                for c in range(3):
                    u = plan[("O", c, 0)]
                    s = parity(par, u)
                    evac(base, u, [(oT[:, 0, 2 * c + e, 0:w], s[:, e * B:e * B + w], ACT.Identity,
                                    dict(bias=bqk[:, 2 * DC + 2 * c + e:2 * DC + 2 * c + e + 1])) for e in range(2)])
            act3(0, p3_first, 2, P, None)
            with act.Fori(1, NB) as b:
                act3(b, p3, 2, P, True)
            act3(NB, p3, 1, TAIL, True)
            for _x in ffn_a(NB, p3_end, end3, par3_end, 1, TAIL, TAIL):
                pass

        @block.tensor
        def _(pe):
            def fill(base, u, need=0):
                wait_for(pe, slot_a, base[1] + u[3])
                wait_for(pe, slot_v, base[2] + max(u[4], need))

            zero = (0, 0, 0)
            pe.wait_ge(consts, 1)
            for i in range(NPREP):
                pe.wait_ge(w_in_s[i % 2], 16 * (i // 2 + 1))
                for c in range(3):
                    u = prep[("W", i, c)]
                    fill(zero, u)
                    for k in range(2):
                        for t in range(2):
                            mm = pe.transpose(slot[u[0] % 2][:, k * B + t * P:k * B + (t + 1) * P],
                                              wst[i % 2][:, t, (2 * c + k) * P:(2 * c + k + 1) * P], ident[:])
                    mm.then_inc(slot_full, 1)
                pe.wait_ge(slot_full, 3 * i + 3)
                pe.sem_inc(w_turned, 1)
            pe.wait_ge(small_in, 16 * 9)
            u = prep[("W", "pm", 0)]
            fill(zero, u)
            for c in range(2):
                mm = pe.transpose(slot[u[0] % 2][:, c * P:(c + 1) * P], pm2[:, c, :], ident[:])
            mm.then_inc(slot_full, 1)
            u = prep[("W", "win", 0)]
            fill(zero, u)
            for k in range(DC):
                mm = pe.transpose(slot[u[0] % 2][:, 32 * k:32 * k + NN], winr[0:NN, k * P:(k + 1) * P], ident[0:NN, 0:NN])
            mm.then_inc(slot_full, 1)

            def turn(base, par, plan, kind, what, nt, tok):
                for c in range(3):
                    u = plan[(kind, c, 0)]
                    fill(base, u)
                    for k in range(2):
                        for t in range(nt):
                            mm = pe.transpose(parity(par, u)[:, k * B + t * P:k * B + t * P + tok],
                                              what[0:tok, t, (2 * c + k) * P:(2 * c + k + 1) * P], ident[0:tok, 0:tok])
                    mm.then_inc(slot_full, 1)

            def project_heads(base, par, plan, kind, wgt, m, w, need=0):
                u = plan[(kind, m, 0)]
                fill(base, u, need)
                for i, (s, r) in enumerate(PAIRS):
                    for k in range(DC):
                        mm = pe.matmul(parity(par, u)[:, 0:w], wgt[:, r, k, m * P:(m + 1) * P], xT[:, s, k, 0:w],
                                       start=(i == 0 and k == 0), stop=(i == 2 and k == DC - 1))
                mm.then_inc(slot_full, 1)
                return mm

            def add_kv(n, half, nt, tok):
                wait_for(pe, kv_added, 2 * n + half)
                if half == 0:
                    pe.wait_ge(v_lo, 2 * n + nt)
                for i in range(12):
                    h, c = 6 * half + i // 2, i % 2
                    o = zps[:, (i // 6) * BANK + (i % 6) * DV:(i // 6) * BANK + (i % 6 + 1) * DV]
                    for t in range(nt):
                        for q, (s, r) in enumerate(PAIRS):
                            mm = pe.matmul(o, kfeat[0:tok, s, t, h * M + c * P:h * M + (c + 1) * P],
                                           vp[0:tok, r, t, h * DV:(h + 1) * DV],
                                           start=(t == 0 and q == 0), stop=(t == nt - 1 and q == 2))
                mm.then_inc(kv_full, 1)

            def histogram(base, par, plan, n):
                u = plan[("H", 0, 0)]
                pe.wait_ge(hots_built, n + 1)
                fill(base, u)
                for i in range(HC):
                    mm = pe.matmul(parity(par, u)[:, 0:NTP], onesb[:, i, :], onesa[:, i, :], start=(i == 0), stop=(i == HC - 1))
                mm.then_inc(slot_full, 1)

            def v_step(n, t, tok, i):
                s, r = PAIRS[i // DC]
                k = i % DC
                if i == 0:
                    wait_for(pe, v_lo, n - 1)
                for c0, c1 in ((0, BANK), (BANK, D)):
                    mm = pe.matmul(acc[t][0:tok, c0:c1], xT[:, s, k, t * P:t * P + tok], wv[:, r, k, c0:c1],
                                   start=(i == 0), stop=(i == 17))
                if i == 17:
                    mm.then_inc(v_full, 1)

            def pe1(b, plan, nt, tok, base, par, first=False):
                w = B if nt == 2 else tok
                pe.wait_ge(normed, 2 * b + nt)
                turn(base, par, plan, "T", xb, nt, tok)
                if not first:
                    add_kv(b - 1, 0, 2, P)
                for m in range(3):
                    project_heads(base, par, plan, "K", wk, m, w, need=3)
                if not first:
                    add_kv(b - 1, 1, 2, P)
                for m in range(3, DC):
                    project_heads(base, par, plan, "K", wk, m, w)
                histogram(base, par, plan, b)
                for t in range(nt):
                    for p in range(H // 2):
                        u = plan[("F", t, p)]
                        fill(base, u, need=plan[("K", p, 0)][2] + 1)
                        for e in range(2):
                            for r in range(2):
                                mm = pe.matmul(parity(par, u)[0:tok, e * M:(e + 1) * M], hd[:, 2 * p + e, t * P:t * P + tok],
                                               pmT[:, r, :], start=(r == 0), stop=(r == 1))
                        mm.then_inc(slot_full, 1)
                        for i in range(3 * p, 3 * p + 3):
                            v_step(2 * b + t, t, tok, i)
            pe.wait_ge(slot_v, prep_n[2])
            pe1(0, p1_first, 2, P, bases1(0), par1, first=True)
            with pe.Fori(1, NB) as b:
                pe1(b, p1, 2, P, bases1(b), par1)
            pe1(NB, p1_tail, 1, TAIL, tail1, par1_tail)
            add_kv(NB, 0, 1, TAIL)
            add_kv(NB, 1, 1, TAIL)

            half = H // 2 * DV
            pe.wait_ge(v_summed, 2 * NT)
            for i in range(2):
                mm = pe.matmul(acc[0][:, i * BANK:i * BANK + half], epsk[:], vacc[:, i * half:(i + 1) * half], start=True, stop=True)
            mm.then_inc(mid_full, 1)
            pe.wait_ge(deg_done, 1)
            pe.matmul(acc[1][:, 0:NTP], ones[:], degs[:], start=True, stop=True).then_inc(mid_full, 1)
            pe.wait_ge(mid_v, 1)
            pe.matmul(acc[1][:, BANK:BANK + H], ones[:], kf[:, 0:H], start=True, stop=True).then_inc(mid_full, 1)
            pe.wait_ge(mid_v, 2)
            kvv = kvs[:].rearrange("p (h c) d -> p h c d", c=2)
            for i in range(2):
                for c in range(2):
                    mm = pe.matmul(acc[0][:, i * BANK:i * BANK + half].rearrange("p (h d) -> p h d", d=DV), epsk[:],
                                   kvv[:, 6 * i:6 * i + 6, c, :], start=(c == 0), stop=(c == 1))
            mm.then_inc(mid_full, 1)
            pe.wait_ge(kv_ready, 1)

            def aggregate(b, u, nt):
                j, per = u // (WIN // UNIT), WIN // UNIT
                if u % per == 0:
                    wait_for(pe, z_read, 2 * b + j)
                pe.wait_ge(hot_ready, 2 * per * b + u + 1)
                for i in range(UNIT):
                    k = UNIT * u + i
                    pe.wait_ge(got[k % RING], 16 * ((2 * WIN // RING) * b + k // RING + 1))
                    for s in range(2):
                        for c0, c1 in ((0, BANK), (BANK, D)):
                            mm = pe.matmul(zps[:, c0:c1], hot[:, u % SRING, i, :], ring[:, k % RING, s * D + c0:s * D + c1],
                                           start=(k % WIN == 0 and s == 0), stop=False)
                    mm.then_inc(chunk_used, 1)

            def own_rows(b, j, tok):
                pe.wait_ge(own_s[j], 16 * (b + 1))
                for s in range(2):
                    for c0, c1 in ((0, BANK), (BANK, D)):
                        mm = pe.matmul(zps[:, c0:c1], ident16[0:tok, :], own[0:tok, j, s * D + c0:s * D + c1],
                                       start=False, stop=(s == 1))
                mm.then_inc(z_full, 1)

            def ffn_pe(plan, base, par, nt, tok, w, n_norm, n_coef, n_acc):
                pe.wait_ge(x1_normed, n_norm)
                turn(base, par, plan, "X", xb, nt, tok)
                yield
                for t in range(nt):
                    u = plan[("L", t, 0)]
                    fill(base, u, need=plan[("X", 2, 0)][2] + 1)
                    for i, (s, r) in enumerate(PAIRS):
                        for k in range(DC):
                            mm = pe.matmul(parity(par, u)[0:tok, 0:NN], x1T[:, s, k, t * P:t * P + tok], winT[:, r, k, :],
                                           start=(i == 0 and k == 0), stop=(i == 2 and k == DC - 1))
                    mm.then_inc(slot_full, 1)
                yield
                u = plan[("C", 0, 0)]
                pe.wait_ge(coef, n_coef)
                fill(base, u)
                for t in range(nt):
                    mm = pe.transpose(parity(par, u)[0:96, :].bitcast(F16)[:, t * P:t * P + tok], co[0:tok, t, :], ident16[0:tok, 0:tok])
                mm.then_inc(slot_full, 1)
                yield
                pe.wait_ge(slot_a, base[1] + u[1] + 1)
                for t in range(nt):
                    wait_for(pe, acc_read, n_acc + t - 1)
                    ac = acc[(t + n_acc0(n_acc)) % 2]
                    for c0, c1 in ((0, BANK), (BANK, D)):
                        mm = pe.matmul(ac[0:tok, c0:c1], coT[:, t * P:t * P + tok], wo[:, c0:c1], start=True, stop=True)
                    mm.then_inc(acc_full, 1)
                yield

            def n_acc0(n):
                return n % 2 if isinstance(n, int) else 0

            def attend(b, plan, h, nt, tok, w):
                for t in range(nt):
                    o = acc[t][0:tok, (h // 6) * BANK + (h % 6) * DV:(h // 6) * BANK + (h % 6 + 1) * DV]
                    for c in range(2):
                        for i, (s, r) in enumerate(PAIRS):
                            mm = pe.matmul(o, qfeat[:, h % 4, s, c, t * P:t * P + tok], kvp[:, r, 2 * h + c, :],
                                           start=(c == 0 and i == 0), stop=(c == 1 and i == 2))
                    if h == H - 1:
                        mm.then_inc(acc_full, 1)

            def pe3(b, plan, nt, tok, prev):
                base, w = bases3(b), (B if nt == 2 else tok)
                par = par3_first if prev is None else par3
                ab = acc_base(b)
                f = ffn_pe(plan, base, par, 2, P, B, 2 * b, b, ab) if prev else None
                pe.wait_ge(xt_in, 16 * (b + 1))
                ahead, unit_at, z_ends = unit_plan(nt)
                for m in range(DC):
                    mm = project_heads(base, par, plan, "Q", wq, m, w)
                    if prev and m in (1, 3):
                        next(f)
                    if m == 3:
                        for u in range(ahead - 1):
                            aggregate(b, u, nt)
                mm.then_inc(q_done, 1) if False else None
                pe.wait_ge(slot_full, base[0] + plan[("Q", 5, 0)][0] + 1)
                pe.sem_inc(q_done, 1)
                aggregate(b, ahead - 1, nt)
                if prev:
                    next(f)
                    next(f)
                na = ab + (2 if prev else 0)
                for t in range(nt):
                    wait_for(pe, acc_read, na + t - 1)
                for h in range(H + 1):
                    if h < H:
                        uf = plan[("F", h, 0)]
                        fill(base, uf, need=plan[("Q", h // 2, 0)][2] + 1)
                        for c in range(2):
                            for r in range(2):
                                mm = pe.matmul(parity(par, uf)[:, c * B:c * B + w], pmT[:, r, c * P:(c + 1) * P], hd[:, h, 0:w],
                                               start=(r == 0), stop=(r == 1))
                        mm.then_inc(slot_full, 1)
                        if unit_at[h] is not None:
                            aggregate(b, unit_at[h], nt)
                        if h in z_ends:
                            own_rows(b, z_ends.index(h), tok)
                    if h >= 1:
                        pe.wait_ge(slot_v, base[2] + plan[("F", h - 1, 0)][2] + 1)
                        attend(b, plan, h - 1, nt, tok, w)
                pe.wait_ge(z_read, 2 * b + nt)
                turn(base, par, plan, "Z", zz, nt, tok)
                pe.wait_ge(slot_v, base[2] + plan[("Z", 2, 0)][2] + 1)
                no = na + nt
                for t in range(nt):
                    if t == 0:
                        wait_for(pe, acc_read, no - 1)
                        convolve(nt, t, tok)
                pe.wait_ge(o_ready, 2 * b + nt)
                turn(base, par, plan, "O", oo, nt, tok)
                if nt == 2:
                    wait_for(pe, acc_read, no)
                    convolve(nt, 1, tok)
                pe.wait_ge(slot_v, base[2] + plan[("O", 2, 0)][2] + 1)
                for t in range(nt):
                    ac = acc[t] if nt == 2 else acc[1]
                    for i, (s, r) in enumerate(PAIRS):
                        for k in range(DC):
                            for c0, c1 in ((0, BANK), (BANK, D)):
                                mm = pe.matmul(ac[0:tok, c0:c1], oT[:, s, k, t * P:t * P + tok], wp[:, r, k, c0:c1],
                                               start=False, stop=(i == 2 and k == DC - 1))
                    mm.then_inc(acc_full, 1)

            def convolve(nt, t, tok):
                ac = acc[t] if nt == 2 else acc[1]
                for i, (s, r) in enumerate(PAIRS):
                    for k in range(DC):
                        for c0, c1 in ((0, BANK), (BANK, D)):
                            pe.matmul(ac[0:tok, c0:c1], zT[:, s, k, t * P:t * P + tok], wg[:, r, k, c0:c1],
                                      start=(i == 0 and k == 0), stop=False)
            pe3(0, p3_first, 2, P, None)
            with pe.Fori(1, NB) as b:
                pe3(b, p3, 2, P, True)
            pe3(NB, p3, 1, TAIL, True)
            n_last = acc_base(NB) + 4
            for _x in ffn_pe(p3_end, end3, par3_end, 1, TAIL, TAIL, 2 * NB + 1, NB + 1, n_last):
                pass

        @block.vector
        def _(dve):
            v = nc.vector
            v.memset(wout3, 0.0).then_inc(vconsts, 1)
            v.memset(kvs[:], 0.0)
            v.memset(degs[:], 0.0)
            v.memset(co[:], 0.0)
            v.memset(cf[:], 0.0)
            v.memset(vp[:, 1, :, :], 0.0)
            v.memset(vp[:, 0, :, :], 1.0).then_inc(vconsts, 1)
            dve.wait_ge(vconsts, 2)
            n_links = [0]

            class Chain:
                base, n = 0, 0

            def link(ins):
                Chain.n += 1
                ins.then_inc(vch, 1)
                dve.wait_ge(vch, Chain.base + Chain.n)
            del n_links

            def low(base, u, ops):
                dve.wait_ge(slot_a, base[1] + u[1] + 1)
                for f in ops:
                    last = f()
                last.then_inc(slot_v, 1)

            def stt(o, i0, sc, i1, op0, op1):
                return v.scalar_tensor_tensor(out=o, in0=i0, scalar=sc, in1=i1, op0=op0, op1=op1)

            dve.wait_ge(edges_in, 16)
            def split_edges():
                tmp = ed[:, 0:EC]
                link(v.tensor_scalar(tmp, dcol, P - 1, None, ALU.bitwise_and))
                v.tensor_copy(lo7[:], tmp)
                tmp2 = ed[:, EC:2 * EC]
                link(v.tensor_scalar(tmp2, dcol, 7, None, ALU.arith_shift_right))
                link(v.tensor_copy(hi7[:], tmp2))
            split_edges()
            dve.wait_ge(small_in, 16 * 9)
            v.tensor_scalar(bqk[:], bqk_r[:], WS, None, ALU.mult)
            v.tensor_copy(wo[:], wout3)
            link(v.tensor_tensor(gpb[:], gpb[:], pbr, ALU.add))
            link(v.tensor_tensor(wo[64:96, :], wout3[64:96, :], wo[64:96, :], ALU.subtract))
            v.memset(den[:], 0.0).then_inc(small_v, 1)

            def layernorm(n, t, tok, s_in, s_rstd, src_, dst_, s_stats, s_norm):
                for c in range(2):
                    v.bn_stats(st[0:tok, t, c, :], src_[0:tok, t, c * D // 2:(c + 1) * D // 2]).then_inc(vch, 1)
                Chain.n += 2
                wait_apart(dve, vch, Chain.base + Chain.n, stats_passed)
                v.bn_aggr(mv[0:tok, t, :], st[0:tok, t, :, :]).then_inc(s_stats, 1)

            def normalise(n, t, tok, s_rstd, s_stats, src_, dst_, s_norm):
                dve.wait_ge(s_rstd, 2 * n + 2)
                v.tensor_scalar(dst_[0:tok, t, :], src_[0:tok, t, :], mv[0:tok, t, 0:1], rs[0:tok, t:t + 1],
                                ALU.subtract, ALU.mult).then_inc(s_norm, 1)

            dve.wait_ge(x_in, 16)
            for t in range(2):
                layernorm(t, t, P, x_in, rstd, xa, xb, stats, normed)
            for t in range(2):
                normalise(t, t, P, rstd, stats, xa, xb, normed)
            for i in range(NPREP):
                w, c0 = (wk, wv, wq, wp)[i // 3], (i % 3) * B
                for c in range(3):
                    u = prep[("W", i, c)]
                    low((0, 0, 0), u, [lambda w=w, c0=c0, c=c, u=u: stt(
                        w[:, 1, 2 * c:2 * c + 2, c0:c0 + B], slot[u[0] % 2][:].rearrange("p (k n) -> p k n", k=2), WS,
                        w[:, 0, 2 * c:2 * c + 2, c0:c0 + B], ALU.mult, ALU.subtract)])
            u = prep[("W", "pm", 0)]
            low((0, 0, 0), u, [lambda: stt(pmT[:, 1, :], slot[u[0] % 2][:, 0:M], 1.0, pmT[:, 0, :], ALU.mult, ALU.subtract)])
            u2 = prep[("W", "win", 0)]
            low((0, 0, 0), u2, [lambda: stt(winT[:, 1, :, :], slot[u2[0] % 2][:, 0:DC * 32].rearrange("p (k n) -> p k n", k=DC)[:, :, 0:NN],
                                            1.0, winT[:, 0, :, :], ALU.mult, ALU.subtract)])
            for i in range(DC // 2):
                n = NPREP + i
                dve.wait_ge(wg_hi, i + 1)
                stt(wg[:, 1, 2 * i:2 * i + 2, :], wst[n % 2][:, :, :], WS, wg[:, 0, 2 * i:2 * i + 2, :], ALU.mult, ALU.subtract).then_inc(wg_lo, 1)
            dve.wait_ge(consts, 5)
            CH0 = Chain.n

            def turned_lo(base, par, plan, kind, dst_, w):
                for c in range(3):
                    u = plan[(kind, c, 0)]
                    low(base, u, [lambda c=c, u=u: stt(dst_[:, 1, 2 * c:2 * c + 2, 0:w],
                                                       parity(par, u)[:].rearrange("p (k n) -> p k n", k=2)[:, :, 0:w], 1.0,
                                                       dst_[:, 0, 2 * c:2 * c + 2, 0:w], ALU.mult, ALU.subtract)])

            def heads_lo(base, par, plan, kind, m, col, w):
                u = plan[(kind, m, 0)]
                s = parity(par, u)
                low(base, u, [lambda e=e: stt(hd[64 - 64 * e:128 - 64 * e, 2 * m + e, 0:w], s[64 * e:64 * e + 64, 0:w],
                                              bqk[64 * e:64 * e + 64, col + m:col + m + 1],
                                              hd[64 * e:64 * e + 64, 2 * m + e, 0:w], ALU.add, ALU.subtract) for e in range(2)])

            def flush_kv(n, half):
                dve.wait_ge(kv_full, 2 * n + half + 1)
                dst_ = kvs[:, 12 * half:12 * half + 12, :].rearrange("p (a i) d -> p a i d", a=2)
                src_ = zps[:].rearrange("p (a n) -> p a n", a=2)[:, :, 0:6 * DV].rearrange("p a (i d) -> p a i d", d=DV)
                wait_for(dve, kv_added, 2 * n + half)
                v.tensor_tensor(dst_, src_, dst_, ALU.add).then_inc(kv_added, 1)

            def build_hots(b):
                q = HC // 2
                for i, (c0, c1) in enumerate(((0, q), (q, HC))):
                    n = c1 - c0
                    v.tensor_tensor(onesb[:, c0:c1, :], iota16[:].unsqueeze(1).broadcast_to([P, n, P]),
                                    lo7[:, bass.ds(b * HC + c0, n)].unsqueeze(2).broadcast_to([P, n, P]), ALU.is_equal)
                last = v.tensor_tensor(onesa[:, :, :], iota16[:, 0:NTP].unsqueeze(1).broadcast_to([P, HC, NTP]),
                                       hi7[:, bass.ds(b * HC, HC)].unsqueeze(2).broadcast_to([P, HC, NTP]), ALU.is_equal)
                last.then_inc(hots_built, 1)

            def add_degrees(base, par, plan, b):
                u = plan[("H", 0, 0)]
                dve.wait_ge(slot_full, base[0] + u[0] + 1)
                v.tensor_tensor(degs[:], parity(par, u)[:, 0:NTP], degs[:], ALU.add).then_inc(slot_v, 1)

            def dve1(b, plan, nt, tok, base, par, first=False, nt_next=2, tok_next=P):
                w = B if nt == 2 else tok
                turned_lo(base, par, plan, "T", xT, w)
                build_hots(b)
                if not first:
                    flush_kv(b - 1, 0)
                for m in range(3):
                    heads_lo(base, par, plan, "K", m, DC, w)
                if not first:
                    flush_kv(b - 1, 1)
                for m in range(3, DC):
                    heads_lo(base, par, plan, "K", m, DC, w)
                add_degrees(base, par, plan, b)
                for t in range(nt):
                    for p in range(H // 2):
                        u = plan[("F", t, p)]
                        low(base, u, [lambda t=t, p=p, u=u: stt(kfeat[0:tok, 1, t, 2 * p * M:(2 * p + 2) * M], parity(par, u)[0:tok, :], 0.0,
                                                                kfeat[0:tok, 0, t, 2 * p * M:(2 * p + 2) * M], ALU.max, ALU.subtract)])
                        if nt_next and t == 0 and p in (1, 3):
                            tt = p // 2
                            if tt == 0:
                                dve.wait_ge(x_in, 16 * (b + 2))
                            if tt < nt_next:
                                layernorm(0, tt, tok_next, x_in, rstd, xa, xb, stats, normed)
                        if nt_next and t == 0 and p == 5:
                            dve.wait_ge(xn_out, 16 * (b + 1))
                            for tt in range(nt_next):
                                normalise(2 * b + 2 + tt, tt, tok_next, rstd, stats, xa, xb, normed)
                    dve.wait_ge(v_hi, 2 * b + t + 1)
                    v.tensor_tensor(vp[0:tok, 1, t, :].rearrange("p (h d) -> p h d", h=H)[:, :, 0:DH],
                                    acc[t][0:tok, 0:D].rearrange("p (h d) -> p h d", h=H),
                                    vp[0:tok, 0, t, :].rearrange("p (h d) -> p h d", h=H)[:, :, 0:DH], ALU.subtract).then_inc(v_lo, 1)

            dve1(0, p1_first, 2, P, bases1(0), par1, first=True)
            per = Chain.n - CH0
            with dve.Fori(1, NB - 1) as b:
                Chain.base, Chain.n = CH0 + b * per, 0
                dve1(b, p1, 2, P, bases1(b), par1)
            Chain.base, Chain.n = 0, CH0 + (NB - 1) * per
            dve1(NB - 1, p1, 2, P, bases1(NB - 1), par1, nt_next=1, tok_next=TAIL)
            dve1(NB, p1_tail, 1, TAIL, tail1, par1_tail, nt_next=0)
            flush_kv(NB, 0)
            flush_kv(NB, 1)

            dve.wait_ge(slot_v, base3[2])
            dve.wait_ge(kv_added, 2 * NB + 2)
            v.tensor_copy(scanA[:], degs[:]).then_inc(deg_done, 1)
            kvv = kvs[:].rearrange("p (h c) d -> p h c d", c=2)
            dve.wait_ge(mid_full, 1)
            vs = acc[0][:].rearrange("p (a n) -> p a n", a=2)[:, :, 0:6 * DV].rearrange("p a (h d) -> p a h d", d=DV)
            for c in range(2):
                for i in range(2):
                    last = v.tensor_tensor(kvv[:, 6 * i:6 * i + 6, c, :], vs[:, i, :, :], kvv[:, 6 * i:6 * i + 6, c, :], ALU.add)
                    if (c, i) != (1, 1):
                        link(last)
            link(last)
            v.tensor_tensor(kf[:, 0:H], kvv[:, :, 0, DH], kvv[:, :, 1, DH], ALU.add).then_inc(mid_v, 1)
            dve.wait_ge(mid_full, 2)
            link(v.tensor_copy(cnt[:], acc[1][:, 0:NTP]))
            link(v.tensor_copy(scanA[:], cnt[:]))
            a_, b_ = scanA, scanC
            s = 1
            while s < NTP:
                v.tensor_copy(b_[:, 0:s], a_[:, 0:s]).then_inc(vch, 1)
                Chain.n += 1
                link(v.tensor_tensor(b_[:, s:NTP], a_[:, s:NTP], a_[:, 0:NTP - s], ALU.add))
                a_, b_ = b_, a_
                s *= 2
            link(v.tensor_tensor(e0f[:], a_[:], cnt[:], ALU.subtract))
            link(v.tensor_copy(e0[:], e0f[:]))
            dve.wait_ge(dinv_done, 1)
            v.tensor_scalar(dinvT[:], dinv[:], TS, None, ALU.mult)
            link(v.tensor_scalar(dinvZ[:], dinv[:], WS / TS, None, ALU.mult))
            v.memset(den[:], 0.0).then_inc(dinv_done, 1)
            v.memset(rec[:], 0.0).then_inc(ranges_done, 1)
            dve.wait_ge(mid_full, 3)
            link(v.reciprocal(kf[:, 0:H], acc[1][:, BANK:BANK + H]))
            link(v.tensor_scalar(kf[:, H:2 * H], kf[:, 0:H], 1024.0, None, ALU.mult))
            kvf = kvs[:].rearrange("p (h c) d -> p h (c d)", c=2)
            link(v.tensor_tensor(kvf, kvf, kf[:, H:2 * H].unsqueeze(2).broadcast_to([P, H, 2 * DV]), ALU.mult))
            link(v.tensor_copy(kvp[:, 0, :, :], kvs[:]))
            link(v.tensor_tensor(kvp[:, 1, :, :], kvs[:], kvp[:, 0, :, :], ALU.subtract))
            v.memset(sg[:], 0.0).then_inc(mid_v, 1)
            dve.wait_ge(mid_full, 4)
            link(v.tensor_copy(cn.rearrange("p (a h) d -> p a h d", a=2), vs))
            v.memset(ns[:], 0.0).then_inc(kv_ready, 1)

            def table_lo(t, i, tok):
                dve.wait_ge(t_hi, t + 1)
                stt(tout[i][0:tok, D:2 * D], tin[i][0:tok, :], dinvT[0:tok, bass.ds(t, 1)], tout[i][0:tok, 0:D], ALU.mult, ALU.subtract).then_inc(t_lo, 1)
            with dve.Fori(0, NT // 4) as g:
                for i in range(4):
                    table_lo(4 * g + i, i, P)
            for t in range(NT // 4 * 4, NT):
                table_lo(t, t % 4, P if t < NT - 1 else TAIL)

            def localise(b, j):
                dve.wait_ge(win_s[j], 32 * (b + 1))
                link(v.tensor_scalar(dstl[:, j, :], dstw[:, j, :], tile_base[:, bass.ds(2 * b + j, 1)], None, ALU.subtract))

            def build_unit(b, u):
                j, k = u // (WIN // UNIT), UNIT * (u % (WIN // UNIT))
                wait_for(dve, chunk_used, 2 * WIN * b + UNIT * (u - SRING) + UNIT)
                v.tensor_tensor(hot[:, u % SRING, :, :], iota16[:].unsqueeze(1).broadcast_to([P, UNIT, P]),
                                dstl[:, j, k:k + UNIT].unsqueeze(2).broadcast_to([P, UNIT, P]), ALU.is_equal).then_inc(hot_ready, 1)

            def tree(nt, tok):
                T = slice(0, nt)
                R, C, G, S_, NS_ = (z[0:tok] for z in (rr, cf, gl, sg, ns))
                link(v.tensor_scalar(NS_[:, T, :], S_[:, T, :], -1.0, 1.0, ALU.mult, ALU.add))
                v.tensor_copy(R[:, T, 1:2], NS_[:, T, 0:1])
                link(v.tensor_copy(R[:, T, 2:3], S_[:, T, 0:1]))
                for n0, n1 in ((1, 3), (3, 7), (7, 10)):
                    kids = R[:, T, 2 * n0 + 1:2 * n1 + 1].rearrange("p t (n e) -> p t n e", e=2)
                    v.tensor_tensor(kids[:, :, :, 0], R[:, T, n0:n1], NS_[:, T, n0:n1], ALU.mult)
                    link(v.tensor_tensor(kids[:, :, :, 1], R[:, T, n0:n1], S_[:, T, n0:n1], ALU.mult))
                kids = C[:, T, 1:NN].rearrange("p t (n e) -> p t n e", e=2)
                rk = R[:, T, 1:NN].rearrange("p t (n e) -> p t n e", e=2)
                for e in range(2):
                    v.tensor_tensor(kids[:, :, :, e], rk[:, :, :, e], G[:, T, 0:10], ALU.mult)
                link(v.tensor_tensor(ux[0:tok, T, 10:20], R[:, T, 10:20], G[:, T, 10:20], ALU.mult))
                v.tensor_reduce(su[0:tok, T, 0:1], ux[0:tok, T, 10:20], mybir.AxisListType.X, ALU.add)
                link(v.tensor_reduce(su[0:tok, T, 1:2], R[:, T, 15:20], mybir.AxisListType.X, ALU.add))
                link(v.tensor_scalar(su[0:tok, T, 2:3], su[0:tok, T, 1:2], -1.0, 6.0, ALU.mult, ALU.add))
                link(v.tensor_tensor(su[0:tok, T, 3:4], su[0:tok, T, 2:3], G[:, T, 20:21], ALU.mult))
                link(v.tensor_tensor(su[0:tok, T, 0:1], su[0:tok, T, 0:1], su[0:tok, T, 3:4], ALU.add))
                link(v.tensor_tensor(C[:, T, 20:21], C[:, T, 20:21], su[0:tok, T, 0:1], ALU.add))
                v.tensor_copy(co[0:tok, T, 0:NN], C[:, T, :])
                link(v.tensor_copy(co[0:tok, T, 64:64 + NN], C[:, T, :]))
                v.tensor_tensor(co[0:tok, T, 32:32 + NN], C[:, T, :], co[0:tok, T, 0:NN], ALU.subtract).then_inc(coef, 1)

            def ffn_v(plan, base, par, nt, tok, w, n_acc, n_stored, par_acc=0):
                turned_lo(base, par, plan, "X", x1T, w)
                yield
                for t in range(nt):
                    u = plan[("L", t, 0)]
                    dve.wait_ge(slot_a, base[1] + u[1] + 1)
                    v.tensor_scalar(sg[0:tok, t, :], parity(par, u)[0:tok, 0:NN], 0.0, None, ALU.is_gt).then_inc(slot_v, 1)
                dve.wait_ge(slot_v, base[2] + plan[("L", nt - 1, 0)][2] + 1)
                tree(nt, tok)
                yield
                wait_for(dve, stored, n_stored)
                for t in range(nt):
                    dve.wait_ge(acc_full, n_acc + t + 1)
                    v.tensor_tensor(yo[0:tok, t, :], acc[(t + par_acc) % 2][0:tok, 0:D], x1[0:tok, t, :], ALU.add).then_inc(acc_read, 1)
                dve.wait_ge(acc_read, n_acc + nt)
                v.memset(ux[0:1, 0, 0:1], 0.0).then_inc(y_out, nt)
                yield

            def dve3(b, plan, nt, tok, prev):
                base, w = bases3(b), (B if nt == 2 else tok)
                par = par3_first if prev is None else par3
                ab = acc_base(b)
                f = ffn_v(plan, base, par, 2, P, B, ab, 16 * (b - 1)) if prev else None
                localise(b, 0)
                ahead, unit_at, _ = unit_plan(nt)
                build_unit(b, 0)
                build_unit(b, 1)
                for m in range(DC):
                    heads_lo(base, par, plan, "Q", m, 0, w)
                    if prev and m in (1, 3):
                        next(f)
                        if m == 3:
                            pass
                    if m == 3:
                        if ahead > 2:
                            build_unit(b, 2)
                if prev:
                    next(f)
                if nt == 2:
                    localise(b, 1)
                for h in range(H):
                    if unit_at[h] is not None:
                        build_unit(b, unit_at[h])
                    uf = plan[("F", h, 0)]
                    low(base, uf, [lambda h=h, uf=uf: stt(qfeat[:, h % 4, 1, :, 0:w], parity(par, uf)[:].rearrange("p (c n) -> p c n", c=2)[:, :, 0:w],
                                                          0.0, qfeat[:, h % 4, 0, :, 0:w], ALU.max, ALU.subtract)])
                na = ab + (2 if prev else 0)
                dve.wait_ge(acc_full, na + nt)
                for t in range(nt):
                    view = acc[t][0:tok, :].rearrange("p (a n) -> p a n", a=2)[:, :, 0:6 * DV].rearrange("p a (h d) -> p a h d", d=DV)
                    cv = cn[0:tok].rearrange("p (a h) d -> p a h d", a=2)
                    ov = oo[0:tok, t, :].rearrange("p (a h d) -> p a h d", a=2, d=DH)
                    dv = den[0:tok, t, :].rearrange("p (a h) -> p a h", a=2)
                    v.tensor_tensor(ov, view[:, :, :, 0:DH], cv[:, :, :, 0:DH], ALU.add).then_inc(vch, 1)
                    Chain.n += 1
                    v.tensor_tensor(dv, view[:, :, :, DH], cv[:, :, :, DH], ALU.add).then_inc(acc_read, 1)
                    dve.wait_ge(acc_read, na + t + 1)
                    link(v.reciprocal(rec[0:tok, t, :], den[0:tok, t, :]))
                    oh = oo[0:tok, t, :].rearrange("p (h d) -> p h d", h=H)
                    v.tensor_tensor(oh, oh, rec[0:tok, t, :].unsqueeze(2).broadcast_to([tok, H, DH]), ALU.mult).then_inc(o_ready, 1)
                turned_lo(base, par, plan, "Z", zT, w)
                for c in range(3):
                    u_ = plan[("O", c, 0)]
                    s_ = parity(par, u_)
                    low(base, u_, [lambda e=e, c=c, s_=s_: stt(oT[:, 1, 2 * c + e, 0:w], s_[:, e * B:e * B + w],
                                                              bqk[:, 2 * DC + 2 * c + e:2 * DC + 2 * c + e + 1],
                                                              oT[:, 0, 2 * c + e, 0:w], ALU.add, ALU.subtract) for e in range(2)])
                no = na + nt
                for t in range(nt):
                    ac = acc[t] if nt == 2 else acc[1]
                    dve.wait_ge(acc_full, no + t + 1)
                    dve.wait_ge(xr_biased, 2 * b + t + 1)
                    stt(x1[0:tok, t, :], ac[0:tok, 0:D], 1.0 / (WS * WS), xa[0:tok, t, :], ALU.mult, ALU.add).then_inc(acc_read, 1)
                    dve.wait_ge(acc_read, no + t + 1)
                    layernorm(0, t, tok, None, None, x1, None, x1_stats, None)

            def norm_x1(n, nt, tok):
                for t in range(nt):
                    normalise(n + t, t, tok, x1_rstd, x1_stats, x1, xb, x1_normed)
            C3 = Chain.n
            dve3(0, p3_first, 2, P, None)
            C3b = Chain.n
            norm_x1(0, 2, P)
            per3 = 2 + 12 + 2 * 2 + 2 * 2
            with dve.Fori(1, NB) as b:
                Chain.base, Chain.n = C3b + (b - 1) * per3, 0
                dve3(b, p3, 2, P, True)
                norm_x1(2 * b, 2, P)
                assert Chain.n == per3
            Chain.base, Chain.n = 0, C3b + (NB - 1) * per3
            dve3(NB, p3, 1, TAIL, True)
            norm_x1(2 * NB, 1, TAIL)
            n_last = acc_base(NB) + 4
            for _x in ffn_v(p3_end, end3, par3_end, 1, TAIL, TAIL, n_last, 16 * NB, par_acc=n_last % 2):
                pass
            del C3


_INS = ["x", "src", "dst", "L0_gnn_W", "L0_gnn_b", "L0_mix_qkv_w", "L0_mix_qkv_b", "L0_mix_proj_w", "L0_mix_proj_b",
        "L0_mix_proj_mat", "L0_ffn_weights_in", "L0_ffn_weights_out"]


def build(nc, arrays):
    args = [nc.dram_tensor(f"in_{n}", arrays[f"in_{n}"].shape, mybir.dt.from_np(arrays[f"in_{n}"].dtype), kind="ExternalInput").ap()
            for n in _INS]
    out = nc.dram_tensor("out_0", arrays["in_x"].shape, F32, kind="ExternalOutput").ap()
    gps_layer(nc, *args, out)


def kernel(**inputs):
    import numpy as np
    import concourse.bacc as bacc
    from concourse.bass_utils import run_bass_kernel_spmd

    nc = bacc.Bacc("TRN2", target_bir_lowering=False, num_devices=1)
    arrays = {f"in_{n}": np.ascontiguousarray(inputs[n]) for n in _INS}
    build(nc, arrays)
    return run_bass_kernel_spmd(nc, [arrays], core_ids=[0]).results[0]["out_0"]
```

```python
from contextlib import ExitStack

import concourse.bass as bass
from concourse import mybir

P = 128
ALU = mybir.AluOpType
ACT = mybir.ActivationFunctionType
F32 = mybir.dt.float32
F16 = mybir.dt.float16
I32 = mybir.dt.int32
U32 = mybir.dt.uint32

D = 768
DC = D // P
H = 12
DH = D // H
DV = DH + 1
M = 256
NN = 21
B = 2 * P
BANK = 512
WS = 8.0
ZS = 128.0
TS = 16.0
EPS_LN = 1e-5
EPS_FEAT = 1e-3
G = 4
GN = P // G
WIN = 5
RING = 10
SRING = 4
BIG = 1 << 20
PAIRS = ((0, 0), (1, 0), (0, 1))


def wait_for(eng, sem, value):
    if not (isinstance(value, int) and value <= 0):
        eng.wait_ge(sem, value)


def wait_apart(eng, sem, value, passed):
    if not (isinstance(value, int) and value <= 0):
        eng.wait_ge(sem, value)
        eng.sem_inc(passed, 1)


def slots(names, readers, before):
    out, n, a, v, last = {}, 0, 0, 0, before
    for u in names:
        r_last = readers[last] if last else "av"
        out[u] = (n, a, v, a - ("a" in r_last), v - ("v" in r_last))
        r = readers[u[0]]
        n, a, v, last = n + 1, a + ("a" in r), v + ("v" in r), u[0]
    return out, (n, a, v)


def gps_layer(nc, x, src, dst, gnn_w, gnn_b, qkv_w, qkv_b, proj_w, proj_b, proj_mat, w_in, w_out, out):
    N, E = x.shape[0], src.shape[0]
    NB, TAIL = N // B, N % B
    assert 0 < TAIL <= P and NB >= 3 and NB % 2 == 0
    NT = 2 * NB + 1
    NTP = NT + 1
    HC = -(-(E + WIN * P) // (P * (NB + 1)))
    EC = HC * (NB + 1)
    EP = EC * P
    NS = -(-E // (WIN * P))
    NPASS = -(-NT // 3)
    assert NS * WIN * P <= EP

    with ExitStack() as ctx:
        def sb(name, shape, dt):
            return ctx.enter_context(nc.sbuf_tensor(name, shape, dt))

        def sem(name):
            return ctx.enter_context(nc.semaphore(name))

        src_pad = nc.dram_tensor("src_pad", (EP,), I32).ap()
        dst_pad = nc.dram_tensor("dst_pad", (EP + P,), I32).ap()
        xn_dram = nc.dram_tensor("xn_dram", (N, D), F32).ap()
        xnt_dram = nc.dram_tensor("xnt_dram", ((NB + 1) * P, 2 * DC * B), F16).ap()
        table = nc.dram_tensor("table", (N, 2 * D), F16).ap()
        sums = nc.dram_tensor("sums", (NPASS * 3 * P, D), F32).ap()

        acc = [ctx.enter_context(nc.psum_tensor(f"acc{i}", [P, 2 * BANK], F32)) for i in range(2)]
        zps = ctx.enter_context(nc.psum_tensor("zps", [P, 2 * BANK], F32))
        slot = [ctx.enter_context(nc.psum_tensor(f"slot{i}", [P, BANK], F32)) for i in range(2)]

        ident = sb("ident", [P, P], F32)
        ident16 = sb("ident16", [P, P], F16)
        ones = sb("ones", [P, P], F32)
        epsk = sb("epsk", [P, P], F32)
        iota_i = sb("iota_i", [P, P], I32)
        iota16 = sb("iota16", [P, P], F16)
        padrow = sb("padrow", [P, 2 * P], I32)
        wq = sb("wq", [P, 2, DC, D], F16)
        wp = sb("wp", [P, 2, DC, D], F16)
        wg = sb("wg", [P, 2, DC, D], F16)
        region = sb("region", [P, 2 * 2 * DC * D], F16)
        wk = region[:, 0:2 * DC * D].rearrange("p (s k n) -> p s k n", s=2, k=DC)
        wv = region[:, 2 * DC * D:4 * DC * D].rearrange("p (s k n) -> p s k n", s=2, k=DC)
        pmT = sb("pmT", [P, 2, M], F16)
        winT = sb("winT", [P, 2, DC, NN], F16)
        wo = sb("wo", [96, D], F16)
        bqk_r = sb("bqk_r", [P, 3 * DC], F32)
        bqk = sb("bqk", [P, 3 * DC], F32)
        gpb = sb("gpb", [P, D], F32)
        lo7 = sb("lo7", [P, EC], F16)
        hi7 = sb("hi7", [P, EC], F16)
        degs = sb("degs", [P, NTP], F32)
        dinvT = sb("dinvT", [P, NTP], F32)
        dinvZ = sb("dinvZ", [P, NTP], F32)
        dinv = sb("dinv", [P, NTP], F32)
        scanA = sb("scanA", [P, NTP], F32)
        scanB = sb("scanB", [P, NTP], F32)
        scanC = sb("scanC", [P, NTP], F32)
        mhalf = sb("mhalf", [P, NTP], F32)
        var_eps = sb("var_eps", [P, 2], F32)
        eps_ln = sb("eps_ln", [P, 1], F32)
        cnt = sb("cnt", [P, NTP], F32)
        e0f = sb("e0f", [P, NTP], F32)
        e0 = sb("e0", [P, NTP], I32)
        below = sb("below", [P, G], F32)
        tile_base = sb("tile_base", [P, NTP + 2], F32)
        tile_i = sb("tile_i", [P, NTP + 2], I32)
        bad = sb("bad", [P, 4], F32)
        flag = sb("flag", [1, 1], I32)
        kvs = sb("kvs", [P, 24, DV], F32)
        kvp = sb("kvp", [P, 2, 24, DV], F16)
        vacc = sb("vacc", [P, H * DV], F32)
        cn = vacc[:].rearrange("p (h d) -> p h d", h=H)
        kf = sb("kf", [P, 2 * H], F32)
        xa = sb("xa", [P, 2, D], F32)
        xb = sb("xb", [P, 2, D], F32)
        st = sb("st", [P, 2, 2, 6], F32)
        mv = sb("mv", [P, 2, 2], F32)
        rs = sb("rs", [P, 2], F32)
        xT = sb("xT", [P, 2, DC, B], F16)
        hd = sb("hd", [P, H, B], F16)
        vp = sb("vp", [P, 2, 2, H * DV], F16)
        big = sb("big", [P, 2 * 2 * H * M], F16)
        kfeat = big[:].rearrange("p (s t n) -> p s t n", s=2, t=2)
        oT = big[:, 0:2 * DC * B].rearrange("p (s k n) -> p s k n", s=2, k=DC)
        zT = big[:, 2 * DC * B:4 * DC * B].rearrange("p (s k n) -> p s k n", s=2, k=DC)
        x1T = big[:, 4 * DC * B:6 * DC * B].rearrange("p (s k n) -> p s k n", s=2, k=DC)
        yo = big[:, 6 * DC * B:6 * DC * B + 4 * D].bitcast(F32).rearrange("p (t n) -> p t n", t=2)
        ed = big[:, 0:4 * EC].bitcast(I32)
        winr = big[0:32, 6144:6144 + 2 * D].bitcast(F32)
        wout3 = big[0:96, 6144 + 2 * D:6144 + 4 * D].bitcast(F32)
        pm2 = big[:, 6144 + 4 * D:6144 + 4 * D + 4 * P].bitcast(F32).rearrange("p (c n) -> p c n", c=2)
        hots = sb("hots", [P, max(HC * P, 16 * B)], F16)
        onesb = hots[:, 0:HC * P].rearrange("p (c n) -> p c n", c=HC)
        qfeat = hots[:, 0:16 * B].rearrange("p (r s c n) -> p r s c n", r=4, s=2, c=2)
        tiles_hot = sb("tiles_hot", [P, max(HC * NTP, SRING * P)], F16)
        onesa = tiles_hot[:, 0:HC * NTP].rearrange("p (c n) -> p c n", c=HC)
        hot = tiles_hot[:, 0:SRING * P].rearrange("p (r g n) -> p r g n", r=SRING, g=G)
        zz = sb("zz", [P, 2, D], F32)
        oo = sb("oo", [P, 2, D], F32)
        x1 = kvs[:].rearrange("p a d -> p (a d)")[:, 0:2 * D].rearrange("p (t n) -> p t n", t=2)
        pbr = hd[:].rearrange("p h n -> p (h n)")[:, 0:2 * D].bitcast(F32)
        own = vp[:].rearrange("p s t n -> p (s t n)")[:, 0:4 * D].rearrange("p (j n) -> p j n", j=2)
        srcw = sb("srcw", [P, 2, G, WIN], I32)
        dstw = sb("dstw", [P, 2, G, WIN], I32)
        dstl = sb("dstl", [P, 2, G, WIN], F32)
        den = sb("den", [P, 2, H], F32)
        rec = sb("rec", [P, 2, H], F32)
        gl = sb("gl", [P, 2, NN], F32)
        sg = sb("sg", [P, 2, NN], F32)
        ns = sb("ns", [P, 2, NN], F32)
        rr = sb("rr", [P, 2, NN], F32)
        cf = sb("cf", [P, 2, NN], F32)
        ux = sb("ux", [P, 2, NN], F32)
        su = sb("su", [P, 2, 4], F32)
        co = sb("co", [P, 2, 96], F16)
        coT = sb("coT", [96, B], F16)
        ring = region[:].rearrange("p (r n) -> p r n", n=2 * D)
        assert ring.shape[1] >= RING
        tin = [region[:, i * 2 * D:(i + 1) * 2 * D].bitcast(F32) for i in range(4)]
        tout = [region[:, (4 + i) * 2 * D:(5 + i) * 2 * D] for i in range(4)]
        dcol = hots[:, 0:2 * EC].bitcast(I32)
        dnext = hots[:, 2 * EC:4 * EC].bitcast(I32)
        assert 4 * EC <= 6144 and 4 * EC <= max(HC * P, 16 * B)
        same = zz[:, 0, 0:P]
        zero16 = tiles_hot[:, 0:BANK]
        sums3 = [zz[:, 0, :], zz[:, 1, :], xa[:, 0, :]]
        all_hot = oo[:].rearrange("p t n -> p (t n)").bitcast(F16)[:, 0:3 * WIN * P].rearrange("p (j k n) -> p j k n", j=3, k=WIN)
        away = dstl[:].rearrange("p j g k -> p (j g k)")[:, 0:3 * WIN].rearrange("p (j k) -> p j k", j=3)
        wst = [zz, oo]

        padded = sem("padded")
        pad_ready = sem("pad_ready")
        edges_in = sem("edges_in")
        edges_split = sem("edges_split")
        consts = sem("consts")
        vconsts = sem("vconsts")
        w_in_s = [sem("w_in0"), sem("w_in1")]
        small_in = sem("small_in")
        w_turned = sem("w_turned")
        wg_hi = sem("wg_hi")
        wg_lo = sem("wg_lo")
        small_v = sem("small_v")
        slot_full = sem("slot_full")
        slot_a = sem("slot_a")
        slot_v = sem("slot_v")
        x_in = sem("x_in")
        stats = sem("stats")
        rstd = sem("rstd")
        normed = sem("normed")
        xn_out = sem("xn_out")
        xnt_out = sem("xnt_out")
        v_full = sem("v_full")
        v_hi = sem("v_hi")
        v_lo = sem("v_lo")
        v_summed = sem("v_summed")
        kv_full = sem("kv_full")
        kv_added = sem("kv_added")
        hots_built = sem("hots_built")
        vch = sem("vch")
        pch = sem("pch")
        mid_full = sem("mid_full")
        deg_done = sem("deg_done")
        dinv_done = sem("dinv_done")
        ranges_done = sem("ranges_done")
        mid_v = sem("mid_v")
        kv_ready = sem("kv_ready")
        tin_s = [sem(f"tin{i}") for i in range(4)]
        tout_s = [sem(f"tout{i}") for i in range(4)]
        t_hi = sem("t_hi")
        t_lo = sem("t_lo")
        xt_in = sem("xt_in")
        q_done = sem("q_done")
        win_s = [sem("win0"), sem("win1")]
        own_s = [sem("own0"), sem("own1")]
        local = sem("local")
        hot_ready = sem("hot_ready")
        unit_used = sem("unit_used")
        got = [sem(f"got{i}") for i in range(RING)]
        z_full = sem("z_full")
        z_read = sem("z_read")
        xr_in = sem("xr_in")
        xr_biased = sem("xr_biased")
        acc_full = sem("acc_full")
        acc_read = sem("acc_read")
        o_ready = sem("o_ready")
        x1_stats = sem("x1_stats")
        x1_rstd = sem("x1_rstd")
        x1_normed = sem("x1_normed")
        gelu_done = sem("gelu_done")
        coef = sem("coef")
        stored = sem("stored")
        stats_passed = sem("stats_passed")
        bad_in = sem("bad_in")
        bad_full = sem("bad_full")
        flag_ready = sem("flag_ready")
        all_go = sem("all_go")
        all_zero = sem("all_zero")
        all_in = sem("all_in")
        all_got = [sem(f"all_got{k}") for k in range(WIN)]
        all_away = sem("all_away")
        all_hots = sem("all_hots")
        all_used = sem("all_used")
        all_sum = sem("all_sum")
        all_read = sem("all_read")
        all_out = sem("all_out")
        row_in = sem("row_in")
        row_chain = sem("row_chain")
        row_ready = sem("row_ready")
        row_out = sem("row_out")
        edges_passed = sem("edges_passed")
        all_done = sem("all_done")
        gather_passed = sem("gather_passed")

        READ = {"W": "av", "T": "av", "K": "av", "F": "av", "H": "v", "Q": "av", "X": "av", "L": "av",
                "C": "a", "Y": "v", "Z": "av", "O": "av"}
        NPREP = 3 * DC // 2 + DC // 2
        prep, prep_n = slots([("W", i, c) for i in range(NPREP) for c in range(3)]
                             + [("W", "pm", 0), ("W", "win", 0)], READ, None)

        def feat_uses(nt):
            return [("F", t, p) for t in range(nt) for p in range(H // 2)]

        def pass1(nt, before):
            f = feat_uses(nt)
            return slots([("T", c, 0) for c in range(3)] + [("K", m, 0) for m in range(DC)] + f[:4] + [("H", 0, 0)]
                         + f[4:], READ, before)
        p1, p1_n = pass1(2, "F")
        p1_first, _ = pass1(2, "W")
        p1_tail, p1_tail_n = pass1(1, "F")
        base1 = prep_n
        tail1 = tuple(base1[i] + NB * p1_n[i] for i in range(3))
        base3 = tuple(tail1[i] + p1_tail_n[i] for i in range(3))
        assert base1[0] % 2 == 0 and p1_n[0] % 2 == 0

        def pass3(nt_prev, before, body=True):
            def q(*ms):
                return [("Q", m, 0) for m in ms] if body else []

            def f(*hs):
                return [("F", h, 0) for h in hs] if body else []

            def prev(*us):
                return [u for u in us if u[1] < nt_prev or u[0] in "XC"] if nt_prev else []
            names = q(0, 1) + f(0, 1) + q(2) + f(2, 3) + q(3) + prev(("X", 0, 0), ("X", 1, 0), ("X", 2, 0))
            names += f(4, 5) + q(4) + prev(("L", 0, 0), ("L", 1, 0)) + f(6, 7) + q(5) + f(8, 9, 10, 11)
            if body:
                names += [("Z", c, 0) for c in range(3)]
            names += prev(("C", 0, 0))
            if body:
                names += [("O", c, 0) for c in range(3)]
            names += prev(*[("Y", t, i) for t in range(2) for i in range(2)])
            return slots(names, READ, before)
        p3_first, p3_first_n = pass3(0, "F")
        p3, p3_n = pass3(2, "O")
        p3_end, p3_end_n = pass3(1, "O", body=False)
        assert p3_n[0] % 2 == 0

        def bases1(b):
            return tuple(base1[i] + b * p1_n[i] for i in range(3))

        def bases3(b):
            if isinstance(b, int) and b == 0:
                return base3
            return tuple(base3[i] + p3_first_n[i] + (b - 1) * p3_n[i] for i in range(3))
        end3 = tuple(base3[i] + p3_first_n[i] + NB * p3_n[i] for i in range(3))

        def parity(base, u):
            return slot[(base + u[0]) % 2]
        par1 = base1[0] % 2
        par1_tail = tail1[0] % 2
        par3_first = base3[0] % 2
        par3 = (base3[0] + p3_first_n[0]) % 2
        par3_end = end3[0] % 2

        block = ctx.enter_context(nc.Block())

        @block.sync
        def _(sp):
            sp.dma_start(dst_pad[0:E].rearrange("(a n) -> a n", a=1), dst.rearrange("(a n) -> a n", a=1)).then_inc(padded, 16)
            sp.dma_start(src_pad[0:E].rearrange("(a n) -> a n", a=1), src.rearrange("(a n) -> a n", a=1)).then_inc(padded, 16)
            k_first = [DC // 2 + i for i in range(DC)] + [i for i in range(DC // 2)]
            rows = [("qkv", i) for i in k_first] + [("proj", i) for i in range(DC // 2)] + [("gnn", i) for i in range(DC // 2)]
            srcs = {"qkv": qkv_w, "proj": proj_w, "gnn": gnn_w}
            sp.dma_start(pm2[:, :, 0:DH], proj_mat.rearrange("(c p) d -> p c d", p=P)).then_inc(small_in, 16)
            sp.dma_start(pm2[:, :, DH:P], proj_mat.rearrange("(c p) d -> p c d", p=P)).then_inc(small_in, 16)
            sp.dma_start(winr[0:NN, :], w_in).then_inc(small_in, 16)
            sp.wait_ge(vconsts, 1)
            for g in range(3):
                sp.dma_start(wout3[32 * g:32 * g + NN, :], w_out).then_inc(small_in, 16)
            sp.dma_start(bqk_r[:], qkv_b.rearrange("(c p) -> p c", p=P), allow_slow_non_contiguous=True).then_inc(small_in, 16)
            sp.dma_start(gpb[:], gnn_b.rearrange("(a n) -> a n", a=1).broadcast_to([P, D])).then_inc(small_in, 16)
            sp.dma_start(pbr, proj_b.rearrange("(a n) -> a n", a=1).broadcast_to([P, D])).then_inc(small_in, 16)
            sp.dma_start(xa[:, :, :], x[0:B, :].rearrange("(t p) d -> p t d", p=P)).then_inc(x_in, 16)
            sp.wait_ge(pad_ready, 2)
            n_dst, n_src = EP + P - E, EP - E
            for dram, row, n in ((dst_pad, 0, n_dst), (src_pad, 1, n_src)):
                cols = -(-n // 2 // 1)
                del cols
                full, rest = n // P, n % P
                sp.dma_start(dram[E:E + full * P].rearrange("(r n) -> r n", n=P),
                             padrow[0:full, row * P:(row + 1) * P]).then_inc(padded, 16)
                if rest:
                    sp.dma_start(dram[E + full * P:E + n].rearrange("(a n) -> a n", a=1),
                                 padrow[0:1, row * P:row * P + rest]).then_inc(padded, 16)
            npad = 2 + sum(1 + bool(n % P) for n in (n_dst, n_src))
            sp.wait_ge(padded, 16 * npad)
            sp.dma_start(dcol, dst_pad[0:EP].rearrange("(p c) -> p c", p=P)).then_inc(edges_in, 16)
            sp.dma_start(dnext, dst_pad[1:EP + 1].rearrange("(p c) -> p c", p=P)).then_inc(edges_in, 16)
            for n, (kind, i) in enumerate(rows):
                if n >= 2:
                    m = n - 2
                    if m < NPREP:
                        sp.wait_ge(w_turned, m + 1)
                    else:
                        sp.wait_ge(wg_lo, m - NPREP + 1)
                sp.dma_start(wst[n % 2][:, :, :], srcs[kind][i * B:(i + 1) * B, :].rearrange("(t p) d -> p t d", p=P)).then_inc(w_in_s[n % 2], 16)

            def store_norm(b, nt, tok):
                if nt == 2:
                    sp.dma_start(xn_dram[bass.ds(b * B, B), :].rearrange("(t p) d -> p t d", p=P), xb[:, :, :]).then_inc(xn_out, 16)
                else:
                    sp.dma_start(xn_dram[b * B:b * B + tok, :], xb[0:tok, 0, :]).then_inc(xn_out, 16)

            def store_turned(b, w, n_v):
                sp.wait_ge(slot_v, n_v)
                sp.dma_start(xnt_dram[bass.ds(b * P, P), :].rearrange("p (s n) -> p s n", s=2 * DC)[:, :, 0:w],
                             xT[:, :, :, 0:w].rearrange("p s k n -> p (s k) n")).then_inc(xnt_out, 16)

            with sp.Fori(0, NB - 1) as b:
                sp.wait_ge(normed, 2 * b + 2)
                sp.dma_start(xa[:, :, :], x[bass.ds((b + 1) * B, B), :].rearrange("(t p) d -> p t d", p=P)).then_inc(x_in, 16)
                store_norm(b, 2, P)
                store_turned(b, B, bases1(b)[2] + 3)
            b = NB - 1
            sp.wait_ge(normed, 2 * b + 2)
            sp.dma_start(xa[0:TAIL, 0, :], x[NB * B:N, :]).then_inc(x_in, 16)
            store_norm(b, 2, P)
            store_turned(b, B, bases1(b)[2] + 3)
            sp.wait_ge(normed, 2 * NB + 1)
            store_norm(NB, 1, TAIL)
            store_turned(NB, TAIL, tail1[2] + 3)
            sp.wait_ge(xn_out, 16 * (NB + 1))
            sp.wait_ge(xnt_out, 16 * (NB + 1))

            sp.wait_ge(kv_added, 2 * (NB + 1) + 1)
            def table_in(t, i, tok):
                sp.dma_start(tin[i][0:tok, :], xn_dram[bass.ds(t * P, tok), :]).then_inc(tin_s[i], 16)

            def table_out(t, i, tok):
                sp.wait_ge(t_lo, t + 1)
                sp.dma_start(table[bass.ds(t * P, tok), :], tout[i][0:tok, :]).then_inc(tout_s[i], 16)

            for i in range(4):
                table_in(i, i, P)
            with sp.Fori(0, NT // 4 - 1) as g:
                for i in range(4):
                    table_out(4 * g + i, i, P)
                    table_in(4 * g + 4 + i, i, P)
            for i in range(4):
                table_out(NT // 4 * 4 - 4 + i, i, P)
            for t in range(NT // 4 * 4, NT):
                tok = P if t < NT - 1 else TAIL
                table_in(t, t % 4, tok)
                table_out(t, t % 4, tok)
            for i in range(4):
                sp.wait_ge(tout_s[i], 16 * ((NT - 1 - i) // 4 + 1))
            def general_sums():
                sp.sem_inc(all_go, 1)
                sp.sem_inc(all_out, 1)
                with sp.Fori(0, NPASS) as n:
                    with sp.Fori(0, NS) as i:
                        wait_apart(sp, all_used, n * NS + i + 1, edges_passed)
                        sp.dma_start(srcw[:, 0, 0, :], src_pad[bass.ds(i * (WIN * P), WIN * P)].rearrange("(p k) -> p k", p=P)).then_inc(all_in, 16)
                        sp.dma_start(dstw[:, 0, 0, :], dst_pad[bass.ds(i * (WIN * P), WIN * P)].rearrange("(p k) -> p k", p=P)).then_inc(all_in, 16)
                    wait_apart(sp, all_read, n + 2, edges_passed)
                    for j in range(3):
                        sp.dma_start(sums[bass.ds((3 * n + j) * P, P), :], sums3[j]).then_inc(all_out, 16)
                sp.wait_ge(all_out, 48 * NPASS + 1)

                def row(t, tok):
                    sp.dma_start(zz[0:tok, 0, :], sums[bass.ds(t * P, tok), :]).then_inc(row_in, 16)
                    sp.dma_start(own[0:tok, 0, :], table[bass.ds(t * P, tok), :]).then_inc(row_in, 16)
                    wait_apart(sp, row_ready, t + 1, edges_passed)
                    sp.dma_start(table[bass.ds(t * P, tok), :], own[0:tok, 1, :]).then_inc(row_out, 16)
                    wait_apart(sp, row_out, 16 * t + 16, edges_passed)
                with sp.Fori(0, NT - 1) as t:
                    row(t, P)
                row(NT - 1, TAIL)
                sp.sem_inc(all_done, 1)
                sp.wait_ge(all_done, 2)
            sp.wait_ge(flag_ready, 1)
            with sp.If(sp.value_load(flag[0:1, 0:1], min_val=0, max_val=1) > 0):
                general_sums()
            sp.wait_ge(ranges_done, 1)

            def load_turned(b, w):
                sp.dma_start(xT[:, :, :, 0:w].rearrange("p s k n -> p (s k) n"),
                             xnt_dram[bass.ds(b * P, P), :].rearrange("p (s n) -> p s n", s=2 * DC)[:, :, 0:w]).then_inc(xt_in, 16)

            def load_window(b, j, tok):
                for g in range(G):
                    at = sp.value_load(e0[g:g + 1, bass.ds(2 * b + j, 1)], min_val=0, max_val=E)
                    sp.dma_start(srcw[:, j, g, :], src_pad[bass.ds(at, WIN * P)].rearrange("(p k) -> p k", p=P)).then_inc(win_s[j], 16)
                    sp.dma_start(dstw[:, j, g, :], dst_pad[bass.ds(at, WIN * P)].rearrange("(p k) -> p k", p=P)).then_inc(win_s[j], 16)
                sp.dma_start(own[0:tok, j, :], table[bass.ds(b * B + j * P, tok), :]).then_inc(own_s[j], 16)

            def load_residual(b, nt, tok):
                if nt == 2:
                    sp.dma_start(xa[:, :, :], x[bass.ds(b * B, B), :].rearrange("(t p) d -> p t d", p=P)).then_inc(xr_in, 16)
                else:
                    sp.dma_start(xa[0:tok, 0, :], x[b * B:b * B + tok, :]).then_inc(xr_in, 16)

            def store_out(b, n_v, nt=2, tok=P):
                sp.wait_ge(slot_v, n_v)
                if nt == 2:
                    sp.dma_start(out[bass.ds(b * B, B), :].rearrange("(t p) d -> p t d", p=P), yo[:, :, :]).then_inc(stored, 16)
                else:
                    sp.dma_start(out[b * B:b * B + tok, :], yo[0:tok, 0, :]).then_inc(stored, 16)

            load_turned(0, B)
            load_window(0, 0, P)
            load_window(0, 1, P)
            load_residual(0, 2, P)

            def loads(b, nt=2, tok=P, store=True):
                sp.wait_ge(z_full, 2 * b - 1)
                load_window(b, 0, P if nt == 2 else tok)
                sp.wait_ge(q_done, b)
                load_turned(b, B if nt == 2 else tok)
                if nt == 2:
                    sp.wait_ge(z_full, 2 * b)
                    load_window(b, 1, P)
                if store:
                    store_out(b - 2, bases3(b - 1)[2] + p3[("Y", 1, 1)][2] + 1)
                sp.wait_ge(x1_stats, 2 * b)
                if store:
                    sp.wait_ge(stored, 16 * (b - 1))
                load_residual(b, nt, tok)
            loads(1, store=False)
            with sp.Fori(2, NB) as b:
                loads(b)
            loads(NB, 1, TAIL)
            store_out(NB - 1, bases3(NB)[2] + p3[("Y", 1, 1)][2] + 1)
            store_out(NB, end3[2] + p3_end[("Y", 0, 1)][2] + 1, 1, TAIL)
            sp.wait_ge(stored, 16 * (NB + 1))

        @block.gpsimd
        def _(pool):
            g = nc.gpsimd
            n_chain = [0]

            def link(ins):
                n_chain[0] += 1
                ins.then_inc(pch, 1)
                pool.wait_ge(pch, n_chain[0])
            g.memset(padrow[:, 0:P], BIG).then_inc(pad_ready, 1)
            g.memset(padrow[:, P:2 * P], 0).then_inc(pad_ready, 1)
            link(g.memset(ident[:], 0.0))
            link(g.affine_select(out=ident[:], in_=ident[:], compare_op=ALU.not_equal, fill=1.0, base=0,
                                 pattern=[[-1, P]], channel_multiplier=1))
            g.tensor_copy(ident16[:], ident[:]).then_inc(consts, 1)
            link(g.iota(iota_i[:], pattern=[[1, P]], base=0, channel_multiplier=0))
            g.tensor_copy(iota16[:], iota_i[:]).then_inc(consts, 1)
            link(g.iota(tile_i[:], pattern=[[P, NTP + 2]], base=0, channel_multiplier=0))
            g.tensor_copy(tile_base[:], tile_i[:]).then_inc(consts, 1)
            link(g.memset(ones[:], 1.0))
            g.memset(epsk[:], ZS * EPS_FEAT).then_inc(consts, 1)
            link(g.memset(mhalf[:], -0.5))
            link(g.memset(eps_ln[:], EPS_LN))
            for i in range(G):
                link(g.affine_select(out=below[:, i:i + 1], in_=ones[:, 0:1], compare_op=ALU.is_gt, fill=0.0,
                                     base=GN * i, pattern=[[0, 1]], channel_multiplier=-1))
            g.memset(var_eps[:], 0.0).then_inc(consts, 1)
            link(g.memset(vacc[:], 0.0))

            def inverse_std(n_stats, t, tok):
                pool.wait_ge(stats, n_stats)
                g.tensor_tensor(var_eps[0:tok, t:t + 1], mv[0:tok, t, 1:2], eps_ln[0:tok, :], ALU.add).then_inc(rstd, 1)
                pool.wait_ge(rstd, 2 * n_stats - 1)
                g.tensor_tensor(rs[0:tok, t:t + 1], var_eps[0:tok, t:t + 1], mhalf[0:tok, 0:1], ALU.pow).then_inc(rstd, 1)

            def sum_v(n, t, tok):
                pool.wait_ge(v_lo, n + 1)
                wait_for(pool, v_summed, 2 * n)
                g.tensor_tensor(vacc[0:tok, :], vacc[0:tok, :], vp[0:tok, 0, t, :], ALU.add).then_inc(v_summed, 1)
                pool.wait_ge(v_summed, 2 * n + 1)
                g.tensor_tensor(vacc[0:tok, :], vacc[0:tok, :], vp[0:tok, 1, t, :], ALU.add).then_inc(v_summed, 1)
            inverse_std(1, 0, P)
            inverse_std(2, 1, P)

            def gp1(b, nt_next, tok_next):
                for t in range(nt_next):
                    inverse_std(2 * b + 3 + t, t, tok_next)
                for t in range(2):
                    sum_v(2 * b + t, t, P)
            gp1(0, 2, P)
            with pool.Fori(1, NB - 1) as b:
                gp1(b, 2, P)
            gp1(NB - 1, 1, TAIL)
            sum_v(2 * NB, 0, TAIL)

            pool.wait_ge(deg_done, 1)
            link(g.tensor_scalar(scanB[:], degs[:], 1.0, None, ALU.add))
            g.tensor_tensor(dinv[:], scanB[:], mhalf[:], ALU.pow).then_inc(dinv_done, 1)

            def general_sums():
                pool.wait_ge(all_go, 1)
                with pool.Fori(0, NPASS) as n:
                    with pool.Fori(0, NS) as i:
                        wait_apart(pool, all_in, 32 * (n * NS + i) + 32, gather_passed)
                        for k in range(WIN):
                            g.indirect_dma_start(ring[:, k, :], None, table,
                                                 bass.IndirectOffsetOnAxis(ap=srcw[:, 0, 0, k:k + 1].bitcast(U32), axis=0)).then_inc(all_got[k], 16)
                pool.wait_ge(all_done, 2)
            pool.wait_ge(flag_ready, 1)
            with pool.If(pool.value_load(flag[0:1, 0:1], min_val=0, max_val=1) > 0):
                general_sums()

            def gather(b, k):
                j, u, g_, r = k // (G * WIN), k % (G * WIN) // G, k % G, k % RING
                if k % (G * WIN) == 0:
                    wait_apart(pool, win_s[j], 2 * G * 16 * (b + 1), gather_passed)
                wait_apart(pool, unit_used, 2 * WIN * b + (k - RING) // G + 1, gather_passed)
                g.indirect_dma_start(ring[:, r, :], None, table,
                                     bass.IndirectOffsetOnAxis(ap=srcw[:, j, g_, u:u + 1].bitcast(U32), axis=0)).then_inc(got[r], 16)

            def bias_residual(b, nt, tok):
                pool.wait_ge(xr_in, 16 * (b + 1))
                for t in range(nt):
                    g.tensor_tensor(xa[0:tok, t, :], xa[0:tok, t, :], gpb[0:tok, :], ALU.add).then_inc(xr_biased, 1)

            def inverse_std_x1(n, t, tok):
                pool.wait_ge(x1_stats, n)
                g.tensor_tensor(var_eps[0:tok, t:t + 1], mv[0:tok, t, 1:2], eps_ln[0:tok, :], ALU.add).then_inc(x1_rstd, 1)
                pool.wait_ge(x1_rstd, 2 * n - 1)
                g.tensor_tensor(rs[0:tok, t:t + 1], var_eps[0:tok, t:t + 1], mhalf[0:tok, 0:1], ALU.pow).then_inc(x1_rstd, 1)

            def gp3(b, nt=2, tok=P, prev=True):
                n = 3 * RING if nt == 2 else G * WIN
                for k in range(n):
                    gather(b, k)
                if prev:
                    for t in range(2):
                        inverse_std_x1(2 * b - 1 + t, t, P)
                for k in range(n, nt * G * WIN):
                    gather(b, k)
                bias_residual(b, nt, tok)
            gp3(0, prev=False)
            with pool.Fori(1, NB) as b:
                gp3(b)
            gp3(NB, 1, TAIL)
            inverse_std_x1(2 * NB + 1, 0, TAIL)

        @block.scalar
        def _(act):
            a = nc.scalar

            def evac(base, u, ops):
                act.wait_ge(slot_full, base[0] + u[0] + 1)
                for o, i, f, kw in ops:
                    last = a.activation(o, i, f, **kw)
                last.then_inc(slot_a, 1)

            def weight_dest(i):
                w = (wk, wv, wq, wp)[i // 3]
                return w, (i % 3) * B
            for i in range(NPREP):
                w, c0 = weight_dest(i)
                for c in range(3):
                    u = prep[("W", i, c)]
                    evac((0, 0, 0), u, [(w[:, 0, 2 * c:2 * c + 2, c0:c0 + B],
                                         slot[u[0] % 2][:].rearrange("p (k n) -> p k n", k=2), ACT.Copy, dict(scale=WS))])
            u = prep[("W", "pm", 0)]
            evac((0, 0, 0), u, [(pmT[:, 0, :], slot[u[0] % 2][:, 0:M], ACT.Copy, {})])
            u = prep[("W", "win", 0)]
            evac((0, 0, 0), u, [(winT[:, 0, :, :], slot[u[0] % 2][:, 0:DC * 32].rearrange("p (k n) -> p k n", k=DC)[:, :, 0:NN], ACT.Copy, {})])
            for i in range(DC // 2):
                n = NPREP + i
                act.wait_ge(w_in_s[n % 2], 16 * (n // 2 + 1))
                a.activation(wg[:, 0, 2 * i:2 * i + 2, :], wst[n % 2][:, :, :], ACT.Copy, scale=WS).then_inc(wg_hi, 1)

            def turned_hi(base, par, plan, kind, dst_, w, cs=range(3)):
                for c in cs:
                    u = plan[(kind, c, 0)]
                    evac(base, u, [(dst_[:, 0, 2 * c:2 * c + 2, 0:w],
                                    parity(par, u)[:].rearrange("p (k n) -> p k n", k=2)[:, :, 0:w], ACT.Copy, {})])

            def heads_hi(base, par, plan, kind, m, col, w):
                u = plan[(kind, m, 0)]
                s = parity(par, u)
                evac(base, u, [(hd[64 * e:64 * e + 64, 2 * m + e, 0:w], s[64 * e:64 * e + 64, 0:w], ACT.Identity,
                                dict(bias=bqk[64 * e:64 * e + 64, col + m:col + m + 1])) for e in range(2)])

            def act1(b, plan, nt, tok, base, par):
                w = B if nt == 2 else tok
                wait_for(act, xnt_out, 16 * b)
                turned_hi(base, par, plan, "T", xT, w)
                for m in range(DC):
                    heads_hi(base, par, plan, "K", m, DC, w)
                for t in range(nt):
                    for p in range(H // 2):
                        u = plan[("F", t, p)]
                        evac(base, u, [(kfeat[0:tok, 0, t, 2 * p * M:(2 * p + 2) * M], parity(par, u)[0:tok, :], ACT.Relu, {})])
                    act.wait_ge(v_full, 2 * b + t + 1)
                    wait_for(act, v_summed, 2 * (2 * b + t) - 2)
                    a.activation(vp[0:tok, 0, t, :].rearrange("p (h d) -> p h d", h=H)[:, :, 0:DH],
                                 acc[t][0:tok, 0:D].rearrange("p (h d) -> p h d", h=H), ACT.Copy).then_inc(v_hi, 1)
            act.wait_ge(small_v, 1)
            act1(0, p1_first, 2, P, bases1(0), par1)
            with act.Fori(1, NB) as b:
                act1(b, p1, 2, P, bases1(b), par1)
            act1(NB, p1_tail, 1, TAIL, tail1, par1_tail)

            act.wait_ge(dinv_done, 2)

            def table_hi(t, i, tok, n_in, n_out):
                act.wait_ge(tin_s[i], n_in)
                wait_for(act, tout_s[i], n_out)
                a.activation(tout[i][0:tok, 0:D], tin[i][0:tok, :], ACT.Copy, scale=dinvT[0:tok, bass.ds(t, 1)]).then_inc(t_hi, 1)
            for i in range(4):
                table_hi(i, i, P, 16, 0)
            with act.Fori(1, NT // 4) as g:
                for i in range(4):
                    table_hi(4 * g + i, i, P, 16 * g + 16, 16 * g)
            for t in range(NT // 4 * 4, NT):
                table_hi(t, t % 4, P if t < NT - 1 else TAIL, 16 * (t // 4 + 1), 16 * (t // 4))

            def general_sums():
                act.sem_inc(all_read, 1)
                with act.Fori(0, NPASS) as n:
                    act.wait_ge(all_sum, n + 1)
                    act.wait_ge(all_out, 48 * n + 1)
                    for o, to in zip((acc[0], acc[1], zps), sums3):
                        last = a.activation(to, o[:, 0:D], ACT.Copy)
                    last.then_inc(all_read, 1)
                act.wait_ge(all_done, 2)
            act.wait_ge(flag_ready, 1)
            with act.If(act.value_load(flag[0:1, 0:1], min_val=0, max_val=1) > 0):
                general_sums()

            def logits_hi(base, par, plan, nt, tok):
                for t in range(nt):
                    u = plan[("L", t, 0)]
                    evac(base, u, [(gl[0:tok, t, :], parity(par, u)[0:tok, 0:NN], ACT.Gelu, {})])

            def coefficients(base, par, plan, w):
                u = plan[("C", 0, 0)]
                evac(base, u, [(coT[:, 0:w], parity(par, u)[0:96, :].bitcast(F16)[:, 0:w], ACT.Copy, {})])

            def read_z(n, t, tok):
                act.wait_ge(z_full, n + 1)
                a.activation(zz[0:tok, t, :], zps[0:tok, 0:D], ACT.Copy, scale=dinvZ[0:tok, bass.ds(n, 1)]).then_inc(z_read, 1)

            def act3(b, plan, nt, tok, prev):
                base, w = bases3(b), (B if nt == 2 else tok)
                par = par3_first if prev is None else par3
                read_z(2 * b, 0, tok)

                def features(h):
                    u = plan[("F", h, 0)]
                    evac(base, u, [(qfeat[:, h % 4, 0, :, 0:w], parity(par, u)[:].rearrange("p (c n) -> p c n", c=2)[:, :, 0:w], ACT.Relu, {})])

                def q_heads(m):
                    heads_hi(base, par, plan, "Q", m, 0, w)
                q_heads(0)
                q_heads(1)
                features(0)
                features(1)
                q_heads(2)
                features(2)
                features(3)
                q_heads(3)
                if prev:
                    turned_hi(base, par, plan, "X", x1T, B)
                features(4)
                features(5)
                q_heads(4)
                if prev:
                    logits_hi(base, par, plan, 2, P)
                features(6)
                features(7)
                q_heads(5)
                for h in range(8, 10):
                    features(h)
                if nt == 2:
                    read_z(2 * b + 1, 1, tok)
                features(10)
                features(11)
                turned_hi(base, par, plan, "Z", zT, w)
                if prev:
                    coefficients(base, par, plan, B)
                for c in range(3):
                    u = plan[("O", c, 0)]
                    s = parity(par, u)
                    evac(base, u, [(oT[:, 0, 2 * c + e, 0:w], s[:, e * B:e * B + w], ACT.Identity,
                                    dict(bias=bqk[:, 2 * DC + 2 * c + e:2 * DC + 2 * c + e + 1])) for e in range(2)])
            act3(0, p3_first, 2, P, None)
            with act.Fori(1, NB) as b:
                act3(b, p3, 2, P, True)
            act3(NB, p3, 1, TAIL, True)
            turned_hi(end3, par3_end, p3_end, "X", x1T, TAIL)
            logits_hi(end3, par3_end, p3_end, 1, TAIL)
            coefficients(end3, par3_end, p3_end, TAIL)

        @block.tensor
        def _(pe):
            def fill(base, u, need=0):
                wait_for(pe, slot_a, base[1] + u[3])
                wait_for(pe, slot_v, base[2] + max(u[4], need))

            zero = (0, 0, 0)
            pe.wait_ge(consts, 1)
            for i in range(NPREP):
                pe.wait_ge(w_in_s[i % 2], 16 * (i // 2 + 1))
                for c in range(3):
                    u = prep[("W", i, c)]
                    fill(zero, u)
                    for k in range(2):
                        for t in range(2):
                            mm = pe.transpose(slot[u[0] % 2][:, k * B + t * P:k * B + (t + 1) * P],
                                              wst[i % 2][:, t, (2 * c + k) * P:(2 * c + k + 1) * P], ident[:])
                    mm.then_inc(slot_full, 1)
                pe.wait_ge(slot_full, 3 * i + 3)
                pe.sem_inc(w_turned, 1)
            pe.wait_ge(small_in, 16 * 9)
            u = prep[("W", "pm", 0)]
            fill(zero, u)
            for c in range(2):
                mm = pe.transpose(slot[u[0] % 2][:, c * P:(c + 1) * P], pm2[:, c, :], ident[:])
            mm.then_inc(slot_full, 1)
            u = prep[("W", "win", 0)]
            fill(zero, u)
            for k in range(DC):
                mm = pe.transpose(slot[u[0] % 2][:, 32 * k:32 * k + NN], winr[0:NN, k * P:(k + 1) * P], ident[0:NN, 0:NN])
            mm.then_inc(slot_full, 1)

            def turn(base, par, plan, kind, what, nt, tok, cs=range(3)):
                for c in cs:
                    u = plan[(kind, c, 0)]
                    fill(base, u)
                    for k in range(2):
                        for t in range(nt):
                            mm = pe.transpose(parity(par, u)[:, k * B + t * P:k * B + t * P + tok],
                                              what[0:tok, t, (2 * c + k) * P:(2 * c + k + 1) * P], ident[0:tok, 0:tok])
                    mm.then_inc(slot_full, 1)

            def project_heads(base, par, plan, kind, wgt, m, w, need=0):
                u = plan[(kind, m, 0)]
                fill(base, u)
                for i, (s, r) in enumerate(PAIRS):
                    if i == 1 and need:
                        pe.wait_ge(slot_v, base[2] + need)
                    for k in range(DC):
                        mm = pe.matmul(parity(par, u)[:, 0:w], wgt[:, r, k, m * P:(m + 1) * P], xT[:, s, k, 0:w],
                                       start=(i == 0 and k == 0), stop=(i == 2 and k == DC - 1))
                mm.then_inc(slot_full, 1)
                return mm

            def add_kv(n, half, nt, tok):
                pe.wait_ge(kv_added, 2 * n + half)
                if half == 0:
                    pe.wait_ge(v_lo, 2 * n + nt)
                kvq = (zps, acc[0])[half]
                for i in range(12):
                    h, c = 6 * half + i // 2, i % 2
                    o = kvq[:, (i // 6) * BANK + (i % 6) * DV:(i // 6) * BANK + (i % 6 + 1) * DV]
                    for t in range(nt):
                        for q, (s, r) in enumerate(PAIRS):
                            mm = pe.matmul(o, kfeat[0:tok, s, t, h * M + c * P:h * M + (c + 1) * P],
                                           vp[0:tok, r, t, h * DV:(h + 1) * DV],
                                           start=(t == 0 and q == 0), stop=(t == nt - 1 and q == 2))
                mm.then_inc(kv_full, 1)

            def histogram(base, par, plan, n):
                u = plan[("H", 0, 0)]
                pe.wait_ge(hots_built, n + 1)
                fill(base, u)
                for i in range(HC):
                    mm = pe.matmul(parity(par, u)[:, 0:NTP], onesb[:, i, :], onesa[:, i, :], start=(i == 0), stop=(i == HC - 1))
                mm.then_inc(slot_full, 1)

            def v_step(n, t, tok, i, kv_n):
                s, r = PAIRS[i // DC]
                k = i % DC
                if i == 0 and t == 0:
                    pe.wait_ge(kv_added, kv_n)
                if i == 0 and t == 1:
                    wait_for(pe, v_lo, n - 1)
                for c0, c1 in ((0, BANK), (BANK, D)):
                    mm = pe.matmul(acc[t][0:tok, c0:c1], xT[:, s, k, t * P:t * P + tok], wv[:, r, k, c0:c1],
                                   start=(i == 0), stop=(i == 17))
                if i == 17:
                    mm.then_inc(v_full, 1)

            def pe1(b, plan, nt, tok, base, par, first=False):
                w = B if nt == 2 else tok
                pe.wait_ge(normed, 2 * b + nt)
                turn(base, par, plan, "T", xb, nt, tok, (0, 1))
                if not first:
                    add_kv(b - 1, 0, 2, P)
                turn(base, par, plan, "T", xb, nt, tok, (2,))
                if not first:
                    add_kv(b - 1, 1, 2, P)
                pe.wait_ge(slot_a, base[1] + 3)
                for m in range(DC):
                    project_heads(base, par, plan, "K", wk, m, w, need=3 if m == 0 else 0)
                for t in range(nt):
                    for p in range(H // 2):
                        u = plan[("F", t, p)]
                        fill(base, u, need=plan[("K", p, 0)][2] + 1)
                        for e in range(2):
                            for r in range(2):
                                mm = pe.matmul(parity(par, u)[0:tok, e * M:(e + 1) * M], hd[:, 2 * p + e, t * P:t * P + tok],
                                               pmT[:, r, :], start=(r == 0), stop=(r == 1))
                        mm.then_inc(slot_full, 1)
                        for i in range(3 * p, 3 * p + 3):
                            v_step(2 * b + t, t, tok, i, 2 * b + 1)
                        if t == 0 and p == 3:
                            histogram(base, par, plan, b)
            pe.wait_ge(slot_v, prep_n[2])
            pe1(0, p1_first, 2, P, bases1(0), par1, first=True)
            with pe.Fori(1, NB) as b:
                pe1(b, p1, 2, P, bases1(b), par1)
            pe1(NB, p1_tail, 1, TAIL, tail1, par1_tail)
            add_kv(NB, 0, 1, TAIL)
            add_kv(NB, 1, 1, TAIL)

            half = H // 2 * DV
            pe.wait_ge(v_summed, 2 * NT)
            pe.wait_ge(kv_added, 2 * NB + 3)
            for i in range(2):
                mm = pe.matmul(acc[0][:, i * BANK:i * BANK + half], epsk[:], vacc[:, i * half:(i + 1) * half], start=True, stop=True)
            mm.then_inc(mid_full, 1)
            pe.wait_ge(deg_done, 1)
            pe.matmul(acc[1][:, 0:NTP], ones[:], degs[:], start=True, stop=True)
            pe.matmul(acc[1][0:G, NTP:2 * NTP], below[:], degs[:], start=True, stop=True).then_inc(mid_full, 1)
            pe.wait_ge(mid_v, 1)
            pe.matmul(acc[1][:, BANK:BANK + H], ones[:], kf[:, 0:H], start=True, stop=True).then_inc(mid_full, 1)
            pe.wait_ge(mid_v, 2)
            kvv = kvs[:].rearrange("p (h c) d -> p h c d", c=2)
            for i in range(2):
                for c in range(2):
                    mm = pe.matmul(acc[0][:, i * BANK:i * BANK + half].rearrange("p (h d) -> p h d", d=DV), epsk[:],
                                   kvv[:, 6 * i:6 * i + 6, c, :], start=(c == 0), stop=(c == 1))
            mm.then_inc(mid_full, 1)
            pe.wait_ge(bad_in, 1)
            pe.matmul(acc[1][:, 2 * NTP:3 * NTP], same, degs[:], start=True, stop=True).then_inc(bad_full, 1)
            pe.wait_ge(bad_in, 2)
            pe.matmul(acc[1][:, 3 * NTP:3 * NTP + 1], ones[:], bad[:, 3:4], start=True, stop=True).then_inc(bad_full, 1)
            pe.wait_ge(kv_ready, 1)

            def general_sums():
                places = [(acc[0], 0), (acc[1], 1), (zps, 2)]

                def edge(first):
                    for o, _ in places:
                        for c0, c1 in ((0, BANK), (BANK, D)):
                            mm = pe.matmul(o[:, c0:c1], zero16[:, 0:P], zero16[:, 0:c1 - c0], start=first, stop=not first)
                    return mm
                pe.wait_ge(all_zero, 1)
                pe.sem_inc(all_used, 1)
                with pe.Fori(0, NPASS) as n:
                    pe.wait_ge(all_read, n + 1)
                    edge(True)
                    with pe.Fori(0, NS) as i:
                        pe.wait_ge(all_hots, n * NS + i + 1)
                        for k in range(WIN):
                            pe.wait_ge(all_got[k], 16 * (n * NS + i) + 16)
                        for k in range(WIN):
                            for o, j in places:
                                for h in range(2):
                                    for c0, c1 in ((0, BANK), (BANK, D)):
                                        mm = pe.matmul(o[:, c0:c1], all_hot[:, j, k, :], ring[:, k, h * D + c0:h * D + c1],
                                                       start=False, stop=False)
                        mm.then_inc(all_used, 1)
                    edge(False).then_inc(all_sum, 1)
                pe.wait_ge(all_done, 2)
            pe.wait_ge(flag_ready, 1)
            with pe.If(pe.value_load(flag[0:1, 0:1], min_val=0, max_val=1) > 0):
                general_sums()

            def aggregate(b, u):
                j = u // WIN
                if u % WIN == 0:
                    wait_for(pe, z_read, 2 * b + j)
                pe.wait_ge(hot_ready, 2 * WIN * b + u + 1)
                for g in range(G):
                    k = G * u + g
                    pe.wait_ge(got[k % RING], 16 * ((2 * G * WIN // RING) * b + k // RING + 1))
                for s in range(2):
                    for c0, c1 in ((0, BANK), (BANK, D)):
                        for g in range(G):
                            mm = pe.matmul(zps[g * GN:(g + 1) * GN, c0:c1], hot[:, u % SRING, g, :],
                                           ring[:, (G * u + g) % RING, s * D + c0:s * D + c1],
                                           start=(u % WIN == 0 and s == 0), stop=False)
                mm.then_inc(unit_used, 1)

            def own_rows(b, j, tok):
                pe.wait_ge(own_s[j], 16 * (b + 1))
                for s in range(2):
                    for c0, c1 in ((0, BANK), (BANK, D)):
                        mm = pe.matmul(zps[:, c0:c1], ident16[0:tok, :], own[0:tok, j, s * D + c0:s * D + c1],
                                       start=False, stop=(s == 1))
                mm.then_inc(z_full, 1)

            def logits(base, par, plan, t, tok):
                u = plan[("L", t, 0)]
                fill(base, u, need=plan[("X", 2, 0)][2] + 1)
                for i, (s, r) in enumerate(PAIRS):
                    for k in range(DC):
                        mm = pe.matmul(parity(par, u)[0:tok, 0:NN], x1T[:, s, k, t * P:t * P + tok], winT[:, r, k, :],
                                       start=(i == 0 and k == 0), stop=(i == 2 and k == DC - 1))
                mm.then_inc(slot_full, 1)

            def turn_coefficients(base, par, plan, nt, tok, n_coef):
                u = plan[("C", 0, 0)]
                pe.wait_ge(coef, n_coef)
                fill(base, u)
                for t in range(nt):
                    mm = pe.transpose(parity(par, u)[0:96, :].bitcast(F16)[:, t * P:t * P + tok], co[0:tok, t, :], ident16[0:tok, 0:tok])
                mm.then_inc(slot_full, 1)

            def tree_rows(base, par, plan, t, tok, halves=(0, 1)):
                pe.wait_ge(slot_a, base[1] + plan[("C", 0, 0)][1] + 1)
                for i in halves:
                    c0, c1 = ((0, BANK), (BANK, D))[i]
                    u = plan[("Y", t, i)]
                    fill(base, u)
                    pe.matmul(parity(par, u)[0:tok, 0:c1 - c0], coT[:, t * P:t * P + tok], wo[:, c0:c1],
                              start=True, stop=True).then_inc(slot_full, 1)

            def attend(b, plan, h, nt, tok, w):
                for t in range(nt):
                    o = acc[t][0:tok, (h // 6) * BANK + (h % 6) * DV:(h // 6) * BANK + (h % 6 + 1) * DV]
                    for c in range(2):
                        for i, (s, r) in enumerate(PAIRS):
                            mm = pe.matmul(o, qfeat[:, h % 4, s, c, t * P:t * P + tok], kvp[:, r, 2 * h + c, :],
                                           start=(c == 0 and i == 0), stop=(c == 1 and i == 2))
                    if h == H - 1:
                        mm.then_inc(acc_full, 1)

            def pe3(b, plan, nt, tok, prev):
                base, w = bases3(b), (B if nt == 2 else tok)
                par = par3_first if prev is None else par3
                own_rows(b, 0, tok)
                pe.wait_ge(xt_in, 16 * (b + 1))
                units = iter(range(WIN, 2 * WIN) if nt == 2 else ())

                def unit():
                    u_ = next(units, None)
                    if u_ is not None:
                        aggregate(b, u_)

                def features(h):
                    uf = plan[("F", h, 0)]
                    fill(base, uf, need=plan[("Q", h // 2, 0)][2] + 1)
                    for c in range(2):
                        for r in range(2):
                            mm = pe.matmul(parity(par, uf)[:, c * B:c * B + w], pmT[:, r, c * P:(c + 1) * P], hd[:, h, 0:w],
                                           start=(r == 0), stop=(r == 1))
                    mm.then_inc(slot_full, 1)

                def attend_to(h):
                    pe.wait_ge(slot_v, base[2] + plan[("F", h, 0)][2] + 1)
                    attend(b, plan, h, nt, tok, w)
                def project(m):
                    project_heads(base, par, plan, "Q", wq, m, w)

                def turn_x1(c):
                    if prev:
                        turn(base, par, plan, "X", xb, 2, P, (c,))
                project(0)
                project(1)
                features(0)
                unit()
                features(1)
                project(2)
                features(2)
                if prev:
                    pe.wait_ge(acc_read, 4 * b)
                attend_to(0)
                attend_to(1)
                unit()
                features(3)
                project(3)
                if prev:
                    pe.wait_ge(x1_normed, 2 * b)
                turn_x1(0)
                attend_to(2)
                attend_to(3)
                turn_x1(1)
                turn_x1(2)
                features(4)
                unit()
                features(5)
                project(4)
                if prev:
                    logits(base, par, plan, 0, P)
                attend_to(4)
                attend_to(5)
                if prev:
                    logits(base, par, plan, 1, P)
                features(6)
                features(7)
                unit()
                project(5)
                pe.wait_ge(slot_full, base[0] + plan[("Q", 5, 0)][0] + 1)
                pe.sem_inc(q_done, 1)
                features(8)
                attend_to(6)
                attend_to(7)
                unit()
                features(9)
                if nt == 2:
                    own_rows(b, 1, P)
                features(10)
                attend_to(8)
                features(11)
                attend_to(9)
                pe.wait_ge(z_read, 2 * b + nt)
                turn(base, par, plan, "Z", zz, nt, tok, (0,))
                attend_to(10)
                turn(base, par, plan, "Z", zz, nt, tok, (1,))
                attend_to(11)
                turn(base, par, plan, "Z", zz, nt, tok, (2,))
                nxt = iter(range(WIN) if nt == 2 else ())

                def unit_ahead():
                    u_ = next(nxt, None)
                    if u_ is not None:
                        aggregate(b + 1, u_)
                if prev:
                    turn_coefficients(base, par, plan, 2, P, b)
                unit_ahead()
                pe.wait_ge(slot_a, base[1] + plan[("Z", 2, 0)][1] + 1)
                pe.wait_ge(acc_read, 4 * b + 1)
                for i in range(3):
                    if i == 1:
                        pe.wait_ge(slot_v, base[2] + plan[("Z", 2, 0)][2] + 1)
                    convolve(0, tok, i)
                unit_ahead()
                if nt == 2:
                    pe.wait_ge(acc_read, 4 * b + 2)
                for i in range(3):
                    if i == 0:
                        pe.wait_ge(o_ready, 2 * b + nt)
                    turn(base, par, plan, "O", oo, nt, tok, (i,))
                    if nt == 2:
                        convolve(1, tok, i)
                unit_ahead()
                pe.wait_ge(slot_v, base[2] + plan[("O", 2, 0)][2] + 1)
                for t in range(nt):
                    for i in range(3):
                        mm = attention_out(t, tok, i)
                        if i == 2:
                            mm.then_inc(acc_full, 1)
                        if prev and t == 0:
                            tree_rows(base, par, plan, i // 2, P, (i % 2,))
                        if (t, i) == (1, 1):
                            unit_ahead()
                    if t == 0:
                        if prev:
                            tree_rows(base, par, plan, 1, P, (1,))
                        unit_ahead()

            def attention_out(t, tok, i):
                s, r = PAIRS[i]
                for k in range(DC):
                    for c0, c1 in ((0, BANK), (BANK, D)):
                        mm = pe.matmul(acc[t][0:tok, c0:c1], oT[:, s, k, t * P:t * P + tok], wp[:, r, k, c0:c1],
                                       start=False, stop=(i == 2 and k == DC - 1))
                return mm

            def convolve(t, tok, i):
                s, r = PAIRS[i]
                for k in range(DC):
                    for c0, c1 in ((0, BANK), (BANK, D)):
                        pe.matmul(acc[t][0:tok, c0:c1], zT[:, s, k, t * P:t * P + tok], wg[:, r, k, c0:c1],
                                  start=(i == 0 and k == 0), stop=False)
            for u in range(WIN):
                aggregate(0, u)
            pe3(0, p3_first, 2, P, None)
            with pe.Fori(1, NB) as b:
                pe3(b, p3, 2, P, True)
            pe3(NB, p3, 1, TAIL, True)
            pe.wait_ge(x1_normed, 2 * NB + 1)
            turn(end3, par3_end, p3_end, "X", xb, 1, TAIL)
            logits(end3, par3_end, p3_end, 0, TAIL)
            turn_coefficients(end3, par3_end, p3_end, 1, TAIL, NB + 1)
            tree_rows(end3, par3_end, p3_end, 0, TAIL)

        @block.vector
        def _(dve):
            v = nc.vector
            v.memset(wout3, 0.0).then_inc(vconsts, 1)
            v.memset(kvs[:], 0.0).then_inc(kv_added, 1)
            v.memset(degs[:], 0.0)
            v.memset(co[:], 0.0)
            v.memset(cf[:], 0.0)
            v.memset(vp[:, 1, :, :], 0.0)
            v.memset(vp[:, 0, :, :], 1.0).then_inc(vconsts, 1)
            dve.wait_ge(vconsts, 2)
            n_links = [0]

            class Chain:
                base, n = 0, 0

            def link(ins):
                Chain.n += 1
                ins.then_inc(vch, 1)
                dve.wait_ge(vch, Chain.base + Chain.n)
            del n_links

            def low(base, u, ops):
                dve.wait_ge(slot_a, base[1] + u[1] + 1)
                for f in ops:
                    last = f()
                last.then_inc(slot_v, 1)

            def stt(o, i0, sc, i1, op0, op1):
                return v.scalar_tensor_tensor(out=o, in0=i0, scalar=sc, in1=i1, op0=op0, op1=op1)

            dve.wait_ge(edges_in, 32)
            def split_edges():
                tmp = ed[:, 0:EC]
                link(v.tensor_scalar(tmp, dcol, P - 1, None, ALU.bitwise_and))
                v.tensor_copy(lo7[:], tmp)
                tmp2 = ed[:, EC:2 * EC]
                link(v.tensor_scalar(tmp2, dcol, 7, None, ALU.arith_shift_right))
                link(v.tensor_copy(hi7[:], tmp2))
                down = tmp.bitcast(F32)
                link(v.tensor_tensor(down, dcol, dnext, ALU.is_gt))
                link(v.tensor_reduce(bad[:, 0:1], down, mybir.AxisListType.X, ALU.max))
            split_edges()
            dve.wait_ge(small_in, 16 * 9)
            v.tensor_scalar(bqk[:], bqk_r[:], WS, None, ALU.mult)
            v.tensor_copy(wo[:], wout3)
            link(v.tensor_tensor(gpb[:], gpb[:], pbr, ALU.add))
            link(v.tensor_tensor(wo[64:96, :], wout3[64:96, :], wo[64:96, :], ALU.subtract))
            v.memset(den[:], 0.0).then_inc(small_v, 1)

            def layernorm(n, t, tok, s_in, s_rstd, src_, dst_, s_stats, s_norm):
                for c in range(2):
                    v.bn_stats(st[0:tok, t, c, :], src_[0:tok, t, c * D // 2:(c + 1) * D // 2]).then_inc(vch, 1)
                Chain.n += 2
                wait_apart(dve, vch, Chain.base + Chain.n, stats_passed)
                v.bn_aggr(mv[0:tok, t, :], st[0:tok, t, :, :]).then_inc(s_stats, 1)

            def normalise(n, t, tok, s_rstd, s_stats, src_, dst_, s_norm):
                dve.wait_ge(s_rstd, 2 * n + 2)
                v.tensor_scalar(dst_[0:tok, t, :], src_[0:tok, t, :], mv[0:tok, t, 0:1], rs[0:tok, t:t + 1],
                                ALU.subtract, ALU.mult).then_inc(s_norm, 1)

            dve.wait_ge(x_in, 16)
            for t in range(2):
                layernorm(t, t, P, x_in, rstd, xa, xb, stats, normed)
            for t in range(2):
                normalise(t, t, P, rstd, stats, xa, xb, normed)
            for i in range(NPREP):
                w, c0 = (wk, wv, wq, wp)[i // 3], (i % 3) * B
                for c in range(3):
                    u = prep[("W", i, c)]
                    low((0, 0, 0), u, [lambda w=w, c0=c0, c=c, u=u: stt(
                        w[:, 1, 2 * c:2 * c + 2, c0:c0 + B], slot[u[0] % 2][:].rearrange("p (k n) -> p k n", k=2), WS,
                        w[:, 0, 2 * c:2 * c + 2, c0:c0 + B], ALU.mult, ALU.subtract)])
            u = prep[("W", "pm", 0)]
            low((0, 0, 0), u, [lambda: stt(pmT[:, 1, :], slot[u[0] % 2][:, 0:M], 1.0, pmT[:, 0, :], ALU.mult, ALU.subtract)])
            u2 = prep[("W", "win", 0)]
            low((0, 0, 0), u2, [lambda: stt(winT[:, 1, :, :], slot[u2[0] % 2][:, 0:DC * 32].rearrange("p (k n) -> p k n", k=DC)[:, :, 0:NN],
                                            1.0, winT[:, 0, :, :], ALU.mult, ALU.subtract)])
            for i in range(DC // 2):
                n = NPREP + i
                dve.wait_ge(wg_hi, i + 1)
                stt(wg[:, 1, 2 * i:2 * i + 2, :], wst[n % 2][:, :, :], WS, wg[:, 0, 2 * i:2 * i + 2, :], ALU.mult, ALU.subtract).then_inc(wg_lo, 1)
            dve.wait_ge(consts, 5)
            CH0 = Chain.n

            def turned_lo(base, par, plan, kind, dst_, w, cs=range(3)):
                for c in cs:
                    u = plan[(kind, c, 0)]
                    low(base, u, [lambda c=c, u=u: stt(dst_[:, 1, 2 * c:2 * c + 2, 0:w],
                                                       parity(par, u)[:].rearrange("p (k n) -> p k n", k=2)[:, :, 0:w], 1.0,
                                                       dst_[:, 0, 2 * c:2 * c + 2, 0:w], ALU.mult, ALU.subtract)])

            def heads_lo(base, par, plan, kind, m, col, w):
                u = plan[(kind, m, 0)]
                s = parity(par, u)
                low(base, u, [lambda e=e: stt(hd[64 - 64 * e:128 - 64 * e, 2 * m + e, 0:w], s[64 * e:64 * e + 64, 0:w],
                                              bqk[64 * e:64 * e + 64, col + m:col + m + 1],
                                              hd[64 * e:64 * e + 64, 2 * m + e, 0:w], ALU.add, ALU.subtract) for e in range(2)])

            def flush_kv(n, half):
                dve.wait_ge(kv_full, 2 * n + half + 1)
                dst_ = kvs[:, 12 * half:12 * half + 12, :].rearrange("p (a i) d -> p a i d", a=2)
                src_ = (zps, acc[0])[half][:].rearrange("p (a n) -> p a n", a=2)[:, :, 0:6 * DV].rearrange("p a (i d) -> p a i d", d=DV)
                v.tensor_tensor(dst_, src_, dst_, ALU.add).then_inc(kv_added, 1)

            PIECES = 8

            def build_hots(b, i):
                c0, c1 = HC * i // PIECES, HC * (i + 1) // PIECES
                n = c1 - c0
                v.tensor_tensor(onesb[:, c0:c1, :], iota16[:].unsqueeze(1).broadcast_to([P, n, P]),
                                lo7[:, bass.ds(b * HC + c0, n)].unsqueeze(2).broadcast_to([P, n, P]), ALU.is_equal)
                last = v.tensor_tensor(onesa[:, c0:c1, :], iota16[:, 0:NTP].unsqueeze(1).broadcast_to([P, n, NTP]),
                                       hi7[:, bass.ds(b * HC + c0, n)].unsqueeze(2).broadcast_to([P, n, NTP]), ALU.is_equal)
                if i == PIECES - 1:
                    last.then_inc(hots_built, 1)

            def add_degrees(base, par, plan, b):
                u = plan[("H", 0, 0)]
                dve.wait_ge(slot_full, base[0] + u[0] + 1)
                v.tensor_tensor(degs[:], parity(par, u)[:, 0:NTP], degs[:], ALU.add).then_inc(slot_v, 1)

            def dve1(b, plan, nt, tok, base, par, first=False, nt_next=2, tok_next=P):
                w = B if nt == 2 else tok
                if first:
                    turned_lo(base, par, plan, "T", xT, w)
                else:
                    turned_lo(base, par, plan, "T", xT, w, (0, 1))
                    flush_kv(b - 1, 0)
                    turned_lo(base, par, plan, "T", xT, w, (2,))
                    flush_kv(b - 1, 1)
                for m in range(DC):
                    heads_lo(base, par, plan, "K", m, DC, w)
                    build_hots(b, m)
                for t in range(nt):
                    for p in range(H // 2):
                        u = plan[("F", t, p)]
                        low(base, u, [lambda t=t, p=p, u=u: stt(kfeat[0:tok, 1, t, 2 * p * M:(2 * p + 2) * M], parity(par, u)[0:tok, :], 0.0,
                                                                kfeat[0:tok, 0, t, 2 * p * M:(2 * p + 2) * M], ALU.max, ALU.subtract)])
                        if t == 0 and p < 2:
                            build_hots(b, DC + p)
                        if t == 0 and p == 3:
                            add_degrees(base, par, plan, b)
                        if nt_next and t == 0 and p in (2, 4):
                            tt = p // 2 - 1
                            if tt == 0:
                                dve.wait_ge(x_in, 16 * (b + 2))
                            if tt < nt_next:
                                layernorm(0, tt, tok_next, x_in, rstd, xa, xb, stats, normed)
                        if nt_next and t == 1 and p == 0:
                            dve.wait_ge(xn_out, 16 * (b + 1))
                        if nt_next and t == 1 and p in (0, 2) and p // 2 < nt_next:
                            normalise(2 * b + 2 + p // 2, p // 2, tok_next, rstd, stats, xa, xb, normed)
                    dve.wait_ge(v_hi, 2 * b + t + 1)
                    v.tensor_tensor(vp[0:tok, 1, t, :].rearrange("p (h d) -> p h d", h=H)[:, :, 0:DH],
                                    acc[t][0:tok, 0:D].rearrange("p (h d) -> p h d", h=H),
                                    vp[0:tok, 0, t, :].rearrange("p (h d) -> p h d", h=H)[:, :, 0:DH], ALU.subtract).then_inc(v_lo, 1)

            dve1(0, p1_first, 2, P, bases1(0), par1, first=True)
            per = Chain.n - CH0
            with dve.Fori(1, NB - 1) as b:
                Chain.base, Chain.n = CH0 + b * per, 0
                dve1(b, p1, 2, P, bases1(b), par1)
            Chain.base, Chain.n = 0, CH0 + (NB - 1) * per
            dve1(NB - 1, p1, 2, P, bases1(NB - 1), par1, nt_next=1, tok_next=TAIL)
            dve1(NB, p1_tail, 1, TAIL, tail1, par1_tail, nt_next=0)
            flush_kv(NB, 0)
            flush_kv(NB, 1)

            v.memset(same, 0.0).then_inc(vch, 1)
            Chain.n += 1
            dve.wait_ge(vch, Chain.base + Chain.n)
            for i in range(G):
                last = v.memset(zz[i * GN:(i + 1) * GN, 0, i * GN:(i + 1) * GN], 1.0)
            last.then_inc(bad_in, 1)
            dve.wait_ge(slot_v, base3[2])
            dve.wait_ge(kv_added, 2 * NB + 3)
            v.tensor_copy(scanA[:], degs[:]).then_inc(deg_done, 1)
            kvv = kvs[:].rearrange("p (h c) d -> p h c d", c=2)
            dve.wait_ge(mid_full, 1)
            vs = acc[0][:].rearrange("p (a n) -> p a n", a=2)[:, :, 0:6 * DV].rearrange("p a (h d) -> p a h d", d=DV)
            for c in range(2):
                for i in range(2):
                    last = v.tensor_tensor(kvv[:, 6 * i:6 * i + 6, c, :], vs[:, i, :, :], kvv[:, 6 * i:6 * i + 6, c, :], ALU.add)
                    if (c, i) != (1, 1):
                        link(last)
            link(last)
            v.tensor_tensor(kf[:, 0:H], kvv[:, :, 0, DH], kvv[:, :, 1, DH], ALU.add).then_inc(mid_v, 1)
            dve.wait_ge(mid_full, 2)
            link(v.tensor_copy(cnt[:], acc[1][:, 0:NTP]))
            link(v.tensor_copy(scanA[:], cnt[:]))
            a_, b_ = scanA, scanC
            s = 1
            while s < NTP:
                v.tensor_copy(b_[:, 0:s], a_[:, 0:s]).then_inc(vch, 1)
                Chain.n += 1
                link(v.tensor_tensor(b_[:, s:NTP], a_[:, s:NTP], a_[:, 0:NTP - s], ALU.add))
                a_, b_ = b_, a_
                s *= 2
            link(v.tensor_tensor(e0f[:], a_[:], cnt[:], ALU.subtract))
            link(v.tensor_tensor(e0f[0:G, :], e0f[0:G, :], acc[1][0:G, NTP:2 * NTP], ALU.add))
            link(v.tensor_copy(e0[:], e0f[:]))
            dve.wait_ge(dinv_done, 1)
            v.tensor_scalar(dinvT[:], dinv[:], TS, None, ALU.mult)
            link(v.tensor_scalar(dinvZ[:], dinv[:], WS / TS, None, ALU.mult))
            v.memset(den[:], 0.0).then_inc(dinv_done, 1)
            v.memset(rec[:], 0.0).then_inc(ranges_done, 1)
            dve.wait_ge(mid_full, 3)
            link(v.reciprocal(kf[:, 0:H], acc[1][:, BANK:BANK + H]))
            link(v.tensor_scalar(kf[:, H:2 * H], kf[:, 0:H], 1024.0, None, ALU.mult))
            kvf = kvs[:].rearrange("p (h c) d -> p h (c d)", c=2)
            link(v.tensor_tensor(kvf, kvf, kf[:, H:2 * H].unsqueeze(2).broadcast_to([P, H, 2 * DV]), ALU.mult))
            link(v.tensor_copy(kvp[:, 0, :, :], kvs[:]))
            link(v.tensor_tensor(kvp[:, 1, :, :], kvs[:], kvp[:, 0, :, :], ALU.subtract))
            v.memset(sg[:], 0.0).then_inc(mid_v, 1)
            dve.wait_ge(mid_full, 4)
            link(v.tensor_copy(cn.rearrange("p (a h) d -> p a h d", a=2), vs))
            v.memset(ns[:], 0.0).then_inc(kv_ready, 1)
            dve.wait_ge(bad_full, 1)
            link(v.tensor_reduce(bad[:, 1:2], acc[1][:, 2 * NTP:3 * NTP], mybir.AxisListType.X, ALU.max))
            link(v.tensor_scalar(bad[:, 2:3], bad[:, 1:2], float(WIN * P), None, ALU.is_gt))
            v.tensor_tensor(bad[:, 3:4], bad[:, 0:1], bad[:, 2:3], ALU.add).then_inc(bad_in, 1)
            dve.wait_ge(bad_full, 2)
            v.tensor_scalar(flag[:], acc[1][0:1, 3 * NTP:3 * NTP + 1], 0.5, None, ALU.is_gt).then_inc(flag_ready, 1)

            def table_lo(t, i, tok):
                dve.wait_ge(t_hi, t + 1)
                stt(tout[i][0:tok, D:2 * D], tin[i][0:tok, :], dinvT[0:tok, bass.ds(t, 1)], tout[i][0:tok, 0:D], ALU.mult, ALU.subtract).then_inc(t_lo, 1)
            with dve.Fori(0, NT // 4) as g:
                for i in range(4):
                    table_lo(4 * g + i, i, P)
            for t in range(NT // 4 * 4, NT):
                table_lo(t, t % 4, P if t < NT - 1 else TAIL)

            def general_sums():
                v.memset(zero16, 0.0).then_inc(all_zero, 1)
                with dve.Fori(0, NPASS) as n:
                    with dve.Fori(0, NS) as i:
                        dve.wait_ge(all_in, 32 * (n * NS + i) + 32)
                        for j in range(3):
                            last = v.tensor_scalar(away[:, j, :], dstw[:, 0, 0, :], tile_base[:, bass.ds(3 * n + j, 1)], None, ALU.subtract)
                        last.then_inc(all_away, 1)
                        dve.wait_ge(all_away, n * NS + i + 1)
                        for j in range(3):
                            last = v.tensor_tensor(all_hot[:, j, :, :], iota16[:].unsqueeze(1).broadcast_to([P, WIN, P]),
                                                   away[:, j, :].unsqueeze(2).broadcast_to([P, WIN, P]), ALU.is_equal)
                        last.then_inc(all_hots, 1)

                def row(t, tok):
                    z, hi, lo = zz[0:tok, 0, :], own[0:tok, 1, 0:D], own[0:tok, 1, D:2 * D]

                    def step(ins, k):
                        ins.then_inc(row_chain, 1)
                        dve.wait_ge(row_chain, 4 * t + k)
                    dve.wait_ge(row_in, 32 * t + 32)
                    step(v.tensor_tensor(z, z, own[0:tok, 0, 0:D], ALU.add), 1)
                    step(v.tensor_tensor(z, z, own[0:tok, 0, D:2 * D], ALU.add), 2)
                    step(v.tensor_scalar(z, z, dinvZ[0:tok, bass.ds(t, 1)], None, ALU.mult), 3)
                    step(v.tensor_copy(hi, z), 4)
                    v.tensor_tensor(lo, z, hi, ALU.subtract).then_inc(row_ready, 1)
                with dve.Fori(0, NT - 1) as t:
                    row(t, P)
                row(NT - 1, TAIL)
                v.memset(dinvZ[:], 1.0)
                v.tensor_scalar(tile_base[:], tile_base[:], 4.0 * BIG, None, ALU.add).then_inc(all_done, 1)
                dve.wait_ge(all_done, 2)
            dve.wait_ge(flag_ready, 1)
            with dve.If(dve.value_load(flag[0:1, 0:1], min_val=0, max_val=1) > 0):
                general_sums()

            def localise(b, j):
                dve.wait_ge(win_s[j], 2 * G * 16 * (b + 1))
                link(v.tensor_scalar(dstl[:, j, :, :], dstw[:, j, :, :], tile_base[:, bass.ds(2 * b + j, 1)], None, ALU.subtract))

            def build_unit(b, u):
                wait_for(dve, unit_used, 2 * WIN * b + u - SRING + 1)
                v.tensor_tensor(hot[:, u % SRING, :, :], iota16[:].rearrange("p (g n) -> p g n", g=G),
                                dstl[:, u // WIN, :, u % WIN:u % WIN + 1].broadcast_to([P, G, GN]), ALU.is_equal).then_inc(hot_ready, 1)

            def tree(nt, tok):
                T = slice(0, nt)
                R, C, GL, S_, NS_ = (z[0:tok] for z in (rr, cf, gl, sg, ns))

                def written(ins):
                    Chain.n += 1
                    ins.then_inc(vch, 1)
                    n = Chain.base + Chain.n
                    return lambda: dve.wait_ge(vch, n)
                w_ = written(v.tensor_scalar(NS_[:, T, :], S_[:, T, :], -1.0, 1.0, ALU.mult, ALU.add))
                yield
                w_()
                v.tensor_copy(R[:, T, 1:2], NS_[:, T, 0:1])
                w_ = written(v.tensor_copy(R[:, T, 2:3], S_[:, T, 0:1]))
                yield
                for n0, n1 in ((1, 3), (3, 7), (7, 10)):
                    kids = R[:, T, 2 * n0 + 1:2 * n1 + 1].rearrange("p t (n e) -> p t n e", e=2)
                    w_()
                    v.tensor_tensor(kids[:, :, :, 0], R[:, T, n0:n1], NS_[:, T, n0:n1], ALU.mult)
                    w_ = written(v.tensor_tensor(kids[:, :, :, 1], R[:, T, n0:n1], S_[:, T, n0:n1], ALU.mult))
                    yield
                kids = C[:, T, 1:NN].rearrange("p t (n e) -> p t n e", e=2)
                rk = R[:, T, 1:NN].rearrange("p t (n e) -> p t n e", e=2)
                w_()
                for e in range(2):
                    v.tensor_tensor(kids[:, :, :, e], rk[:, :, :, e], GL[:, T, 0:10], ALU.mult)
                w_ = written(v.tensor_tensor(ux[0:tok, T, 10:20], R[:, T, 10:20], GL[:, T, 10:20], ALU.mult))
                yield
                w_()
                v.tensor_reduce(su[0:tok, T, 0:1], ux[0:tok, T, 10:20], mybir.AxisListType.X, ALU.add)
                w_ = written(v.tensor_reduce(su[0:tok, T, 1:2], R[:, T, 15:20], mybir.AxisListType.X, ALU.add))
                yield
                w_()
                w_ = written(v.tensor_scalar(su[0:tok, T, 2:3], su[0:tok, T, 1:2], -1.0, 6.0, ALU.mult, ALU.add))
                yield
                w_()
                w_ = written(v.tensor_tensor(su[0:tok, T, 3:4], su[0:tok, T, 2:3], GL[:, T, 20:21], ALU.mult))
                yield
                w_()
                w_ = written(v.tensor_tensor(su[0:tok, T, 0:1], su[0:tok, T, 0:1], su[0:tok, T, 3:4], ALU.add))
                yield
                w_()
                w_ = written(v.tensor_tensor(C[:, T, 20:21], C[:, T, 20:21], su[0:tok, T, 0:1], ALU.add))
                yield
                w_()
                v.tensor_copy(co[0:tok, T, 0:NN], C[:, T, :])
                w_ = written(v.tensor_copy(co[0:tok, T, 64:64 + NN], C[:, T, :]))
                yield
                w_()
                v.tensor_tensor(co[0:tok, T, 32:32 + NN], C[:, T, :], co[0:tok, T, 0:NN], ALU.subtract).then_inc(coef, 1)
                yield

            def signs(base, par, plan, nt, tok):
                for t in range(nt):
                    u = plan[("L", t, 0)]
                    dve.wait_ge(slot_a, base[1] + u[1] + 1)
                    v.tensor_scalar(sg[0:tok, t, :], parity(par, u)[0:tok, 0:NN], 0.0, None, ALU.is_gt).then_inc(slot_v, 1)
                dve.wait_ge(slot_v, base[2] + plan[("L", nt - 1, 0)][2] + 1)

            def add_tree_rows(base, par, plan, t, tok):
                for i, (c0, c1) in enumerate(((0, BANK), (BANK, D))):
                    u = plan[("Y", t, i)]
                    dve.wait_ge(slot_full, base[0] + u[0] + 1)
                    v.tensor_tensor(yo[0:tok, t, c0:c1], parity(par, u)[0:tok, 0:c1 - c0], x1[0:tok, t, c0:c1], ALU.add).then_inc(slot_v, 1)

            def dve3(b, plan, nt, tok, prev):
                base, w = bases3(b), (B if nt == 2 else tok)
                par = par3_first if prev is None else par3
                units = iter(range(WIN, 2 * WIN) if nt == 2 else ())

                def unit():
                    u_ = next(units, None)
                    if u_ is not None:
                        build_unit(b, u_)

                def features(h):
                    uf = plan[("F", h, 0)]
                    low(base, uf, [lambda: stt(qfeat[:, h % 4, 1, :, 0:w], parity(par, uf)[:].rearrange("p (c n) -> p c n", c=2)[:, :, 0:w],
                                               0.0, qfeat[:, h % 4, 0, :, 0:w], ALU.max, ALU.subtract)])
                def q_lo(m):
                    heads_lo(base, par, plan, "Q", m, 0, w)

                def x1_lo(c):
                    if prev:
                        turned_lo(base, par, plan, "X", x1T, B, (c,))

                def tree_step():
                    if prev:
                        next(steps)
                steps = tree(2, P) if prev else None
                if nt == 2:
                    localise(b, 1)
                unit()
                q_lo(0)
                q_lo(1)
                features(0)
                unit()
                if prev:
                    norm_x1(2 * b - 2, 0, P)
                features(1)
                if prev:
                    norm_x1(2 * b - 2, 1, P)
                q_lo(2)
                features(2)
                unit()
                features(3)
                q_lo(3)
                for c in range(3):
                    x1_lo(c)
                features(4)
                unit()
                features(5)
                q_lo(4)
                if prev:
                    signs(base, par, plan, 2, P)
                unit()
                tree_step()
                features(6)
                tree_step()
                tree_step()
                features(7)
                for _ in range(3):
                    tree_step()
                q_lo(5)
                tree_step()
                features(8)
                for _ in range(3):
                    tree_step()
                features(9)
                tree_step()
                tree_step()
                features(10)
                if nt == 2:
                    localise(b + 1, 0)
                features(11)
                if nt == 2:
                    build_unit(b + 1, 0)
                turned_lo(base, par, plan, "Z", zT, w, (0,))
                turned_lo(base, par, plan, "Z", zT, w, (1,))
                tree_step()
                na = 4 * b
                for t in range(nt):
                    dve.wait_ge(acc_full, na + t + 1)
                    view = acc[t][0:tok, :].rearrange("p (a n) -> p a n", a=2)[:, :, 0:6 * DV].rearrange("p a (h d) -> p a h d", d=DV)
                    cv = cn[0:tok].rearrange("p (a h) d -> p a h d", a=2)
                    ov = oo[0:tok, t, :].rearrange("p (a h d) -> p a h d", a=2, d=DH)
                    dv = den[0:tok, t, :].rearrange("p (a h) -> p a h", a=2)
                    v.tensor_tensor(ov, view[:, :, :, 0:DH], cv[:, :, :, 0:DH], ALU.add).then_inc(vch, 1)
                    Chain.n += 1
                    v.tensor_tensor(dv, view[:, :, :, DH], cv[:, :, :, DH], ALU.add).then_inc(acc_read, 1)
                    if t == 0:
                        turned_lo(base, par, plan, "Z", zT, w, (2,))
                if nt == 2:
                    build_unit(b + 1, 1)
                for t in range(nt):
                    dve.wait_ge(acc_read, na + t + 1)
                    link(v.reciprocal(rec[0:tok, t, :], den[0:tok, t, :]))
                    oh = oo[0:tok, t, :].rearrange("p (h d) -> p h d", h=H)
                    v.tensor_tensor(oh, oh, rec[0:tok, t, :].unsqueeze(2).broadcast_to([tok, H, DH]), ALU.mult).then_inc(o_ready, 1)
                if nt == 2:
                    build_unit(b + 1, 2)
                for c in range(3):
                    u_ = plan[("O", c, 0)]
                    s_ = parity(par, u_)
                    low(base, u_, [lambda e=e, c=c, s_=s_: stt(oT[:, 1, 2 * c + e, 0:w], s_[:, e * B:e * B + w],
                                                              bqk[:, 2 * DC + 2 * c + e:2 * DC + 2 * c + e + 1],
                                                              oT[:, 0, 2 * c + e, 0:w], ALU.add, ALU.subtract) for e in range(2)])
                if nt == 2:
                    build_unit(b + 1, 3)
                    build_unit(b + 1, 4)
                if prev:
                    dve.wait_ge(xr_in, 16 * (b + 1))
                    for t in range(2):
                        add_tree_rows(base, par, plan, t, P)
                no = na + nt
                for t in range(nt):
                    ac = acc[t]
                    dve.wait_ge(acc_full, no + t + 1)
                    dve.wait_ge(xr_biased, 2 * b + t + 1)
                    stt(x1[0:tok, t, :], ac[0:tok, 0:D], 1.0 / (WS * WS), xa[0:tok, t, :], ALU.mult, ALU.add).then_inc(acc_read, 1)
                    dve.wait_ge(acc_read, no + t + 1)
                    layernorm(0, t, tok, None, None, x1, None, x1_stats, None)

            def norm_x1(n, t, tok):
                normalise(n + t, t, tok, x1_rstd, x1_stats, x1, xb, x1_normed)
            localise(0, 0)
            for u in range(WIN):
                build_unit(0, u)
            dve3(0, p3_first, 2, P, None)
            C3b = Chain.n
            per3 = 2 + 12 + 2 * 2 + 2 * 2
            with dve.Fori(1, NB) as b:
                Chain.base, Chain.n = C3b + (b - 1) * per3, 0
                dve3(b, p3, 2, P, True)
                assert Chain.n == per3
            Chain.base, Chain.n = 0, C3b + (NB - 1) * per3
            dve3(NB, p3, 1, TAIL, True)
            norm_x1(2 * NB, 0, TAIL)
            turned_lo(end3, par3_end, p3_end, "X", x1T, TAIL)
            signs(end3, par3_end, p3_end, 1, TAIL)
            for _ in tree(1, TAIL):
                pass
            dve.wait_ge(stored, 16 * NB)
            add_tree_rows(end3, par3_end, p3_end, 0, TAIL)


_INS = ["x", "src", "dst", "L0_gnn_W", "L0_gnn_b", "L0_mix_qkv_w", "L0_mix_qkv_b", "L0_mix_proj_w", "L0_mix_proj_b",
        "L0_mix_proj_mat", "L0_ffn_weights_in", "L0_ffn_weights_out"]


def build(nc, arrays):
    args = [nc.dram_tensor(f"in_{n}", arrays[f"in_{n}"].shape, mybir.dt.from_np(arrays[f"in_{n}"].dtype), kind="ExternalInput").ap()
            for n in _INS]
    out = nc.dram_tensor("out_0", arrays["in_x"].shape, F32, kind="ExternalOutput").ap()
    gps_layer(nc, *args, out)


def kernel(**inputs):
    import numpy as np
    import concourse.bacc as bacc
    from concourse.bass_utils import run_bass_kernel_spmd

    nc = bacc.Bacc("TRN2", target_bir_lowering=False, num_devices=1)
    arrays = {f"in_{n}": np.ascontiguousarray(inputs[n]) for n in _INS}
    build(nc, arrays)
    return run_bass_kernel_spmd(nc, [arrays], core_ids=[0]).results[0]["out_0"]
```

```python
from contextlib import ExitStack

import concourse.bass as bass
from concourse import mybir

P = 128
ALU = mybir.AluOpType
ACT = mybir.ActivationFunctionType
F32 = mybir.dt.float32
F16 = mybir.dt.float16
I32 = mybir.dt.int32
U32 = mybir.dt.uint32

D = 768
DC = D // P
H = 12
DH = D // H
DV = DH + 1
M = 256
NN = 21
B = 2 * P
BANK = 512
WS = 8.0
ZS = 128.0
TS = 16.0
EPS_LN = 1e-5
EPS_FEAT = 1e-3
G = 4
GN = P // G
WIN = 5
RING = 10
SRING = 4
BIG = 1 << 20
PAIRS = ((0, 0), (1, 0), (0, 1))


def wait_for(eng, sem, value):
    if not (isinstance(value, int) and value <= 0):
        eng.wait_ge(sem, value)


def wait_apart(eng, sem, value, passed):
    if not (isinstance(value, int) and value <= 0):
        eng.wait_ge(sem, value)
        eng.sem_inc(passed, 1)


def slots(names, readers, before):
    out, n, a, v, last = {}, 0, 0, 0, before
    for u in names:
        r_last = readers[last] if last else "av"
        out[u] = (n, a, v, a - ("a" in r_last), v - ("v" in r_last))
        r = readers[u[0]]
        n, a, v, last = n + 1, a + ("a" in r), v + ("v" in r), u[0]
    return out, (n, a, v)


def gps_layer(nc, x, src, dst, gnn_w, gnn_b, qkv_w, qkv_b, proj_w, proj_b, proj_mat, w_in, w_out, out):
    N, E = x.shape[0], src.shape[0]
    NB, TAIL = N // B, N % B
    assert 0 < TAIL <= P and NB >= 3 and NB % 2 == 0
    NT = 2 * NB + 1
    NTP = NT + 1
    NH = 2 * NB // 3
    R = 2 * NB // (NB - NH)
    assert NH >= 2 and R * (NB - NH) == 2 * NB and R % 2 == 0 and NB - NH >= 2
    HC = -(-(E + WIN * P) // (P * NH))
    EC = HC * NH
    PIECES, FIRST = 16, 11
    ends = [HC * i // PIECES for i in range(PIECES + 1)]
    HR = max(ends[FIRST], HC - ends[FIRST])
    EP = EC * P
    NS = -(-E // (WIN * P))
    NPASS = -(-NT // 3)
    assert NS * WIN * P <= EP

    with ExitStack() as ctx:
        def sb(name, shape, dt):
            return ctx.enter_context(nc.sbuf_tensor(name, shape, dt))

        def sem(name):
            return ctx.enter_context(nc.semaphore(name))

        src_pad = nc.dram_tensor("src_pad", (EP,), I32).ap()
        dst_pad = nc.dram_tensor("dst_pad", (EP + P,), I32).ap()
        xn_dram = nc.dram_tensor("xn_dram", (N, D), F32).ap()
        xnt_dram = nc.dram_tensor("xnt_dram", ((NB + 1) * P, 2 * DC * B), F16).ap()
        table = nc.dram_tensor("table", (N, 2 * D), F16).ap()
        sums = nc.dram_tensor("sums", (NPASS * 3 * P, D), F32).ap()

        acc = [ctx.enter_context(nc.psum_tensor(f"acc{i}", [P, 2 * BANK], F32)) for i in range(2)]
        zps = ctx.enter_context(nc.psum_tensor("zps", [P, 2 * BANK], F32))
        slot = [ctx.enter_context(nc.psum_tensor(f"slot{i}", [P, BANK], F32)) for i in range(2)]

        ident = sb("ident", [P, P], F32)
        ident16 = sb("ident16", [P, P], F16)
        ones = sb("ones", [P, P], F32)
        epsk = sb("epsk", [P, P], F32)
        iota_i = sb("iota_i", [P, P], I32)
        iota16 = sb("iota16", [P, P], F16)
        padrow = sb("padrow", [P, 2 * P], I32)
        wq = sb("wq", [P, 2, DC, D], F16)
        wp = sb("wp", [P, 2, DC, D], F16)
        wg = sb("wg", [P, 2, DC, D], F16)
        region = sb("region", [P, 2 * 2 * DC * D], F16)
        wk = region[:, 0:2 * DC * D].rearrange("p (s k n) -> p s k n", s=2, k=DC)
        wv = region[:, 2 * DC * D:4 * DC * D].rearrange("p (s k n) -> p s k n", s=2, k=DC)
        pmT = sb("pmT", [P, 2, M], F16)
        winT = sb("winT", [P, 2, DC, NN], F16)
        wo = sb("wo", [96, D], F16)
        bqk_r = sb("bqk_r", [P, 3 * DC], F32)
        bqk = sb("bqk", [P, 3 * DC], F32)
        gpb = sb("gpb", [P, D], F32)
        lo7 = sb("lo7", [P, EC], F16)
        hi7 = sb("hi7", [P, EC], F16)
        degs = sb("degs", [P, NTP], F32)
        dinvT = sb("dinvT", [P, NTP], F32)
        dinvZ = sb("dinvZ", [P, NTP], F32)
        dinv = sb("dinv", [P, NTP], F32)
        scanA = sb("scanA", [P, NTP], F32)
        scanB = sb("scanB", [P, NTP], F32)
        scanC = sb("scanC", [P, NTP], F32)
        mhalf = sb("mhalf", [P, NTP], F32)
        var_eps = sb("var_eps", [P, 2], F32)
        eps_ln = sb("eps_ln", [P, 1], F32)
        cnt = sb("cnt", [P, NTP], F32)
        e0f = sb("e0f", [P, NTP], F32)
        e0 = sb("e0", [P, NTP], I32)
        below = sb("below", [P, G], F32)
        tile_base = sb("tile_base", [P, NTP + 2], F32)
        tile_i = sb("tile_i", [P, NTP + 2], I32)
        bad = sb("bad", [P, 4], F32)
        flag = sb("flag", [1, 1], I32)
        kvs = sb("kvs", [P, 24, DV], F32)
        kvp = sb("kvp", [P, 2, 24, DV], F16)
        vacc = sb("vacc", [P, H * DV], F32)
        cn = vacc[:].rearrange("p (h d) -> p h d", h=H)
        kf = sb("kf", [P, 2 * H], F32)
        xa = sb("xa", [P, 2, D], F32)
        xb = sb("xb", [P, 2, D], F32)
        st = sb("st", [P, 2, 2, 6], F32)
        mv = sb("mv", [P, 2, 2], F32)
        rs = sb("rs", [P, 2], F32)
        xT = sb("xT", [P, 2, DC, B], F16)
        hd = sb("hd", [P, H, B], F16)
        vp = sb("vp", [P, 2, 2, H * DV], F16)
        big = sb("big", [P, 2 * 2 * H * M], F16)
        kfeat = big[:].rearrange("p (s t n) -> p s t n", s=2, t=2)
        oT = big[:, 0:2 * DC * B].rearrange("p (s k n) -> p s k n", s=2, k=DC)
        zT = big[:, 2 * DC * B:4 * DC * B].rearrange("p (s k n) -> p s k n", s=2, k=DC)
        x1T = big[:, 4 * DC * B:6 * DC * B].rearrange("p (s k n) -> p s k n", s=2, k=DC)
        yo = big[:, 6 * DC * B:6 * DC * B + 4 * D].bitcast(F32).rearrange("p (t n) -> p t n", t=2)
        ed = big[:, 0:4 * EC].bitcast(I32)
        winr = big[0:32, 6144:6144 + 2 * D].bitcast(F32)
        wout3 = big[0:96, 6144 + 2 * D:6144 + 4 * D].bitcast(F32)
        pm2 = big[:, 6144 + 4 * D:6144 + 4 * D + 4 * P].bitcast(F32).rearrange("p (c n) -> p c n", c=2)
        hots = sb("hots", [P, max(HR * P, 16 * B)], F16)
        onesb = hots[:, 0:HR * P].rearrange("p (c n) -> p c n", c=HR)
        qfeat = hots[:, 0:16 * B].rearrange("p (r s c n) -> p r s c n", r=4, s=2, c=2)
        tiles_hot = sb("tiles_hot", [P, max(HR * NTP, SRING * P)], F16)
        onesa = tiles_hot[:, 0:HR * NTP].rearrange("p (c n) -> p c n", c=HR)
        hot = tiles_hot[:, 0:SRING * P].rearrange("p (r g n) -> p r g n", r=SRING, g=G)
        zz = sb("zz", [P, 2, D], F32)
        oo = sb("oo", [P, 2, D], F32)
        x1 = kvs[:].rearrange("p a d -> p (a d)")[:, 0:2 * D].rearrange("p (t n) -> p t n", t=2)
        pbr = hd[:].rearrange("p h n -> p (h n)")[:, 0:2 * D].bitcast(F32)
        own = vp[:].rearrange("p s t n -> p (s t n)")[:, 0:4 * D].rearrange("p (j n) -> p j n", j=2)
        srcw = sb("srcw", [P, 2, G, WIN], I32)
        dstw = sb("dstw", [P, 2, G, WIN], I32)
        dstl = sb("dstl", [P, 2, G, WIN], F32)
        den = sb("den", [P, 2, H], F32)
        rec = sb("rec", [P, 2, H], F32)
        gl = sb("gl", [P, 2, NN], F32)
        sg = sb("sg", [P, 2, NN], F32)
        ns = sb("ns", [P, 2, NN], F32)
        rr = sb("rr", [P, 2, NN], F32)
        cf = sb("cf", [P, 2, NN], F32)
        ux = sb("ux", [P, 2, NN], F32)
        su = sb("su", [P, 2, 4], F32)
        co = sb("co", [P, 2, 96], F16)
        coT = sb("coT", [96, B], F16)
        ring = region[:].rearrange("p (r n) -> p r n", n=2 * D)
        assert ring.shape[1] >= RING
        tin = [zz[:, i, :] for i in range(2)]
        tout = [oo[:, i, :].bitcast(F16) for i in range(2)]
        dcol = hots[:, 0:2 * EC].bitcast(I32)
        dnext = hots[:, 2 * EC:4 * EC].bitcast(I32)
        assert 4 * EC <= 6144 and 4 * EC <= max(HR * P, 16 * B)
        same = region[:, 0:2 * P].bitcast(F32)
        zero16 = tiles_hot[:, 0:BANK]
        sums3 = [zz[:, 0, :], zz[:, 1, :], xa[:, 0, :]]
        all_hot = oo[:].rearrange("p t n -> p (t n)").bitcast(F16)[:, 0:3 * WIN * P].rearrange("p (j k n) -> p j k n", j=3, k=WIN)
        away = dstl[:].rearrange("p j g k -> p (j g k)")[:, 0:3 * WIN].rearrange("p (j k) -> p j k", j=3)
        wst = [zz[:], oo[:]]
        xTf = xT[:].rearrange("p s k n -> p (s k n)").bitcast(F32)
        wst.append(xTf.rearrange("p (t n) -> p t n", t=2))
        NW = len(wst)

        padded = sem("padded")
        pad_ready = sem("pad_ready")
        edges_in = sem("edges_in")
        consts = sem("consts")
        vconsts = sem("vconsts")
        w_in_s = [sem(f"w_in{i}") for i in range(NW)]
        small_in = sem("small_in")
        w_turned = sem("w_turned")
        wg_hi = sem("wg_hi")
        wg_lo = sem("wg_lo")
        small_v = sem("small_v")
        slot_full = sem("slot_full")
        slot_a = sem("slot_a")
        slot_v = sem("slot_v")
        x_in = sem("x_in")
        stats = sem("stats")
        rstd = sem("rstd")
        normed = sem("normed")
        xn_out = sem("xn_out")
        xnt_out = sem("xnt_out")
        v_full = sem("v_full")
        v_hi = sem("v_hi")
        v_lo = sem("v_lo")
        v_summed = sem("v_summed")
        kv_full = sem("kv_full")
        kv_added = sem("kv_added")
        hots_built = sem("hots_built")
        hist_full = sem("hist_full")
        deg_added = sem("deg_added")
        vch = sem("vch")
        pch = sem("pch")
        mid_full = sem("mid_full")
        deg_done = sem("deg_done")
        dinv_done = sem("dinv_done")
        ranges_done = sem("ranges_done")
        mid_v = sem("mid_v")
        kv_ready = sem("kv_ready")
        tin_s = [sem(f"tin{i}") for i in range(2)]
        tout_s = [sem(f"tout{i}") for i in range(2)]
        t_hi = sem("t_hi")
        t_lo = sem("t_lo")
        xt_in = sem("xt_in")
        q_done = sem("q_done")
        win_s = [sem("win0"), sem("win1")]
        own_s = [sem("own0"), sem("own1")]
        hot_ready = sem("hot_ready")
        unit_used = sem("unit_used")
        got = [sem(f"got{i}") for i in range(RING)]
        z_full = sem("z_full")
        z_read = sem("z_read")
        xr_in = sem("xr_in")
        xr_biased = sem("xr_biased")
        acc_full = sem("acc_full")
        acc_read = sem("acc_read")
        o_ready = sem("o_ready")
        x1_stats = sem("x1_stats")
        x1_rstd = sem("x1_rstd")
        x1_normed = sem("x1_normed")
        coef = sem("coef")
        stored = sem("stored")
        stats_passed = sem("stats_passed")
        bad_in = sem("bad_in")
        bad_full = sem("bad_full")
        flag_ready = sem("flag_ready")
        all_go = sem("all_go")
        all_zero = sem("all_zero")
        all_in = sem("all_in")
        all_got = [sem(f"all_got{k}") for k in range(WIN)]
        all_away = sem("all_away")
        all_hots = sem("all_hots")
        all_used = sem("all_used")
        all_sum = sem("all_sum")
        all_read = sem("all_read")
        all_out = sem("all_out")
        row_in = sem("row_in")
        row_chain = sem("row_chain")
        row_ready = sem("row_ready")
        row_out = sem("row_out")
        edges_passed = sem("edges_passed")
        all_done = sem("all_done")
        gather_passed = sem("gather_passed")

        TABLE_AT = [divmod(max(0, 2 * k - 1), H // 2) for k in range(R)]

        V_AT = ((0, 3, 9, 12, 14, 16, 18), (0, 3, 6, 9, 12, 15, 18))

        READ = {"W": "av", "T": "av", "K": "av", "F": "av", "Q": "av", "X": "av", "L": "av",
                "C": "a", "Y": "v", "Z": "av", "O": "av"}
        NPREP = 3 * DC // 2 + DC // 2
        prep, prep_n = slots([("W", i, c) for i in range(NPREP) for c in range(3)]
                             + [("W", "pm", 0), ("W", "win", 0)], READ, None)

        def feat_uses(nt):
            return [("F", t, p) for t in range(nt) for p in range(H // 2)]

        def pass1(nt, before):
            return slots([("T", c, 0) for c in range(3)] + [("K", m, 0) for m in range(DC // 2)] + feat_uses(nt), READ, before)
        p1, p1_n = pass1(2, "F")
        p1_first, _ = pass1(2, "W")
        p1_tail, p1_tail_n = pass1(1, "F")
        base1 = prep_n
        tail1 = tuple(base1[i] + NB * p1_n[i] for i in range(3))
        base3 = tuple(tail1[i] + p1_tail_n[i] for i in range(3))
        assert base1[0] % 2 == 0 and p1_n[0] % 2 == 0

        def pass3(nt_prev, before, body=True):
            def q(*ms):
                return [("Q", m, 0) for m in ms] if body else []

            def f(*hs):
                return [("F", h, 0) for h in hs] if body else []

            def prev(*us):
                return [u for u in us if u[1] < nt_prev or u[0] in "XC"] if nt_prev else []
            names = q(0, 1) + f(0, 1) + q(2) + f(2, 3) + q(3) + prev(("X", 0, 0), ("X", 1, 0), ("X", 2, 0))
            names += f(4, 5) + q(4) + prev(("L", 0, 0), ("L", 1, 0)) + f(6, 7) + q(5) + f(8, 9, 10, 11)
            if body:
                names += [("Z", c, 0) for c in range(3)]
            names += prev(("C", 0, 0))
            if body:
                names += [("O", c, 0) for c in range(3)]
            names += prev(*[("Y", t, i) for t in range(2) for i in range(2)])
            return slots(names, READ, before)
        p3_first, p3_first_n = pass3(0, "F")
        p3, p3_n = pass3(2, "O")
        p3_end, p3_end_n = pass3(1, "O", body=False)
        assert p3_n[0] % 2 == 0

        places0 = [slot[0], slot[1], acc[0][:, 0:BANK], acc[1][:, 0:BANK]]

        def place0(u):
            return places0[u[0] % len(places0)]

        def bases1(b):
            return tuple(base1[i] + b * p1_n[i] for i in range(3))

        def bases3(b):
            if isinstance(b, int) and b == 0:
                return base3
            return tuple(base3[i] + p3_first_n[i] + (b - 1) * p3_n[i] for i in range(3))
        end3 = tuple(base3[i] + p3_first_n[i] + NB * p3_n[i] for i in range(3))

        def parity(base, u):
            return slot[(base + u[0]) % 2]
        par1 = base1[0] % 2
        par1_tail = tail1[0] % 2
        par3_first = base3[0] % 2
        par3 = (base3[0] + p3_first_n[0]) % 2
        par3_end = end3[0] % 2

        block = ctx.enter_context(nc.Block())

        @block.sync
        def _(sp):
            k_first = [DC // 2 + i for i in range(DC)] + [i for i in range(DC // 2)]
            rows = [("qkv", i) for i in k_first] + [("proj", i) for i in range(DC // 2)] + [("gnn", i) for i in range(DC // 2)]
            srcs = {"qkv": qkv_w, "proj": proj_w, "gnn": gnn_w}

            def stage(n):
                kind, i = rows[n]
                sp.dma_start(wst[n % NW][:, :, :], srcs[kind][i * B:(i + 1) * B, :].rearrange("(t p) d -> p t d", p=P)).then_inc(w_in_s[n % NW], 16)
            for n in range(NW):
                stage(n)
            sp.dma_start(dst_pad[0:E].rearrange("(a n) -> a n", a=1), dst.rearrange("(a n) -> a n", a=1)).then_inc(padded, 16)
            sp.dma_start(src_pad[0:E].rearrange("(a n) -> a n", a=1), src.rearrange("(a n) -> a n", a=1)).then_inc(padded, 16)
            sp.dma_start(pm2[:, :, 0:DH], proj_mat.rearrange("(c p) d -> p c d", p=P)).then_inc(small_in, 16)
            sp.dma_start(pm2[:, :, DH:P], proj_mat.rearrange("(c p) d -> p c d", p=P)).then_inc(small_in, 16)
            sp.dma_start(winr[0:NN, :], w_in).then_inc(small_in, 16)
            sp.wait_ge(vconsts, 1)
            for g in range(3):
                sp.dma_start(wout3[32 * g:32 * g + NN, :], w_out).then_inc(small_in, 16)
            sp.dma_start(bqk_r[:], qkv_b.rearrange("(c p) -> p c", p=P), allow_slow_non_contiguous=True).then_inc(small_in, 16)
            sp.dma_start(gpb[:], gnn_b.rearrange("(a n) -> a n", a=1).broadcast_to([P, D])).then_inc(small_in, 16)
            sp.dma_start(pbr, proj_b.rearrange("(a n) -> a n", a=1).broadcast_to([P, D])).then_inc(small_in, 16)
            sp.dma_start(xa[:, :, :], x[0:B, :].rearrange("(t p) d -> p t d", p=P)).then_inc(x_in, 16)
            sp.wait_ge(pad_ready, 2)
            n_dst, n_src = EP + P - E, EP - E
            for dram, row, n in ((dst_pad, 0, n_dst), (src_pad, 1, n_src)):
                full, rest = n // P, n % P
                sp.dma_start(dram[E:E + full * P].rearrange("(r n) -> r n", n=P),
                             padrow[0:full, row * P:(row + 1) * P]).then_inc(padded, 16)
                if rest:
                    sp.dma_start(dram[E + full * P:E + n].rearrange("(a n) -> a n", a=1),
                                 padrow[0:1, row * P:row * P + rest]).then_inc(padded, 16)
            npad = 2 + sum(1 + bool(n % P) for n in (n_dst, n_src))
            for n in range(NW, len(rows)):
                m = n - NW
                assert m < NPREP
                sp.wait_ge(w_turned, m + 1)
                stage(n)
                if n == NW + 1:
                    sp.wait_ge(padded, 16 * npad)
                    sp.dma_start(dcol, dst_pad[0:EP].rearrange("(p c) -> p c", p=P)).then_inc(edges_in, 16)
                    sp.dma_start(dnext, dst_pad[1:EP + 1].rearrange("(p c) -> p c", p=P)).then_inc(edges_in, 16)

            def store_norm(b, nt, tok):
                if nt == 2:
                    sp.dma_start(xn_dram[bass.ds(b * B, B), :].rearrange("(t p) d -> p t d", p=P), xb[:, :, :]).then_inc(xn_out, 16)
                else:
                    sp.dma_start(xn_dram[b * B:b * B + tok, :], xb[0:tok, 0, :]).then_inc(xn_out, 16)

            def store_turned(b, w, n_v):
                sp.wait_ge(slot_v, n_v)
                sp.dma_start(xnt_dram[bass.ds(b * P, P), :].rearrange("p (s n) -> p s n", s=2 * DC)[:, :, 0:w],
                             xT[:, :, :, 0:w].rearrange("p s k n -> p (s k) n")).then_inc(xnt_out, 16)

            def table_in(t, i, tok=P):
                sp.dma_start(tin[i][0:tok, :], xn_dram[bass.ds(t * P, tok), :]).then_inc(tin_s[i], 16)

            def table_out(t, i, tok=P):
                sp.wait_ge(t_lo, t + 1)
                sp.dma_start(table[bass.ds(t * P, tok), :], tout[i][0:tok, :]).then_inc(tout_s[i], 16)

            def next_x(b):
                sp.wait_ge(normed, 2 * b + 2)
                sp.dma_start(xa[:, :, :], x[bass.ds((b + 1) * B, B), :].rearrange("(t p) d -> p t d", p=P)).then_inc(x_in, 16)

            def stores(b, with_table):
                store_norm(b, 2, P)
                first = R * (b - NH)
                if with_table:
                    sp.wait_ge(xn_out, 16 * (b + 1))
                    for k in range(2):
                        table_in(first + k, k)
                store_turned(b, B, bases1(b)[2] + 3)
                if with_table:
                    for k in range(R):
                        table_out(first + k, k % 2)
                        if k + 2 < R:
                            table_in(first + k + 2, k % 2)
            with sp.Fori(0, NH) as b:
                next_x(b)
                stores(b, False)
            sp.wait_ge(wg_lo, DC // 2)
            for i in range(2):
                sp.sem_inc(tout_s[i], 1)
            with sp.Fori(NH, NB - 1) as b:
                next_x(b)
                stores(b, True)
            sp.wait_ge(normed, 2 * NB)
            sp.dma_start(xa[0:TAIL, 0, :], x[NB * B:N, :]).then_inc(x_in, 16)
            stores(NB - 1, True)
            sp.wait_ge(normed, 2 * NB + 1)
            store_norm(NB, 1, TAIL)
            store_turned(NB, TAIL, tail1[2] + 3)
            sp.wait_ge(xn_out, 16 * (NB + 1))
            table_in(NT - 1, 0, TAIL)
            table_out(NT - 1, 0, TAIL)
            sp.wait_ge(xnt_out, 16 * (NB + 1))
            for i in range(2):
                sp.wait_ge(tout_s[i], 16 * (NB + 1 - i) + 1)

            def general_sums():
                sp.sem_inc(all_go, 1)
                sp.sem_inc(all_out, 1)
                with sp.Fori(0, NPASS) as n:
                    with sp.Fori(0, NS) as i:
                        wait_apart(sp, all_used, n * NS + i + 1, edges_passed)
                        sp.dma_start(srcw[:, 0, 0, :], src_pad[bass.ds(i * (WIN * P), WIN * P)].rearrange("(p k) -> p k", p=P)).then_inc(all_in, 16)
                        sp.dma_start(dstw[:, 0, 0, :], dst_pad[bass.ds(i * (WIN * P), WIN * P)].rearrange("(p k) -> p k", p=P)).then_inc(all_in, 16)
                    wait_apart(sp, all_read, n + 2, edges_passed)
                    for j in range(3):
                        sp.dma_start(sums[bass.ds((3 * n + j) * P, P), :], sums3[j]).then_inc(all_out, 16)
                sp.wait_ge(all_out, 48 * NPASS + 1)

                def row(t, tok):
                    sp.dma_start(zz[0:tok, 0, :], sums[bass.ds(t * P, tok), :]).then_inc(row_in, 16)
                    sp.dma_start(own[0:tok, 0, :], table[bass.ds(t * P, tok), :]).then_inc(row_in, 16)
                    wait_apart(sp, row_ready, t + 1, edges_passed)
                    sp.dma_start(table[bass.ds(t * P, tok), :], own[0:tok, 1, :]).then_inc(row_out, 16)
                    wait_apart(sp, row_out, 16 * t + 16, edges_passed)
                with sp.Fori(0, NT - 1) as t:
                    row(t, P)
                row(NT - 1, TAIL)
                sp.sem_inc(all_done, 1)
                sp.wait_ge(all_done, 2)
            sp.wait_ge(flag_ready, 1)
            with sp.If(sp.value_load(flag[0:1, 0:1], min_val=0, max_val=1) > 0):
                general_sums()
            sp.wait_ge(ranges_done, 1)

            def load_turned(b, w):
                sp.dma_start(xT[:, :, :, 0:w].rearrange("p s k n -> p (s k) n"),
                             xnt_dram[bass.ds(b * P, P), :].rearrange("p (s n) -> p s n", s=2 * DC)[:, :, 0:w]).then_inc(xt_in, 16)

            def load_window(b, j, tok):
                for g in range(G):
                    at = sp.value_load(e0[g:g + 1, bass.ds(2 * b + j, 1)], min_val=0, max_val=E)
                    sp.dma_start(srcw[:, j, g, :], src_pad[bass.ds(at, WIN * P)].rearrange("(p k) -> p k", p=P)).then_inc(win_s[j], 16)
                    sp.dma_start(dstw[:, j, g, :], dst_pad[bass.ds(at, WIN * P)].rearrange("(p k) -> p k", p=P)).then_inc(win_s[j], 16)
                sp.dma_start(own[0:tok, j, :], table[bass.ds(b * B + j * P, tok), :]).then_inc(own_s[j], 16)

            def load_residual(b, nt, tok):
                if nt == 2:
                    sp.dma_start(xa[:, :, :], x[bass.ds(b * B, B), :].rearrange("(t p) d -> p t d", p=P)).then_inc(xr_in, 16)
                else:
                    sp.dma_start(xa[0:tok, 0, :], x[b * B:b * B + tok, :]).then_inc(xr_in, 16)

            def store_out(b, n_v, nt=2, tok=P):
                sp.wait_ge(slot_v, n_v)
                if nt == 2:
                    sp.dma_start(out[bass.ds(b * B, B), :].rearrange("(t p) d -> p t d", p=P), yo[:, :, :]).then_inc(stored, 16)
                else:
                    sp.dma_start(out[b * B:b * B + tok, :], yo[0:tok, 0, :]).then_inc(stored, 16)

            load_turned(0, B)
            load_window(0, 0, P)
            load_window(0, 1, P)
            load_residual(0, 2, P)

            def loads(b, nt=2, tok=P, store=True):
                sp.wait_ge(z_full, 2 * b - 1)
                load_window(b, 0, P if nt == 2 else tok)
                sp.wait_ge(q_done, b)
                load_turned(b, B if nt == 2 else tok)
                if nt == 2:
                    sp.wait_ge(z_full, 2 * b)
                    load_window(b, 1, P)
                if store:
                    store_out(b - 2, bases3(b - 1)[2] + p3[("Y", 1, 1)][2] + 1)
                sp.wait_ge(x1_stats, 2 * b)
                if store:
                    sp.wait_ge(stored, 16 * (b - 1))
                load_residual(b, nt, tok)
            loads(1, store=False)
            with sp.Fori(2, NB) as b:
                loads(b)
            loads(NB, 1, TAIL)
            store_out(NB - 1, bases3(NB)[2] + p3[("Y", 1, 1)][2] + 1)
            store_out(NB, end3[2] + p3_end[("Y", 0, 1)][2] + 1, 1, TAIL)
            sp.wait_ge(stored, 16 * (NB + 1))

        @block.gpsimd
        def _(pool):
            g = nc.gpsimd
            n_chain = [0]

            def link(ins):
                n_chain[0] += 1
                ins.then_inc(pch, 1)
                pool.wait_ge(pch, n_chain[0])
            g.memset(padrow[:, 0:P], BIG).then_inc(pad_ready, 1)
            g.memset(padrow[:, P:2 * P], 0).then_inc(pad_ready, 1)
            link(g.memset(ident[:], 0.0))
            link(g.affine_select(out=ident[:], in_=ident[:], compare_op=ALU.not_equal, fill=1.0, base=0,
                                 pattern=[[-1, P]], channel_multiplier=1))
            g.tensor_copy(ident16[:], ident[:]).then_inc(consts, 1)
            link(g.iota(iota_i[:], pattern=[[1, P]], base=0, channel_multiplier=0))
            g.tensor_copy(iota16[:], iota_i[:]).then_inc(consts, 1)
            link(g.iota(tile_i[:], pattern=[[P, NTP + 2]], base=0, channel_multiplier=0))
            g.tensor_copy(tile_base[:], tile_i[:]).then_inc(consts, 1)
            link(g.memset(ones[:], 1.0))
            g.memset(epsk[:], ZS * EPS_FEAT).then_inc(consts, 1)
            link(g.memset(mhalf[:], -0.5))
            link(g.memset(eps_ln[:], EPS_LN))
            for i in range(G):
                link(g.affine_select(out=below[:, i:i + 1], in_=ones[:, 0:1], compare_op=ALU.is_gt, fill=0.0,
                                     base=GN * i, pattern=[[0, 1]], channel_multiplier=-1))
            g.memset(var_eps[:], 0.0).then_inc(consts, 1)
            link(g.memset(vacc[:], 0.0))

            def inverse_std(n_stats, t, tok):
                pool.wait_ge(stats, n_stats)
                g.tensor_tensor(var_eps[0:tok, t:t + 1], mv[0:tok, t, 1:2], eps_ln[0:tok, :], ALU.add).then_inc(rstd, 1)
                pool.wait_ge(rstd, 2 * n_stats - 1)
                g.tensor_tensor(rs[0:tok, t:t + 1], var_eps[0:tok, t:t + 1], mhalf[0:tok, 0:1], ALU.pow).then_inc(rstd, 1)

            def sum_v(n, t, tok):
                pool.wait_ge(v_lo, n + 1)
                wait_for(pool, v_summed, 2 * n)
                g.tensor_tensor(vacc[0:tok, :], vacc[0:tok, :], vp[0:tok, 0, t, :], ALU.add).then_inc(v_summed, 1)
                pool.wait_ge(v_summed, 2 * n + 1)
                g.tensor_tensor(vacc[0:tok, :], vacc[0:tok, :], vp[0:tok, 1, t, :], ALU.add).then_inc(v_summed, 1)
            inverse_std(1, 0, P)
            inverse_std(2, 1, P)

            def gp1(b, nt_next, tok_next):
                for t in range(nt_next):
                    inverse_std(2 * b + 3 + t, t, tok_next)
                for t in range(2):
                    sum_v(2 * b + t, t, P)
            gp1(0, 2, P)
            with pool.Fori(1, NH) as b:
                gp1(b, 2, P)
            pool.wait_ge(deg_done, 1)
            link(g.tensor_scalar(scanB[:], degs[:], 1.0, None, ALU.add))
            g.tensor_tensor(dinv[:], scanB[:], mhalf[:], ALU.pow).then_inc(dinv_done, 1)
            with pool.Fori(NH, NB - 1) as b:
                gp1(b, 2, P)
            gp1(NB - 1, 1, TAIL)
            sum_v(2 * NB, 0, TAIL)

            def general_sums():
                pool.wait_ge(all_go, 1)
                with pool.Fori(0, NPASS) as n:
                    with pool.Fori(0, NS) as i:
                        wait_apart(pool, all_in, 32 * (n * NS + i) + 32, gather_passed)
                        for k in range(WIN):
                            g.indirect_dma_start(ring[:, k, :], None, table,
                                                 bass.IndirectOffsetOnAxis(ap=srcw[:, 0, 0, k:k + 1].bitcast(U32), axis=0)).then_inc(all_got[k], 16)
                pool.wait_ge(all_done, 2)
            pool.wait_ge(flag_ready, 1)
            with pool.If(pool.value_load(flag[0:1, 0:1], min_val=0, max_val=1) > 0):
                general_sums()

            def gather(b, k):
                j, u, g_, r = k // (G * WIN), k % (G * WIN) // G, k % G, k % RING
                if k % (G * WIN) == 0:
                    wait_apart(pool, win_s[j], 2 * G * 16 * (b + 1), gather_passed)
                wait_apart(pool, unit_used, 2 * WIN * b + (k - RING) // G + 1, gather_passed)
                g.indirect_dma_start(ring[:, r, :], None, table,
                                     bass.IndirectOffsetOnAxis(ap=srcw[:, j, g_, u:u + 1].bitcast(U32), axis=0)).then_inc(got[r], 16)

            def bias_residual(b, nt, tok):
                pool.wait_ge(xr_in, 16 * (b + 1))
                for t in range(nt):
                    g.tensor_tensor(xa[0:tok, t, :], xa[0:tok, t, :], gpb[0:tok, :], ALU.add).then_inc(xr_biased, 1)

            def inverse_std_x1(n, t, tok):
                pool.wait_ge(x1_stats, n)
                g.tensor_tensor(var_eps[0:tok, t:t + 1], mv[0:tok, t, 1:2], eps_ln[0:tok, :], ALU.add).then_inc(x1_rstd, 1)
                pool.wait_ge(x1_rstd, 2 * n - 1)
                g.tensor_tensor(rs[0:tok, t:t + 1], var_eps[0:tok, t:t + 1], mhalf[0:tok, 0:1], ALU.pow).then_inc(x1_rstd, 1)

            def gp3(b, nt=2, tok=P, prev=True):
                n = 3 * RING if nt == 2 else G * WIN
                for k in range(n):
                    gather(b, k)
                if prev:
                    for t in range(2):
                        inverse_std_x1(2 * b - 1 + t, t, P)
                for k in range(n, nt * G * WIN):
                    gather(b, k)
                bias_residual(b, nt, tok)
            gp3(0, prev=False)
            with pool.Fori(1, NB) as b:
                gp3(b)
            gp3(NB, 1, TAIL)
            inverse_std_x1(2 * NB + 1, 0, TAIL)

        @block.scalar
        def _(act):
            a = nc.scalar

            def evac(base, u, ops):
                act.wait_ge(slot_full, base[0] + u[0] + 1)
                for o, i, f, kw in ops:
                    last = a.activation(o, i, f, **kw)
                last.then_inc(slot_a, 1)

            def weight_dest(i):
                w = (wk, wv, wq, wp)[i // 3]
                return w, (i % 3) * B
            for i in range(NPREP):
                w, c0 = weight_dest(i)
                for c in range(3):
                    u = prep[("W", i, c)]
                    evac((0, 0, 0), u, [(w[:, 0, 2 * c:2 * c + 2, c0:c0 + B],
                                         place0(u)[:].rearrange("p (k n) -> p k n", k=2), ACT.Copy, dict(scale=WS))])
            u = prep[("W", "pm", 0)]
            evac((0, 0, 0), u, [(pmT[:, 0, :], place0(u)[:, 0:M], ACT.Copy, {})])
            u = prep[("W", "win", 0)]
            evac((0, 0, 0), u, [(winT[:, 0, :, :], place0(u)[:, 0:DC * 32].rearrange("p (k n) -> p k n", k=DC)[:, :, 0:NN], ACT.Copy, {})])
            for i in range(DC // 2):
                n = NPREP + i
                act.wait_ge(w_in_s[n % NW], 16 * (n // NW + 1))
                a.activation(wg[:, 0, 2 * i:2 * i + 2, :], wst[n % NW][:, :, :], ACT.Copy, scale=WS).then_inc(wg_hi, 1)

            def turned_hi(base, par, plan, kind, dst_, w, cs=range(3)):
                for c in cs:
                    u = plan[(kind, c, 0)]
                    evac(base, u, [(dst_[:, 0, 2 * c:2 * c + 2, 0:w],
                                    parity(par, u)[:].rearrange("p (k n) -> p k n", k=2)[:, :, 0:w], ACT.Copy, {})])

            def high_ops(s, m, col, w):
                return [(hd[64 * e:64 * e + 64, 2 * m + e, 0:w], s[64 * e:64 * e + 64, 0:w], ACT.Identity,
                         dict(bias=bqk[64 * e:64 * e + 64, col + m:col + m + 1])) for e in range(2)]

            def keys_hi(base, par, plan, c, w):
                u = plan[("K", c, 0)]
                s = parity(par, u)
                evac(base, u, high_ops(s[:, 0:B], 2 * c, DC, w) + high_ops(s[:, B:2 * B], 2 * c + 1, DC, w))

            def queries_hi(base, par, plan, m, w):
                u = plan[("Q", m, 0)]
                evac(base, u, high_ops(parity(par, u), m, 0, w))

            def table_hi(t, half, i, tok=P):
                act.wait_ge(tin_s[i], 16 * half + 16)
                act.wait_ge(tout_s[i], 16 * half + 1)
                a.activation(tout[i][0:tok, 0:D], tin[i][0:tok, :], ACT.Copy, scale=dinvT[0:tok, bass.ds(t, 1)]).then_inc(t_hi, 1)

            def act1(b, plan, nt, tok, base, par, with_table=False):
                w = B if nt == 2 else tok
                wait_for(act, xnt_out, 16 * b)
                turned_hi(base, par, plan, "T", xT, w)
                for c in range(3):
                    keys_hi(base, par, plan, c, w)
                for t in range(nt):
                    for p in range(H // 2):
                        u = plan[("F", t, p)]
                        evac(base, u, [(kfeat[0:tok, 0, t, 2 * p * M:(2 * p + 2) * M], parity(par, u)[0:tok, :], ACT.Relu, {})])
                        if with_table and (t, p) in TABLE_AT:
                            k = TABLE_AT.index((t, p))
                            table_hi(R * (b - NH) + k, R // 2 * (b - NH) + k // 2, k % 2)
                    act.wait_ge(v_full, 2 * b + t + 1)
                    wait_for(act, v_summed, 2 * (2 * b + t) - 2)
                    a.activation(vp[0:tok, 0, t, :].rearrange("p (h d) -> p h d", h=H)[:, :, 0:DH],
                                 acc[t][0:tok, 0:D].rearrange("p (h d) -> p h d", h=H), ACT.Copy).then_inc(v_hi, 1)
            act.wait_ge(small_v, 1)
            act.wait_ge(wg_lo, DC // 2)
            act1(0, p1_first, 2, P, bases1(0), par1)
            with act.Fori(1, NH) as b:
                act1(b, p1, 2, P, bases1(b), par1)
            act.wait_ge(dinv_done, 2)
            with act.Fori(NH, NB) as b:
                act1(b, p1, 2, P, bases1(b), par1, with_table=True)
            act1(NB, p1_tail, 1, TAIL, tail1, par1_tail)

            table_hi(NT - 1, NB, 0, TAIL)

            def general_sums():
                act.sem_inc(all_read, 1)
                with act.Fori(0, NPASS) as n:
                    act.wait_ge(all_sum, n + 1)
                    act.wait_ge(all_out, 48 * n + 1)
                    for o, to in zip((acc[0], acc[1], zps), sums3):
                        last = a.activation(to, o[:, 0:D], ACT.Copy)
                    last.then_inc(all_read, 1)
                act.wait_ge(all_done, 2)
            act.wait_ge(flag_ready, 1)
            with act.If(act.value_load(flag[0:1, 0:1], min_val=0, max_val=1) > 0):
                general_sums()

            def logits_hi(base, par, plan, nt, tok):
                for t in range(nt):
                    u = plan[("L", t, 0)]
                    evac(base, u, [(gl[0:tok, t, :], parity(par, u)[0:tok, 0:NN], ACT.Gelu, {})])

            def coefficients(base, par, plan, w):
                u = plan[("C", 0, 0)]
                evac(base, u, [(coT[:, 0:w], parity(par, u)[0:96, :].bitcast(F16)[:, 0:w], ACT.Copy, {})])

            def read_z(n, t, tok):
                act.wait_ge(z_full, n + 1)
                a.activation(zz[0:tok, t, :], zps[0:tok, 0:D], ACT.Copy, scale=dinvZ[0:tok, bass.ds(n, 1)]).then_inc(z_read, 1)

            def act3(b, plan, nt, tok, prev):
                base, w = bases3(b), (B if nt == 2 else tok)
                par = par3_first if prev is None else par3
                if prev:
                    read_z(2 * b, 0, tok)

                def features(h):
                    u = plan[("F", h, 0)]
                    evac(base, u, [(qfeat[:, h % 4, 0, :, 0:w], parity(par, u)[:].rearrange("p (c n) -> p c n", c=2)[:, :, 0:w], ACT.Relu, {})])

                def q_heads(m):
                    queries_hi(base, par, plan, m, w)
                q_heads(0)
                q_heads(1)
                features(0)
                features(1)
                q_heads(2)
                features(2)
                features(3)
                q_heads(3)
                if prev:
                    turned_hi(base, par, plan, "X", x1T, B)
                else:
                    read_z(2 * b, 0, tok)
                features(4)
                features(5)
                q_heads(4)
                if prev:
                    logits_hi(base, par, plan, 2, P)
                features(6)
                features(7)
                q_heads(5)
                for h in range(8, 10):
                    features(h)
                if nt == 2:
                    read_z(2 * b + 1, 1, tok)
                features(10)
                features(11)
                turned_hi(base, par, plan, "Z", zT, w)
                if prev:
                    coefficients(base, par, plan, B)
                for c in range(3):
                    u = plan[("O", c, 0)]
                    s = parity(par, u)
                    evac(base, u, [(oT[:, 0, 2 * c + e, 0:w], s[:, e * B:e * B + w], ACT.Identity,
                                    dict(bias=bqk[:, 2 * DC + 2 * c + e:2 * DC + 2 * c + e + 1])) for e in range(2)])
            act3(0, p3_first, 2, P, None)
            with act.Fori(1, NB) as b:
                act3(b, p3, 2, P, True)
            act3(NB, p3, 1, TAIL, True)
            turned_hi(end3, par3_end, p3_end, "X", x1T, TAIL)
            logits_hi(end3, par3_end, p3_end, 1, TAIL)
            coefficients(end3, par3_end, p3_end, TAIL)

        @block.tensor
        def _(pe):
            def fill(base, u, need=0):
                wait_for(pe, slot_a, base[1] + u[3])
                wait_for(pe, slot_v, base[2] + max(u[4], need))

            def fill0(u):
                wait_for(pe, slot_v, u[0] - len(places0) + 1)
            pe.wait_ge(consts, 1)
            for i in range(NPREP):
                pe.wait_ge(w_in_s[i % NW], 16 * (i // NW + 1))
                for c in range(3):
                    u = prep[("W", i, c)]
                    fill0(u)
                    for k in range(2):
                        for t in range(2):
                            mm = pe.transpose(place0(u)[:, k * B + t * P:k * B + (t + 1) * P],
                                              wst[i % NW][:, t, (2 * c + k) * P:(2 * c + k + 1) * P], ident[:])
                    mm.then_inc(slot_full, 1)
                pe.wait_ge(slot_full, 3 * i + 3)
                pe.sem_inc(w_turned, 1)
            pe.wait_ge(small_in, 16 * 9)
            u = prep[("W", "pm", 0)]
            fill0(u)
            for c in range(2):
                mm = pe.transpose(place0(u)[:, c * P:(c + 1) * P], pm2[:, c, :], ident[:])
            mm.then_inc(slot_full, 1)
            u = prep[("W", "win", 0)]
            fill0(u)
            for k in range(DC):
                mm = pe.transpose(place0(u)[:, 32 * k:32 * k + NN], winr[0:NN, k * P:(k + 1) * P], ident[0:NN, 0:NN])
            mm.then_inc(slot_full, 1)

            def turn(base, par, plan, kind, what, nt, tok, cs=range(3)):
                for c in cs:
                    u = plan[(kind, c, 0)]
                    fill(base, u)
                    for k in range(2):
                        for t in range(nt):
                            mm = pe.transpose(parity(par, u)[:, k * B + t * P:k * B + t * P + tok],
                                              what[0:tok, t, (2 * c + k) * P:(2 * c + k + 1) * P], ident[0:tok, 0:tok])
                    mm.then_inc(slot_full, 1)

            def project_heads(base, par, plan, kind, wgt, m, w, need=0):
                u = plan[(kind, m, 0)]
                fill(base, u)
                for i, (s, r) in enumerate(PAIRS):
                    if i == 1 and need:
                        pe.wait_ge(slot_v, base[2] + need)
                    for k in range(DC):
                        mm = pe.matmul(parity(par, u)[:, 0:w], wgt[:, r, k, m * P:(m + 1) * P], xT[:, s, k, 0:w],
                                       start=(i == 0 and k == 0), stop=(i == 2 and k == DC - 1))
                mm.then_inc(slot_full, 1)
                return mm

            def add_kv(n, half, nt, tok, rounds=2 * NH):
                pe.wait_ge(kv_added, 2 * n + half)
                if half == 0:
                    pe.wait_ge(deg_added, rounds)
                    pe.wait_ge(v_lo, 2 * n + nt)
                kvq = (zps, acc[0])[half]
                for i in range(12):
                    h, c = 6 * half + i // 2, i % 2
                    o = kvq[:, (i // 6) * BANK + (i % 6) * DV:(i // 6) * BANK + (i % 6 + 1) * DV]
                    for t in range(nt):
                        for q, (s, r) in enumerate(PAIRS):
                            mm = pe.matmul(o, kfeat[0:tok, s, t, h * M + c * P:h * M + (c + 1) * P],
                                           vp[0:tok, r, t, h * DV:(h + 1) * DV],
                                           start=(t == 0 and q == 0), stop=(t == nt - 1 and q == 2))
                mm.then_inc(kv_full, 1)

            def histogram(n, r):
                pe.wait_ge(hots_built, 2 * n + r + 1)
                wait_for(pe, deg_added, 2 * n + r)
                cols = (ends[FIRST], HC - ends[FIRST])[r]
                for i in range(cols):
                    mm = pe.matmul(zps[:, 0:NTP], onesb[:, i, :], onesa[:, i, :], start=(i == 0), stop=(i == cols - 1))
                mm.then_inc(hist_full, 1)

            def v_step(n, t, tok, i, kv_n):
                s, r = PAIRS[i // DC]
                k = i % DC
                if i == 0 and t == 0:
                    pe.wait_ge(kv_added, kv_n)
                if i == 0 and t == 1:
                    wait_for(pe, v_lo, n - 1)
                for c0, c1 in ((0, BANK), (BANK, D)):
                    mm = pe.matmul(acc[t][0:tok, c0:c1], xT[:, s, k, t * P:t * P + tok], wv[:, r, k, c0:c1],
                                   start=(i == 0), stop=(i == 17))
                if i == 17:
                    mm.then_inc(v_full, 1)

            def project_keys(base, par, plan, c, w, need):
                u = plan[("K", c, 0)]
                fill(base, u)
                for e in range(2):
                    for i, (s, r) in enumerate(PAIRS):
                        if i == 1 and e == 0 and need:
                            pe.wait_ge(slot_v, base[2] + need)
                        for k in range(DC):
                            mm = pe.matmul(parity(par, u)[:, e * B:e * B + w], wk[:, r, k, (2 * c + e) * P:(2 * c + e + 1) * P],
                                           xT[:, s, k, 0:w], start=(i == 0 and k == 0), stop=(i == 2 and k == DC - 1))
                mm.then_inc(slot_full, 1)

            def pe1(b, plan, nt, tok, base, par, first=False, hist=False):
                rounds = 2 * b if hist else 2 * NH
                w = B if nt == 2 else tok
                pe.wait_ge(normed, 2 * b + nt)
                turn(base, par, plan, "T", xb, nt, tok, (0, 1))
                if not first:
                    add_kv(b - 1, 0, 2, P, rounds)
                turn(base, par, plan, "T", xb, nt, tok, (2,))
                if not first:
                    add_kv(b - 1, 1, 2, P)
                pe.wait_ge(slot_a, base[1] + 3)
                for c in range(3):
                    project_keys(base, par, plan, c, w, need=3 if c == 0 else 0)
                for t in range(nt):
                    for p in range(H // 2):
                        for i in range(V_AT[t][p], V_AT[t][p + 1]):
                            v_step(2 * b + t, t, tok, i, 2 * b + 1)
                        u = plan[("F", t, p)]
                        fill(base, u, need=plan[("K", p // 2, 0)][2] + 1)
                        for e in range(2):
                            for r in range(2):
                                mm = pe.matmul(parity(par, u)[0:tok, e * M:(e + 1) * M], hd[:, 2 * p + e, t * P:t * P + tok],
                                               pmT[:, r, :], start=(r == 0), stop=(r == 1))
                        mm.then_inc(slot_full, 1)
                        if hist and (t, p) in ((0, 2), (1, 5)):
                            histogram(b, t)
            pe.wait_ge(slot_v, prep_n[2])
            pe1(0, p1_first, 2, P, bases1(0), par1, first=True, hist=True)
            with pe.Fori(1, NH) as b:
                pe1(b, p1, 2, P, bases1(b), par1, hist=True)
            with pe.Fori(NH, NB) as b:
                pe1(b, p1, 2, P, bases1(b), par1)
            pe1(NB, p1_tail, 1, TAIL, tail1, par1_tail)
            add_kv(NB, 0, 1, TAIL)
            add_kv(NB, 1, 1, TAIL)

            half = H // 2 * DV
            pe.wait_ge(v_summed, 2 * NT)
            pe.wait_ge(kv_added, 2 * NB + 3)
            for i in range(2):
                mm = pe.matmul(acc[0][:, i * BANK:i * BANK + half], epsk[:], vacc[:, i * half:(i + 1) * half], start=True, stop=True)
            mm.then_inc(mid_full, 1)
            pe.wait_ge(deg_done, 1)
            pe.matmul(acc[1][:, 0:NTP], ones[:], degs[:], start=True, stop=True)
            pe.matmul(acc[1][0:G, NTP:2 * NTP], below[:], degs[:], start=True, stop=True).then_inc(mid_full, 1)
            pe.wait_ge(mid_v, 1)
            pe.matmul(acc[1][:, BANK:BANK + H], ones[:], kf[:, 0:H], start=True, stop=True).then_inc(mid_full, 1)
            pe.wait_ge(mid_v, 2)
            kvv = kvs[:].rearrange("p (h c) d -> p h c d", c=2)
            for i in range(2):
                for c in range(2):
                    mm = pe.matmul(acc[0][:, i * BANK:i * BANK + half].rearrange("p (h d) -> p h d", d=DV), epsk[:],
                                   kvv[:, 6 * i:6 * i + 6, c, :], start=(c == 0), stop=(c == 1))
            mm.then_inc(mid_full, 1)
            pe.wait_ge(bad_in, 1)
            pe.matmul(acc[1][:, 2 * NTP:3 * NTP], same, degs[:], start=True, stop=True).then_inc(bad_full, 1)
            pe.wait_ge(bad_in, 2)
            pe.matmul(acc[1][:, 3 * NTP:3 * NTP + 1], ones[:], bad[:, 3:4], start=True, stop=True).then_inc(bad_full, 1)
            pe.wait_ge(kv_ready, 1)

            def general_sums():
                places = [(acc[0], 0), (acc[1], 1), (zps, 2)]

                def edge(first):
                    for o, _ in places:
                        for c0, c1 in ((0, BANK), (BANK, D)):
                            mm = pe.matmul(o[:, c0:c1], zero16[:, 0:P], zero16[:, 0:c1 - c0], start=first, stop=not first)
                    return mm
                pe.wait_ge(all_zero, 1)
                pe.sem_inc(all_used, 1)
                with pe.Fori(0, NPASS) as n:
                    pe.wait_ge(all_read, n + 1)
                    edge(True)
                    with pe.Fori(0, NS) as i:
                        pe.wait_ge(all_hots, n * NS + i + 1)
                        for k in range(WIN):
                            pe.wait_ge(all_got[k], 16 * (n * NS + i) + 16)
                        for k in range(WIN):
                            for o, j in places:
                                for h in range(2):
                                    for c0, c1 in ((0, BANK), (BANK, D)):
                                        mm = pe.matmul(o[:, c0:c1], all_hot[:, j, k, :], ring[:, k, h * D + c0:h * D + c1],
                                                       start=False, stop=False)
                        mm.then_inc(all_used, 1)
                    edge(False).then_inc(all_sum, 1)
                pe.wait_ge(all_done, 2)
            pe.wait_ge(flag_ready, 1)
            with pe.If(pe.value_load(flag[0:1, 0:1], min_val=0, max_val=1) > 0):
                general_sums()

            def aggregate(b, u):
                j = u // WIN
                if u % WIN == 0:
                    wait_for(pe, z_read, 2 * b + j)
                pe.wait_ge(hot_ready, 2 * WIN * b + u + 1)
                for g in range(G):
                    k = G * u + g
                    pe.wait_ge(got[k % RING], 16 * ((2 * G * WIN // RING) * b + k // RING + 1))
                for s in range(2):
                    for c0, c1 in ((0, BANK), (BANK, D)):
                        for g in range(G):
                            mm = pe.matmul(zps[g * GN:(g + 1) * GN, c0:c1], hot[:, u % SRING, g, :],
                                           ring[:, (G * u + g) % RING, s * D + c0:s * D + c1],
                                           start=(u % WIN == 0 and s == 0), stop=False)
                mm.then_inc(unit_used, 1)

            def own_rows(b, j, tok):
                pe.wait_ge(own_s[j], 16 * (b + 1))
                for s in range(2):
                    for c0, c1 in ((0, BANK), (BANK, D)):
                        mm = pe.matmul(zps[:, c0:c1], ident16[0:tok, :], own[0:tok, j, s * D + c0:s * D + c1],
                                       start=False, stop=(s == 1))
                mm.then_inc(z_full, 1)

            def logits(base, par, plan, t, tok):
                u = plan[("L", t, 0)]
                fill(base, u, need=plan[("X", 2, 0)][2] + 1)
                for i, (s, r) in enumerate(PAIRS):
                    for k in range(DC):
                        mm = pe.matmul(parity(par, u)[0:tok, 0:NN], x1T[:, s, k, t * P:t * P + tok], winT[:, r, k, :],
                                       start=(i == 0 and k == 0), stop=(i == 2 and k == DC - 1))
                mm.then_inc(slot_full, 1)

            def turn_coefficients(base, par, plan, nt, tok, n_coef):
                u = plan[("C", 0, 0)]
                pe.wait_ge(coef, n_coef)
                fill(base, u)
                for t in range(nt):
                    mm = pe.transpose(parity(par, u)[0:96, :].bitcast(F16)[:, t * P:t * P + tok], co[0:tok, t, :], ident16[0:tok, 0:tok])
                mm.then_inc(slot_full, 1)

            def tree_rows(base, par, plan, t, tok, halves=(0, 1)):
                pe.wait_ge(slot_a, base[1] + plan[("C", 0, 0)][1] + 1)
                for i in halves:
                    c0, c1 = ((0, BANK), (BANK, D))[i]
                    u = plan[("Y", t, i)]
                    fill(base, u)
                    pe.matmul(parity(par, u)[0:tok, 0:c1 - c0], coT[:, t * P:t * P + tok], wo[:, c0:c1],
                              start=True, stop=True).then_inc(slot_full, 1)

            def attend(b, plan, h, nt, tok, w):
                for t in range(nt):
                    o = acc[t][0:tok, (h // 6) * BANK + (h % 6) * DV:(h // 6) * BANK + (h % 6 + 1) * DV]
                    for c in range(2):
                        for i, (s, r) in enumerate(PAIRS):
                            mm = pe.matmul(o, qfeat[:, h % 4, s, c, t * P:t * P + tok], kvp[:, r, 2 * h + c, :],
                                           start=(c == 0 and i == 0), stop=(c == 1 and i == 2))
                    if h == H - 1:
                        mm.then_inc(acc_full, 1)

            def pe3(b, plan, nt, tok, prev):
                base, w = bases3(b), (B if nt == 2 else tok)
                par = par3_first if prev is None else par3
                if prev:
                    own_rows(b, 0, tok)
                pe.wait_ge(xt_in, 16 * (b + 1))
                units = iter(range(WIN if prev else 0, 2 * WIN) if nt == 2 else ())

                def unit():
                    for _ in range(1 if prev else 2):
                        u_ = next(units, None)
                        if u_ is not None:
                            aggregate(b, u_)
                        if u_ == WIN - 1:
                            own_rows(b, 0, tok)

                def features(h):
                    uf = plan[("F", h, 0)]
                    fill(base, uf, need=plan[("Q", h // 2, 0)][2] + 1)
                    for c in range(2):
                        for r in range(2):
                            mm = pe.matmul(parity(par, uf)[:, c * B:c * B + w], pmT[:, r, c * P:(c + 1) * P], hd[:, h, 0:w],
                                           start=(r == 0), stop=(r == 1))
                    mm.then_inc(slot_full, 1)

                def attend_to(h):
                    pe.wait_ge(slot_v, base[2] + plan[("F", h, 0)][2] + 1)
                    attend(b, plan, h, nt, tok, w)

                def project(m):
                    project_heads(base, par, plan, "Q", wq, m, w)

                def turn_x1(c):
                    if prev:
                        turn(base, par, plan, "X", xb, 2, P, (c,))
                project(0)
                project(1)
                features(0)
                unit()
                features(1)
                project(2)
                features(2)
                if prev:
                    pe.wait_ge(acc_read, 4 * b)
                attend_to(0)
                attend_to(1)
                unit()
                features(3)
                project(3)
                if prev:
                    pe.wait_ge(x1_normed, 2 * b)
                turn_x1(0)
                attend_to(2)
                unit()
                turn_x1(1)
                turn_x1(2)
                attend_to(3)
                features(4)
                features(5)
                project(4)
                if prev:
                    logits(base, par, plan, 0, P)
                attend_to(4)
                attend_to(5)
                unit()
                if prev:
                    logits(base, par, plan, 1, P)
                features(6)
                features(7)
                project(5)
                pe.wait_ge(slot_full, base[0] + plan[("Q", 5, 0)][0] + 1)
                pe.sem_inc(q_done, 1)
                features(8)
                attend_to(6)
                unit()
                features(9)
                attend_to(7)
                if nt == 2:
                    own_rows(b, 1, P)
                features(10)
                attend_to(8)
                features(11)
                attend_to(9)
                pe.wait_ge(z_read, 2 * b + nt)
                turn(base, par, plan, "Z", zz, nt, tok, (0,))
                attend_to(10)
                turn(base, par, plan, "Z", zz, nt, tok, (1,))
                attend_to(11)
                turn(base, par, plan, "Z", zz, nt, tok, (2,))
                nxt = iter(range(WIN) if nt == 2 else ())

                def unit_ahead():
                    u_ = next(nxt, None)
                    if u_ is not None:
                        aggregate(b + 1, u_)
                unit_ahead()
                pe.wait_ge(slot_a, base[1] + plan[("Z", 2, 0)][1] + 1)
                pe.wait_ge(acc_read, 4 * b + 1)
                for i in range(3):
                    if i == 1:
                        pe.wait_ge(slot_v, base[2] + plan[("Z", 2, 0)][2] + 1)
                    convolve(0, tok, i)
                    if i == 0 and prev:
                        turn_coefficients(base, par, plan, 2, P, b)
                unit_ahead()
                if nt == 2:
                    pe.wait_ge(acc_read, 4 * b + 2)
                for i in range(3):
                    if i == 0:
                        pe.wait_ge(o_ready, 2 * b + nt)
                    turn(base, par, plan, "O", oo, nt, tok, (i,))
                    if nt == 2:
                        convolve(1, tok, i)
                unit_ahead()
                pe.wait_ge(slot_v, base[2] + plan[("O", 2, 0)][2] + 1)
                for t in range(nt):
                    for i in range(3):
                        mm = attention_out(t, tok, i)
                        if i == 2:
                            mm.then_inc(acc_full, 1)
                        if prev and t == 0:
                            tree_rows(base, par, plan, i // 2, P, (i % 2,))
                        if (t, i) == (1, 1):
                            unit_ahead()
                    if t == 0:
                        if prev:
                            tree_rows(base, par, plan, 1, P, (1,))
                        unit_ahead()

            def attention_out(t, tok, i):
                s, r = PAIRS[i]
                for k in range(DC):
                    for c0, c1 in ((0, BANK), (BANK, D)):
                        mm = pe.matmul(acc[t][0:tok, c0:c1], oT[:, s, k, t * P:t * P + tok], wp[:, r, k, c0:c1],
                                       start=False, stop=(i == 2 and k == DC - 1))
                return mm

            def convolve(t, tok, i):
                s, r = PAIRS[i]
                for k in range(DC):
                    for c0, c1 in ((0, BANK), (BANK, D)):
                        pe.matmul(acc[t][0:tok, c0:c1], zT[:, s, k, t * P:t * P + tok], wg[:, r, k, c0:c1],
                                  start=(i == 0 and k == 0), stop=False)
            pe3(0, p3_first, 2, P, None)
            with pe.Fori(1, NB) as b:
                pe3(b, p3, 2, P, True)
            pe3(NB, p3, 1, TAIL, True)
            pe.wait_ge(x1_normed, 2 * NB + 1)
            turn(end3, par3_end, p3_end, "X", xb, 1, TAIL)
            logits(end3, par3_end, p3_end, 0, TAIL)
            turn_coefficients(end3, par3_end, p3_end, 1, TAIL, NB + 1)
            tree_rows(end3, par3_end, p3_end, 0, TAIL)

        @block.vector
        def _(dve):
            v = nc.vector
            v.memset(wout3, 0.0).then_inc(vconsts, 1)
            v.memset(kvs[:], 0.0).then_inc(kv_added, 1)
            v.memset(degs[:], 0.0)
            v.memset(co[:], 0.0)
            v.memset(cf[:], 0.0)
            v.memset(vp[:, 1, :, :], 0.0)
            v.memset(vp[:, 0, :, :], 1.0).then_inc(vconsts, 1)
            dve.wait_ge(vconsts, 2)
            class Chain:
                base, n = 0, 0

            def link(ins):
                Chain.n += 1
                ins.then_inc(vch, 1)
                dve.wait_ge(vch, Chain.base + Chain.n)

            def low(base, u, ops):
                dve.wait_ge(slot_a, base[1] + u[1] + 1)
                for f in ops:
                    last = f()
                last.then_inc(slot_v, 1)

            def stt(o, i0, sc, i1, op0, op1):
                return v.scalar_tensor_tensor(out=o, in0=i0, scalar=sc, in1=i1, op0=op0, op1=op1)

            def split_edges():
                dve.wait_ge(edges_in, 32)
                tmp = ed[:, 0:EC]
                link(v.tensor_scalar(tmp, dcol, P - 1, None, ALU.bitwise_and))
                v.tensor_copy(lo7[:], tmp)
                tmp2 = ed[:, EC:2 * EC]
                link(v.tensor_scalar(tmp2, dcol, 7, None, ALU.arith_shift_right))
                link(v.tensor_copy(hi7[:], tmp2))
                down = tmp.bitcast(F32)
                link(v.tensor_tensor(down, dcol, dnext, ALU.is_gt))
                link(v.tensor_reduce(bad[:, 0:1], down, mybir.AxisListType.X, ALU.max))

            def biases():
                dve.wait_ge(small_in, 16 * 9)
                v.tensor_scalar(bqk[:], bqk_r[:], WS, None, ALU.mult)
                v.tensor_copy(wo[:], wout3)
                link(v.tensor_tensor(gpb[:], gpb[:], pbr, ALU.add))
                link(v.tensor_tensor(wo[64:96, :], wout3[64:96, :], wo[64:96, :], ALU.subtract))
                v.memset(den[:], 0.0).then_inc(small_v, 1)

            def statistics(t, tok, src_, s_stats):
                for c in range(2):
                    v.bn_stats(st[0:tok, t, c, :], src_[0:tok, t, c * D // 2:(c + 1) * D // 2]).then_inc(vch, 1)
                Chain.n += 2
                wait_apart(dve, vch, Chain.base + Chain.n, stats_passed)
                v.bn_aggr(mv[0:tok, t, :], st[0:tok, t, :, :]).then_inc(s_stats, 1)

            def normalise(n, t, tok, s_rstd, src_, s_norm):
                dve.wait_ge(s_rstd, 2 * n + 2)
                v.tensor_scalar(xb[0:tok, t, :], src_[0:tok, t, :], mv[0:tok, t, 0:1], rs[0:tok, t:t + 1],
                                ALU.subtract, ALU.mult).then_inc(s_norm, 1)

            for i in range(NPREP):
                if i == 3:
                    biases()
                    dve.wait_ge(x_in, 16)
                    for t in range(2):
                        statistics(t, P, xa, stats)
                if i == 5:
                    for t in range(2):
                        normalise(t, t, P, rstd, xa, normed)
                if i == 7:
                    split_edges()
                w, c0 = (wk, wv, wq, wp)[i // 3], (i % 3) * B
                for c in range(3):
                    u = prep[("W", i, c)]
                    low((0, 0, 0), u, [lambda w=w, c0=c0, c=c, u=u: stt(
                        w[:, 1, 2 * c:2 * c + 2, c0:c0 + B], place0(u)[:].rearrange("p (k n) -> p k n", k=2), WS,
                        w[:, 0, 2 * c:2 * c + 2, c0:c0 + B], ALU.mult, ALU.subtract)])
            u = prep[("W", "pm", 0)]
            low((0, 0, 0), u, [lambda: stt(pmT[:, 1, :], place0(u)[:, 0:M], 1.0, pmT[:, 0, :], ALU.mult, ALU.subtract)])
            u2 = prep[("W", "win", 0)]
            low((0, 0, 0), u2, [lambda: stt(winT[:, 1, :, :], place0(u2)[:, 0:DC * 32].rearrange("p (k n) -> p k n", k=DC)[:, :, 0:NN],
                                            1.0, winT[:, 0, :, :], ALU.mult, ALU.subtract)])
            for i in range(DC // 2):
                n = NPREP + i
                dve.wait_ge(wg_hi, i + 1)
                stt(wg[:, 1, 2 * i:2 * i + 2, :], wst[n % NW][:, :, :], WS, wg[:, 0, 2 * i:2 * i + 2, :], ALU.mult, ALU.subtract).then_inc(wg_lo, 1)
            dve.wait_ge(consts, 5)
            CH0 = Chain.n

            def turned_lo(base, par, plan, kind, dst_, w, cs=range(3)):
                for c in cs:
                    u = plan[(kind, c, 0)]
                    low(base, u, [lambda c=c, u=u: stt(dst_[:, 1, 2 * c:2 * c + 2, 0:w],
                                                       parity(par, u)[:].rearrange("p (k n) -> p k n", k=2)[:, :, 0:w], 1.0,
                                                       dst_[:, 0, 2 * c:2 * c + 2, 0:w], ALU.mult, ALU.subtract)])

            def low_ops(s, m, col, w):
                return [lambda e=e: stt(hd[64 - 64 * e:128 - 64 * e, 2 * m + e, 0:w], s[64 * e:64 * e + 64, 0:w],
                                        bqk[64 * e:64 * e + 64, col + m:col + m + 1],
                                        hd[64 * e:64 * e + 64, 2 * m + e, 0:w], ALU.add, ALU.subtract) for e in range(2)]

            def keys_lo(base, par, plan, c, w):
                u = plan[("K", c, 0)]
                s = parity(par, u)
                low(base, u, low_ops(s[:, 0:B], 2 * c, DC, w) + low_ops(s[:, B:2 * B], 2 * c + 1, DC, w))

            def queries_lo(base, par, plan, m, w):
                u = plan[("Q", m, 0)]
                low(base, u, low_ops(parity(par, u), m, 0, w))

            def flush_kv(n, half):
                dve.wait_ge(kv_full, 2 * n + half + 1)
                dst_ = kvs[:, 12 * half:12 * half + 12, :].rearrange("p (a i) d -> p a i d", a=2)
                src_ = (zps, acc[0])[half][:].rearrange("p (a n) -> p a n", a=2)[:, :, 0:6 * DV].rearrange("p a (i d) -> p a i d", d=DV)
                v.tensor_tensor(dst_, src_, dst_, ALU.add).then_inc(kv_added, 1)

            def build_hots(n, i):
                r, last_ = (0, FIRST - 1) if i < FIRST else (1, PIECES - 1)
                if i in (0, FIRST):
                    wait_for(dve, hist_full, 2 * n + r)
                c0, n_ = ends[i] - r * ends[FIRST], ends[i + 1] - ends[i]
                v.tensor_tensor(onesb[:, c0:c0 + n_, :], iota16[:].unsqueeze(1).broadcast_to([P, n_, P]),
                                lo7[:, bass.ds(n * HC + ends[i], n_)].unsqueeze(2).broadcast_to([P, n_, P]), ALU.is_equal)
                last = v.tensor_tensor(onesa[:, c0:c0 + n_, :], iota16[:, 0:NTP].unsqueeze(1).broadcast_to([P, n_, NTP]),
                                       hi7[:, bass.ds(n * HC + ends[i], n_)].unsqueeze(2).broadcast_to([P, n_, NTP]), ALU.is_equal)
                if i == last_:
                    last.then_inc(hots_built, 1)

            def add_degrees(n):
                dve.wait_ge(hist_full, n + 1)
                v.tensor_tensor(degs[:], zps[:, 0:NTP], degs[:], ALU.add).then_inc(deg_added, 1)

            def table_lo(t, i, tok=P):
                dve.wait_ge(t_hi, t + 1)
                stt(tout[i][0:tok, D:2 * D], tin[i][0:tok, :], dinvT[0:tok, bass.ds(t, 1)], tout[i][0:tok, 0:D], ALU.mult, ALU.subtract).then_inc(t_lo, 1)

            def dve1(b, plan, nt, tok, base, par, first=False, nt_next=2, tok_next=P, hist=False, with_table=False):
                w = B if nt == 2 else tok
                if first:
                    turned_lo(base, par, plan, "T", xT, w)
                else:
                    turned_lo(base, par, plan, "T", xT, w, (0, 1))
                    flush_kv(b - 1, 0)
                    turned_lo(base, par, plan, "T", xT, w, (2,))
                    flush_kv(b - 1, 1)
                for i in range(3 if hist else 0):
                    build_hots(b, i)
                for c in range(3):
                    keys_lo(base, par, plan, c, w)
                    for i in range(3 * c + 3, min(3 * c + 6, FIRST) if hist else 0):
                        build_hots(b, i)
                for t in range(nt):
                    for p in range(H // 2):
                        u = plan[("F", t, p)]
                        low(base, u, [lambda t=t, p=p, u=u: stt(kfeat[0:tok, 1, t, 2 * p * M:(2 * p + 2) * M], parity(par, u)[0:tok, :], 0.0,
                                                                kfeat[0:tok, 0, t, 2 * p * M:(2 * p + 2) * M], ALU.max, ALU.subtract)])
                        at = t * (H // 2) + p
                        if hist and at == 3:
                            add_degrees(2 * b)
                        for i, after in enumerate((3, 5, 7, 9, 9) if hist else ()):
                            if at == after:
                                build_hots(b, FIRST + i)
                        if with_table and (t, p) in TABLE_AT:
                            k = TABLE_AT.index((t, p))
                            table_lo(R * (b - NH) + k, k % 2)
                        if nt_next and t == 0 and p in (2, 4):
                            tt = p // 2 - 1
                            if tt == 0:
                                dve.wait_ge(x_in, 16 * (b + 2))
                            if tt < nt_next:
                                statistics(tt, tok_next, xa, stats)
                        if nt_next and t == 1 and p == 0:
                            dve.wait_ge(xn_out, 16 * (b + 1))
                        if nt_next and t == 1 and p in (0, 2) and p // 2 < nt_next:
                            normalise(2 * b + 2 + p // 2, p // 2, tok_next, rstd, xa, normed)
                    dve.wait_ge(v_hi, 2 * b + t + 1)
                    v.tensor_tensor(vp[0:tok, 1, t, :].rearrange("p (h d) -> p h d", h=H)[:, :, 0:DH],
                                    acc[t][0:tok, 0:D].rearrange("p (h d) -> p h d", h=H),
                                    vp[0:tok, 0, t, :].rearrange("p (h d) -> p h d", h=H)[:, :, 0:DH], ALU.subtract).then_inc(v_lo, 1)

                if hist:
                    add_degrees(2 * b + 1)

            dve1(0, p1_first, 2, P, bases1(0), par1, first=True, hist=True)
            per = Chain.n - CH0
            with dve.Fori(1, NH) as b:
                Chain.base, Chain.n = CH0 + b * per, 0
                dve1(b, p1, 2, P, bases1(b), par1, hist=True)
            dve.wait_ge(deg_added, 2 * NH)
            v.tensor_copy(scanA[:], degs[:]).then_inc(deg_done, 1)
            dve.wait_ge(dinv_done, 1)
            v.tensor_scalar(dinvT[:], dinv[:], TS, None, ALU.mult)
            v.tensor_scalar(dinvZ[:], dinv[:], WS / TS, None, ALU.mult).then_inc(dinv_done, 1)
            dve.wait_ge(dinv_done, 2)
            with dve.Fori(NH, NB - 1) as b:
                Chain.base, Chain.n = CH0 + b * per, 0
                dve1(b, p1, 2, P, bases1(b), par1, with_table=True)
            Chain.base, Chain.n = 0, CH0 + (NB - 1) * per
            dve1(NB - 1, p1, 2, P, bases1(NB - 1), par1, nt_next=1, tok_next=TAIL, with_table=True)
            dve1(NB, p1_tail, 1, TAIL, tail1, par1_tail, nt_next=0)
            flush_kv(NB, 0)
            flush_kv(NB, 1)

            link(v.memset(same, 0.0))
            for i in range(G):
                last = v.memset(same[i * GN:(i + 1) * GN, i * GN:(i + 1) * GN], 1.0)
            last.then_inc(bad_in, 1)
            dve.wait_ge(slot_v, base3[2])
            dve.wait_ge(kv_added, 2 * NB + 3)
            kvv = kvs[:].rearrange("p (h c) d -> p h c d", c=2)
            dve.wait_ge(mid_full, 1)
            vs = acc[0][:].rearrange("p (a n) -> p a n", a=2)[:, :, 0:6 * DV].rearrange("p a (h d) -> p a h d", d=DV)
            for c in range(2):
                for i in range(2):
                    last = v.tensor_tensor(kvv[:, 6 * i:6 * i + 6, c, :], vs[:, i, :, :], kvv[:, 6 * i:6 * i + 6, c, :], ALU.add)
                    if (c, i) != (1, 1):
                        link(last)
            link(last)
            v.tensor_tensor(kf[:, 0:H], kvv[:, :, 0, DH], kvv[:, :, 1, DH], ALU.add).then_inc(mid_v, 1)
            dve.wait_ge(mid_full, 2)
            link(v.tensor_copy(cnt[:], acc[1][:, 0:NTP]))
            link(v.tensor_copy(scanA[:], cnt[:]))
            a_, b_ = scanA, scanC
            s = 1
            while s < NTP:
                v.tensor_copy(b_[:, 0:s], a_[:, 0:s]).then_inc(vch, 1)
                Chain.n += 1
                link(v.tensor_tensor(b_[:, s:NTP], a_[:, s:NTP], a_[:, 0:NTP - s], ALU.add))
                a_, b_ = b_, a_
                s *= 2
            link(v.tensor_tensor(e0f[:], a_[:], cnt[:], ALU.subtract))
            link(v.tensor_tensor(e0f[0:G, :], e0f[0:G, :], acc[1][0:G, NTP:2 * NTP], ALU.add))
            link(v.tensor_copy(e0[:], e0f[:]))
            v.memset(den[:], 0.0)
            v.memset(rec[:], 0.0).then_inc(ranges_done, 1)
            dve.wait_ge(mid_full, 3)
            link(v.reciprocal(kf[:, 0:H], acc[1][:, BANK:BANK + H]))
            link(v.tensor_scalar(kf[:, H:2 * H], kf[:, 0:H], 1024.0, None, ALU.mult))
            kvf = kvs[:].rearrange("p (h c) d -> p h (c d)", c=2)
            link(v.tensor_tensor(kvf, kvf, kf[:, H:2 * H].unsqueeze(2).broadcast_to([P, H, 2 * DV]), ALU.mult))
            link(v.tensor_copy(kvp[:, 0, :, :], kvs[:]))
            link(v.tensor_tensor(kvp[:, 1, :, :], kvs[:], kvp[:, 0, :, :], ALU.subtract))
            v.memset(sg[:], 0.0).then_inc(mid_v, 1)
            dve.wait_ge(mid_full, 4)
            link(v.tensor_copy(cn.rearrange("p (a h) d -> p a h d", a=2), vs))
            v.memset(ns[:], 0.0).then_inc(kv_ready, 1)
            dve.wait_ge(bad_full, 1)
            link(v.tensor_reduce(bad[:, 1:2], acc[1][:, 2 * NTP:3 * NTP], mybir.AxisListType.X, ALU.max))
            link(v.tensor_scalar(bad[:, 2:3], bad[:, 1:2], float(WIN * P), None, ALU.is_gt))
            v.tensor_tensor(bad[:, 3:4], bad[:, 0:1], bad[:, 2:3], ALU.add).then_inc(bad_in, 1)
            dve.wait_ge(bad_full, 2)
            v.tensor_scalar(flag[:], acc[1][0:1, 3 * NTP:3 * NTP + 1], 0.5, None, ALU.is_gt).then_inc(flag_ready, 1)

            table_lo(NT - 1, 0, TAIL)

            def general_sums():
                v.memset(zero16, 0.0).then_inc(all_zero, 1)
                with dve.Fori(0, NPASS) as n:
                    with dve.Fori(0, NS) as i:
                        dve.wait_ge(all_in, 32 * (n * NS + i) + 32)
                        for j in range(3):
                            last = v.tensor_scalar(away[:, j, :], dstw[:, 0, 0, :], tile_base[:, bass.ds(3 * n + j, 1)], None, ALU.subtract)
                        last.then_inc(all_away, 1)
                        dve.wait_ge(all_away, n * NS + i + 1)
                        for j in range(3):
                            last = v.tensor_tensor(all_hot[:, j, :, :], iota16[:].unsqueeze(1).broadcast_to([P, WIN, P]),
                                                   away[:, j, :].unsqueeze(2).broadcast_to([P, WIN, P]), ALU.is_equal)
                        last.then_inc(all_hots, 1)

                def row(t, tok):
                    z, hi, lo = zz[0:tok, 0, :], own[0:tok, 1, 0:D], own[0:tok, 1, D:2 * D]

                    def step(ins, k):
                        ins.then_inc(row_chain, 1)
                        dve.wait_ge(row_chain, 4 * t + k)
                    dve.wait_ge(row_in, 32 * t + 32)
                    step(v.tensor_tensor(z, z, own[0:tok, 0, 0:D], ALU.add), 1)
                    step(v.tensor_tensor(z, z, own[0:tok, 0, D:2 * D], ALU.add), 2)
                    step(v.tensor_scalar(z, z, dinvZ[0:tok, bass.ds(t, 1)], None, ALU.mult), 3)
                    step(v.tensor_copy(hi, z), 4)
                    v.tensor_tensor(lo, z, hi, ALU.subtract).then_inc(row_ready, 1)
                with dve.Fori(0, NT - 1) as t:
                    row(t, P)
                row(NT - 1, TAIL)
                v.memset(dinvZ[:], 1.0)
                v.tensor_scalar(tile_base[:], tile_base[:], 4.0 * BIG, None, ALU.add).then_inc(all_done, 1)
                dve.wait_ge(all_done, 2)
            dve.wait_ge(flag_ready, 1)
            with dve.If(dve.value_load(flag[0:1, 0:1], min_val=0, max_val=1) > 0):
                general_sums()

            def localise(b, j):
                dve.wait_ge(win_s[j], 2 * G * 16 * (b + 1))
                link(v.tensor_scalar(dstl[:, j, :, :], dstw[:, j, :, :], tile_base[:, bass.ds(2 * b + j, 1)], None, ALU.subtract))

            def build_unit(b, u):
                wait_for(dve, unit_used, 2 * WIN * b + u - SRING + 1)
                v.tensor_tensor(hot[:, u % SRING, :, :], iota16[:].rearrange("p (g n) -> p g n", g=G),
                                dstl[:, u // WIN, :, u % WIN:u % WIN + 1].broadcast_to([P, G, GN]), ALU.is_equal).then_inc(hot_ready, 1)

            def tree(nt, tok):
                T = slice(0, nt)
                R, C, GL, S_, NS_ = (z[0:tok] for z in (rr, cf, gl, sg, ns))

                def written(ins):
                    Chain.n += 1
                    ins.then_inc(vch, 1)
                    n = Chain.base + Chain.n
                    return lambda: dve.wait_ge(vch, n)
                w_ = written(v.tensor_scalar(NS_[:, T, :], S_[:, T, :], -1.0, 1.0, ALU.mult, ALU.add))
                yield
                w_()
                v.tensor_copy(R[:, T, 1:2], NS_[:, T, 0:1])
                w_ = written(v.tensor_copy(R[:, T, 2:3], S_[:, T, 0:1]))
                yield
                for n0, n1 in ((1, 3), (3, 7), (7, 10)):
                    kids = R[:, T, 2 * n0 + 1:2 * n1 + 1].rearrange("p t (n e) -> p t n e", e=2)
                    w_()
                    v.tensor_tensor(kids[:, :, :, 0], R[:, T, n0:n1], NS_[:, T, n0:n1], ALU.mult)
                    w_ = written(v.tensor_tensor(kids[:, :, :, 1], R[:, T, n0:n1], S_[:, T, n0:n1], ALU.mult))
                    yield
                kids = C[:, T, 1:NN].rearrange("p t (n e) -> p t n e", e=2)
                rk = R[:, T, 1:NN].rearrange("p t (n e) -> p t n e", e=2)
                w_()
                for e in range(2):
                    v.tensor_tensor(kids[:, :, :, e], rk[:, :, :, e], GL[:, T, 0:10], ALU.mult)
                w_ = written(v.tensor_tensor(ux[0:tok, T, 10:20], R[:, T, 10:20], GL[:, T, 10:20], ALU.mult))
                yield
                w_()
                v.tensor_reduce(su[0:tok, T, 0:1], ux[0:tok, T, 10:20], mybir.AxisListType.X, ALU.add)
                w_ = written(v.tensor_reduce(su[0:tok, T, 1:2], R[:, T, 15:20], mybir.AxisListType.X, ALU.add))
                yield
                w_()
                w_ = written(v.tensor_scalar(su[0:tok, T, 2:3], su[0:tok, T, 1:2], -1.0, 6.0, ALU.mult, ALU.add))
                yield
                w_()
                w_ = written(v.tensor_tensor(su[0:tok, T, 3:4], su[0:tok, T, 2:3], GL[:, T, 20:21], ALU.mult))
                yield
                w_()
                w_ = written(v.tensor_tensor(su[0:tok, T, 0:1], su[0:tok, T, 0:1], su[0:tok, T, 3:4], ALU.add))
                yield
                w_()
                w_ = written(v.tensor_tensor(C[:, T, 20:21], C[:, T, 20:21], su[0:tok, T, 0:1], ALU.add))
                yield
                w_()
                v.tensor_copy(co[0:tok, T, 0:NN], C[:, T, :])
                w_ = written(v.tensor_copy(co[0:tok, T, 64:64 + NN], C[:, T, :]))
                yield
                w_()
                v.tensor_tensor(co[0:tok, T, 32:32 + NN], C[:, T, :], co[0:tok, T, 0:NN], ALU.subtract).then_inc(coef, 1)
                yield

            def signs(base, par, plan, nt, tok):
                for t in range(nt):
                    u = plan[("L", t, 0)]
                    dve.wait_ge(slot_a, base[1] + u[1] + 1)
                    v.tensor_scalar(sg[0:tok, t, :], parity(par, u)[0:tok, 0:NN], 0.0, None, ALU.is_gt).then_inc(slot_v, 1)
                dve.wait_ge(slot_v, base[2] + plan[("L", nt - 1, 0)][2] + 1)

            def add_tree_rows(base, par, plan, t, tok):
                for i, (c0, c1) in enumerate(((0, BANK), (BANK, D))):
                    u = plan[("Y", t, i)]
                    dve.wait_ge(slot_full, base[0] + u[0] + 1)
                    v.tensor_tensor(yo[0:tok, t, c0:c1], parity(par, u)[0:tok, 0:c1 - c0], x1[0:tok, t, c0:c1], ALU.add).then_inc(slot_v, 1)

            def dve3(b, plan, nt, tok, prev):
                base, w = bases3(b), (B if nt == 2 else tok)
                par = par3_first if prev is None else par3
                units = iter(range(WIN if prev else 0, 2 * WIN) if nt == 2 else ())

                def unit():
                    for _ in range(1 if prev else 2):
                        u_ = next(units, None)
                        if u_ is not None:
                            build_unit(b, u_)

                def features(h):
                    uf = plan[("F", h, 0)]
                    low(base, uf, [lambda: stt(qfeat[:, h % 4, 1, :, 0:w], parity(par, uf)[:].rearrange("p (c n) -> p c n", c=2)[:, :, 0:w],
                                               0.0, qfeat[:, h % 4, 0, :, 0:w], ALU.max, ALU.subtract)])

                def q_lo(m):
                    queries_lo(base, par, plan, m, w)

                def x1_lo(c):
                    if prev:
                        turned_lo(base, par, plan, "X", x1T, B, (c,))

                def tree_step():
                    if prev:
                        next(steps)
                steps = tree(2, P) if prev else None
                if nt == 2:
                    localise(b, 1)
                unit()
                q_lo(0)
                q_lo(1)
                features(0)
                unit()
                if prev:
                    norm_x1(2 * b - 2, 0, P)
                features(1)
                if prev:
                    norm_x1(2 * b - 2, 1, P)
                q_lo(2)
                features(2)
                unit()
                features(3)
                q_lo(3)
                for c in range(3):
                    x1_lo(c)
                features(4)
                unit()
                features(5)
                q_lo(4)
                if prev:
                    signs(base, par, plan, 2, P)
                unit()
                tree_step()
                features(6)
                tree_step()
                tree_step()
                features(7)
                for _ in range(3):
                    tree_step()
                q_lo(5)
                tree_step()
                features(8)
                for _ in range(3):
                    tree_step()
                features(9)
                tree_step()
                tree_step()
                features(10)
                if nt == 2:
                    localise(b + 1, 0)
                features(11)
                if nt == 2:
                    build_unit(b + 1, 0)
                turned_lo(base, par, plan, "Z", zT, w, (0,))
                turned_lo(base, par, plan, "Z", zT, w, (1,))
                tree_step()
                na = 4 * b
                for t in range(nt):
                    dve.wait_ge(acc_full, na + t + 1)
                    view = acc[t][0:tok, :].rearrange("p (a n) -> p a n", a=2)[:, :, 0:6 * DV].rearrange("p a (h d) -> p a h d", d=DV)
                    cv = cn[0:tok].rearrange("p (a h) d -> p a h d", a=2)
                    ov = oo[0:tok, t, :].rearrange("p (a h d) -> p a h d", a=2, d=DH)
                    dv = den[0:tok, t, :].rearrange("p (a h) -> p a h", a=2)
                    v.tensor_tensor(ov, view[:, :, :, 0:DH], cv[:, :, :, 0:DH], ALU.add).then_inc(vch, 1)
                    Chain.n += 1
                    v.tensor_tensor(dv, view[:, :, :, DH], cv[:, :, :, DH], ALU.add).then_inc(acc_read, 1)
                    if t == 0:
                        turned_lo(base, par, plan, "Z", zT, w, (2,))
                if nt == 2:
                    build_unit(b + 1, 1)
                for t in range(nt):
                    dve.wait_ge(acc_read, na + t + 1)
                    link(v.reciprocal(rec[0:tok, t, :], den[0:tok, t, :]))
                    oh = oo[0:tok, t, :].rearrange("p (h d) -> p h d", h=H)
                    v.tensor_tensor(oh, oh, rec[0:tok, t, :].unsqueeze(2).broadcast_to([tok, H, DH]), ALU.mult).then_inc(o_ready, 1)
                if nt == 2:
                    build_unit(b + 1, 2)
                for c in range(3):
                    u_ = plan[("O", c, 0)]
                    s_ = parity(par, u_)
                    low(base, u_, [lambda e=e, c=c, s_=s_: stt(oT[:, 1, 2 * c + e, 0:w], s_[:, e * B:e * B + w],
                                                              bqk[:, 2 * DC + 2 * c + e:2 * DC + 2 * c + e + 1],
                                                              oT[:, 0, 2 * c + e, 0:w], ALU.add, ALU.subtract) for e in range(2)])
                if nt == 2:
                    build_unit(b + 1, 3)
                    build_unit(b + 1, 4)
                if prev:
                    dve.wait_ge(xr_in, 16 * (b + 1))
                    for t in range(2):
                        add_tree_rows(base, par, plan, t, P)
                no = na + nt
                for t in range(nt):
                    ac = acc[t]
                    dve.wait_ge(acc_full, no + t + 1)
                    dve.wait_ge(xr_biased, 2 * b + t + 1)
                    stt(x1[0:tok, t, :], ac[0:tok, 0:D], 1.0 / (WS * WS), xa[0:tok, t, :], ALU.mult, ALU.add).then_inc(acc_read, 1)
                    dve.wait_ge(acc_read, no + t + 1)
                    statistics(t, tok, x1, x1_stats)

            def norm_x1(n, t, tok):
                normalise(n + t, t, tok, x1_rstd, x1, x1_normed)
            localise(0, 0)
            dve3(0, p3_first, 2, P, None)
            C3b = Chain.n
            per3 = 2 + 12 + 2 * 2 + 2 * 2
            with dve.Fori(1, NB) as b:
                Chain.base, Chain.n = C3b + (b - 1) * per3, 0
                dve3(b, p3, 2, P, True)
                assert Chain.n == per3
            Chain.base, Chain.n = 0, C3b + (NB - 1) * per3
            dve3(NB, p3, 1, TAIL, True)
            norm_x1(2 * NB, 0, TAIL)
            turned_lo(end3, par3_end, p3_end, "X", x1T, TAIL)
            signs(end3, par3_end, p3_end, 1, TAIL)
            for _ in tree(1, TAIL):
                pass
            dve.wait_ge(stored, 16 * NB)
            add_tree_rows(end3, par3_end, p3_end, 0, TAIL)


_INS = ["x", "src", "dst", "L0_gnn_W", "L0_gnn_b", "L0_mix_qkv_w", "L0_mix_qkv_b", "L0_mix_proj_w", "L0_mix_proj_b",
        "L0_mix_proj_mat", "L0_ffn_weights_in", "L0_ffn_weights_out"]


def build(nc, arrays):
    args = [nc.dram_tensor(f"in_{n}", arrays[f"in_{n}"].shape, mybir.dt.from_np(arrays[f"in_{n}"].dtype), kind="ExternalInput").ap()
            for n in _INS]
    out = nc.dram_tensor("out_0", arrays["in_x"].shape, F32, kind="ExternalOutput").ap()
    gps_layer(nc, *args, out)


def kernel(**inputs):
    import numpy as np
    import concourse.bacc as bacc
    from concourse.bass_utils import run_bass_kernel_spmd

    nc = bacc.Bacc("TRN2", target_bir_lowering=False, num_devices=1)
    arrays = {f"in_{n}": np.ascontiguousarray(inputs[n]) for n in _INS}
    build(nc, arrays)
    return run_bass_kernel_spmd(nc, [arrays], core_ids=[0]).results[0]["out_0"]
```
